# Optimizing a Trainium2 kernel written in Bass

```python
import numpy as np
import jax
import jax.numpy as jnp

def _softmax(x, axis=-1):
    return jax.nn.softmax(x, axis=axis)

def _gelu(x):
    return jax.nn.gelu(x, approximate=True)

def _silu(x):
    return jax.nn.silu(x)

def _sigmoid(x):
    return jax.nn.sigmoid(x)

def _layernorm(x, axis=-1, eps=1e-05):
    m = jnp.mean(x, axis=axis, keepdims=True)
    v = jnp.var(x, axis=axis, keepdims=True)
    return (x - m) / jnp.sqrt(v + eps)

def _scatter_add(tgt, idx, src, axis=0):
    return tgt.at[idx].add(src)

def _segment_sum(src, seg, n):
    return jax.ops.segment_sum(src, seg, n)
kernel_name = 'mk_seq_postln_d1_jaxref_r4_7eecaf'

def setup_inputs(seed: int=0):
    np.random.seed(seed)
    _w = jnp.asarray

    def _L0_attn_setup():
        import jax, jax.numpy as jnp
        import numpy as np
        D_MODEL = 256
        N_HEADS = 16
        HEAD_DIM = D_MODEL // N_HEADS
        WINDOW = 128
        LOCAL_BLOCK = 64
        LATENT_TOKENS = 64
        LATENT_D = 64
        LATENT_HEADS = 4
        LATENT_HD = LATENT_D // LATENT_HEADS
        NEG = -1000000000.0

        def _local_attention(q, k, v):
            B, H, S, hd = q.shape
            bs = min(S, max(WINDOW, LOCAL_BLOCK))
            nb = S // bs
            w = WINDOW
            L = bs + w - 1
            k_pad = jnp.pad(k, ((0, 0), (0, 0), (w - 1, 0), (0, 0)))
            v_pad = jnp.pad(v, ((0, 0), (0, 0), (w - 1, 0), (0, 0)))
            starts = jnp.arange(nb) * bs
            idx = starts[:, None] + jnp.arange(L)[None, :]
            kb = k_pad[:, :, idx]
            vb = v_pad[:, :, idx]
            qb = q.reshape(B, H, nb, bs, hd)
            q_pos = starts[:, None] + jnp.arange(bs)[None, :]
            k_gpos = starts[:, None] + jnp.arange(L)[None, :] - (w - 1)
            dist = q_pos[:, :, None] - k_gpos[:, None, :]
            allowed = (dist > 0) & (dist <= w) & (k_gpos[:, None, :] >= 0)
            scale = 1.0 / np.sqrt(hd)
            scores = jnp.einsum('bhnqd,bhnkd->bhnqk', qb, kb) * scale
            scores = jnp.where(allowed, scores, NEG)
            attn = jax.nn.softmax(scores, axis=-1)
            attn = jnp.where(allowed.any(-1)[None, None, :, :, None], attn, 0.0)
            out = jnp.einsum('bhnqk,bhnkd->bhnqd', attn, vb)
            return out.reshape(B, H, S, hd)
        key = jax.random.key(seed)
        ks = jax.random.split(key, 14)
        B, S = (2, 1024)
        s = 0.02
        f32 = jnp.float32
        return {'x': jax.random.normal(ks[0], (B, S, D_MODEL), f32), 'qkv_w': jax.random.normal(ks[1], (D_MODEL, 3 * D_MODEL), f32) * s, 'qkv_b': jnp.zeros((3 * D_MODEL,), f32), 'rq_w': jax.random.normal(ks[2], (D_MODEL, LATENT_D), f32) * s, 'rq_b': jnp.zeros((LATENT_D,), f32), 'rkv_w': jax.random.normal(ks[3], (D_MODEL, 2 * LATENT_D), f32) * s, 'rkv_b': jnp.zeros((2 * LATENT_D,), f32), 'rout_w': jax.random.normal(ks[4], (LATENT_D, D_MODEL), f32) * s, 'rout_b': jnp.zeros((D_MODEL,), f32), 'out_w': jax.random.normal(ks[5], (D_MODEL, D_MODEL), f32) * s, 'out_b': jnp.zeros((D_MODEL,), f32), 'gl_w': jax.random.normal(ks[6], (HEAD_DIM, 1), f32) * s, 'gr_w': jax.random.normal(ks[7], (HEAD_DIM, 1), f32) * s}
    _L0_attn_in = _L0_attn_setup()

    def _L0_ffn_setup():
        import jax, jax.numpy as jnp
        import numpy as np
        EPS = 1e-08

        def _ternary_linear(x, w):
            alpha = jnp.mean(jnp.abs(w))
            w_t = jnp.sign(w) * (jnp.abs(w) > 0.5 * alpha).astype(w.dtype)
            w_q = w + jax.lax.stop_gradient(w_t - w)
            d = x.shape[-1]
            rms = jnp.sqrt(jnp.sum(x * x, axis=-1, keepdims=True)) / jnp.sqrt(jnp.asarray(d, x.dtype))
            x_norm = x / (rms + EPS)
            return jnp.einsum('bsd,fd->bsf', x_norm, w_q)
        key = jax.random.key(seed)
        k1, k2, k3 = jax.random.split(key, 3)
        d_model, d_ff = (256, 1024)
        B, S = (4, 1024)
        x = jax.random.normal(k1, (B, S, d_model), dtype=jnp.float32)
        w_up = jax.random.normal(k2, (d_ff, d_model), dtype=jnp.float32) * 0.02
        w_down = jax.random.normal(k3, (d_model, d_ff), dtype=jnp.float32) * 0.02
        return {'x': x, 'w_up': w_up, 'w_down': w_down}
    _L0_ffn_in = _L0_ffn_setup()
    _d = {'L0_attn_x': _L0_attn_in['x'], 'L0_attn_qkv_w': _L0_attn_in['qkv_w'], 'L0_attn_qkv_b': _L0_attn_in['qkv_b'], 'L0_attn_rq_w': _L0_attn_in['rq_w'], 'L0_attn_rq_b': _L0_attn_in['rq_b'], 'L0_attn_rkv_w': _L0_attn_in['rkv_w'], 'L0_attn_rkv_b': _L0_attn_in['rkv_b'], 'L0_attn_rout_w': _L0_attn_in['rout_w'], 'L0_attn_rout_b': _L0_attn_in['rout_b'], 'L0_attn_out_w': _L0_attn_in['out_w'], 'L0_attn_out_b': _L0_attn_in['out_b'], 'L0_attn_gl_w': _L0_attn_in['gl_w'], 'L0_attn_gr_w': _L0_attn_in['gr_w'], 'L0_ffn_w_up': _L0_ffn_in['w_up'], 'L0_ffn_w_down': _L0_ffn_in['w_down']}
    _x0 = _d['L0_attn_x']
    _d['L0_attn_x'] = jax.random.normal(jax.random.fold_in(jax.random.key(seed), 1), (16, 512, 256), dtype=_x0.dtype)
    del _x0
    return _d

def reference(L0_attn_x, L0_attn_qkv_w, L0_attn_qkv_b, L0_attn_rq_w, L0_attn_rq_b, L0_attn_rkv_w, L0_attn_rkv_b, L0_attn_rout_w, L0_attn_rout_b, L0_attn_out_w, L0_attn_out_b, L0_attn_gl_w, L0_attn_gr_w, L0_ffn_w_up, L0_ffn_w_down):

    def _L0_attn_ref(x, qkv_w, qkv_b, rq_w, rq_b, rkv_w, rkv_b, rout_w, rout_b, out_w, out_b, gl_w, gr_w):
        import jax, jax.numpy as jnp
        import numpy as np
        D_MODEL = 256
        N_HEADS = 16
        HEAD_DIM = D_MODEL // N_HEADS
        WINDOW = 128
        LOCAL_BLOCK = 64
        LATENT_TOKENS = 64
        LATENT_D = 64
        LATENT_HEADS = 4
        LATENT_HD = LATENT_D // LATENT_HEADS
        NEG = -1000000000.0

        def _local_attention(q, k, v):
            B, H, S, hd = q.shape
            bs = min(S, max(WINDOW, LOCAL_BLOCK))
            nb = S // bs
            w = WINDOW
            L = bs + w - 1
            k_pad = jnp.pad(k, ((0, 0), (0, 0), (w - 1, 0), (0, 0)))
            v_pad = jnp.pad(v, ((0, 0), (0, 0), (w - 1, 0), (0, 0)))
            starts = jnp.arange(nb) * bs
            idx = starts[:, None] + jnp.arange(L)[None, :]
            kb = k_pad[:, :, idx]
            vb = v_pad[:, :, idx]
            qb = q.reshape(B, H, nb, bs, hd)
            q_pos = starts[:, None] + jnp.arange(bs)[None, :]
            k_gpos = starts[:, None] + jnp.arange(L)[None, :] - (w - 1)
            dist = q_pos[:, :, None] - k_gpos[:, None, :]
            allowed = (dist > 0) & (dist <= w) & (k_gpos[:, None, :] >= 0)
            scale = 1.0 / np.sqrt(hd)
            scores = jnp.einsum('bhnqd,bhnkd->bhnqk', qb, kb) * scale
            scores = jnp.where(allowed, scores, NEG)
            attn = jax.nn.softmax(scores, axis=-1)
            attn = jnp.where(allowed.any(-1)[None, None, :, :, None], attn, 0.0)
            out = jnp.einsum('bhnqk,bhnkd->bhnqd', attn, vb)
            return out.reshape(B, H, S, hd)
        B, S, D = x.shape
        qkv = x @ qkv_w + qkv_b
        q, k, v = jnp.split(qkv, 3, axis=-1)

        def heads(t):
            return t.reshape(B, S, N_HEADS, HEAD_DIM).transpose(0, 2, 1, 3)
        local = _local_attention(heads(q), heads(k), heads(v))
        chunk = -(-S // min(LATENT_TOKENS, S))
        nlat = S // chunk
        pooled = x.reshape(B, nlat, chunk, D).mean(axis=2)
        chunk_ids = jnp.arange(S) // chunk
        rq = (x @ rq_w + rq_b).reshape(B, S, LATENT_HEADS, LATENT_HD).transpose(0, 2, 1, 3)
        rkv = pooled @ rkv_w + rkv_b
        rk, rv = jnp.split(rkv, 2, axis=-1)
        rk = rk.reshape(B, nlat, LATENT_HEADS, LATENT_HD).transpose(0, 2, 1, 3)
        rv = rv.reshape(B, nlat, LATENT_HEADS, LATENT_HD).transpose(0, 2, 1, 3)
        lscale = 1.0 / np.sqrt(LATENT_HD)
        lscores = jnp.einsum('bhsd,bhld->bhsl', rq, rk) * lscale
        lat_allowed = jnp.arange(nlat)[None, :] < chunk_ids[:, None]
        lscores = jnp.where(lat_allowed[None, None], lscores, NEG)
        lattn = jax.nn.softmax(lscores, axis=-1)
        lattn = jnp.where(lat_allowed.any(-1)[None, None, :, None], lattn, 0.0)
        lat_out = jnp.einsum('bhsl,bhld->bhsd', lattn, rv)
        lat_out = lat_out.transpose(0, 2, 1, 3).reshape(B, S, LATENT_D)
        remote = lat_out @ rout_w + rout_b
        remote_h = remote.reshape(B, S, N_HEADS, HEAD_DIM).transpose(0, 2, 1, 3)
        gate = jax.nn.sigmoid(local @ gl_w + remote_h @ gr_w)
        mixed = gate * local + (1.0 - gate) * remote_h
        mixed = mixed.transpose(0, 2, 1, 3).reshape(B, S, D)
        return mixed @ out_w + out_b

    def _L0_ffn_ref(x, w_up, w_down):
        import jax, jax.numpy as jnp
        import numpy as np
        EPS = 1e-08

        def _ternary_linear(x, w):
            alpha = jnp.mean(jnp.abs(w))
            w_t = jnp.sign(w) * (jnp.abs(w) > 0.5 * alpha).astype(w.dtype)
            w_q = w + jax.lax.stop_gradient(w_t - w)
            d = x.shape[-1]
            rms = jnp.sqrt(jnp.sum(x * x, axis=-1, keepdims=True)) / jnp.sqrt(jnp.asarray(d, x.dtype))
            x_norm = x / (rms + EPS)
            return jnp.einsum('bsd,fd->bsf', x_norm, w_q)
        h = jax.nn.gelu(_ternary_linear(x, w_up), approximate=False)
        return _ternary_linear(h, w_down)
    x = L0_attn_x
    x = _layernorm(x + _L0_attn_ref(x, L0_attn_qkv_w, L0_attn_qkv_b, L0_attn_rq_w, L0_attn_rq_b, L0_attn_rkv_w, L0_attn_rkv_b, L0_attn_rout_w, L0_attn_rout_b, L0_attn_out_w, L0_attn_out_b, L0_attn_gl_w, L0_attn_gr_w), axis=-1)
    x = _layernorm(x + _L0_ffn_ref(x, L0_ffn_w_up, L0_ffn_w_down), axis=-1)
    return x

_drawn_inputs = setup_inputs


def setup_inputs(seed=0):
    import zlib

    import numpy as np

    out = dict(_drawn_inputs(seed))
    spreads = {'L0_attn_qkv_b': (0.0, 0.504),
     'L0_attn_rq_b': (0.0, 0.8),
     'L0_attn_rkv_b': (0.0, 0.8),
     'L0_attn_rout_b': (0.0, 0.532),
     'L0_attn_out_b': (0.0, 0.1)}
    factors = {'L0_attn_qkv_w': 8.0,
     'L0_attn_rq_w': 8.0,
     'L0_attn_rkv_w': 8.0,
     'L0_attn_rout_w': 8.0,
     'L0_attn_gl_w': 8.0,
     'L0_attn_gr_w': 8.0}
    for name, (base, spread) in spreads.items():
        noise = np.random.default_rng([zlib.crc32(name.encode()), seed]).standard_normal(out[name].shape)
        drawn = base * np.exp(spread * noise) if base else spread * noise
        out[name] = jnp.asarray(drawn.astype(out[name].dtype))
    for name, factor in factors.items():
        out[name] = (out[name] * factor).astype(out[name].dtype)
    return out
```

```python
from contextlib import ExitStack

import concourse.bass as bass
from concourse import mybir

ALU = mybir.AluOpType
ACT = mybir.ActivationFunctionType
F32 = mybir.dt.float32
BF16 = mybir.dt.bfloat16
F16 = mybir.dt.float16
X = mybir.AxisListType.X
RADD = bass.bass_isa.ReduceOp.add

P = 128
NEG = -1.0e30
EPS = 1e-5

B, S, D = 16, 512, 256
H, HD = 16, 16
LH, LHD, LAT = 4, 16, 64
LD = LH * LHD
F = 1024
NB = S // P
KT = D // P
FT = F // P
CHUNK = S // LAT
SCALE = float(HD) ** -0.5
LSCALE = float(LHD) ** -0.5
VW = HD + 2
RW = D + H
PVW = 32

QPART = (0, 0, 0, 1, 1, 2)
KPART = (0, 1, 2, 0, 1, 0)
ROWS = HD * len(QPART)
EXC = ROWS
MAXR = ROWS + 1
KA, KB = ROWS + 1, ROWS + 3
GQ = 64
BAND = GQ + P

NP_, NB_, NA_, NF_ = 22, 4, 2, 16
NALL = NP_ + NB_ + NA_ + NF_
HG = H // 4
NU = HG * NB
NPT = 3


class Seq:

    def __init__(self, i, par, half):
        self.i, self.par, self.half = i, par, half
        self.first = isinstance(i, int) and i == 0
        self.last = isinstance(i, int) and i == B - 1

    def next(self):
        return Seq(self.i + 1, 1 - self.par, self.half + self.par)


def count(s, per, k):
    return s.i * per + (k + 1)


def work_use(s, phase, u):
    if s.first and phase in "PA":
        return u % 2, (NP_ if phase == "A" else 0) // 2 + u // 2
    before = {"P": -(NB_ + NF_), "A": NP_ - NF_, "B": 2 * NP_ + NA_, "F": 2 * NP_ + 2 * NA_ + NB_}[phase]
    if s.last:
        before -= {"P": 0, "A": 0, "B": NP_, "F": NP_ + NA_}[phase]
    return u % 2, s.i * (NALL // 2) + (before // 2 + u // 2)


def score_use(s, phase, u):
    return u % 2, s.i * NU + ((NU if phase == "B" else 0) // 2 + u // 2)


def over_sequences(eng, body):
    body(Seq(0, 0, 0))
    body(Seq(1, 1, 0))
    with eng.Fori(1, B // 2 - 1) as pair:
        body(Seq(pair * 2, 0, pair))
        body(Seq(pair * 2 + 1, 1, pair))
    body(Seq(B - 2, 0, B // 2 - 1))
    body(Seq(B - 1, 1, B // 2 - 1))


def build(nc, x, qkv_w, qkv_b, rq_w, rq_b, rkv_w, rkv_b, rout_w, rout_b, out_w, out_b, gl_w, gr_w,
          w_up, w_down, out):
    with ExitStack() as ctx:
        def sb(name, shape, dt=F32):
            return ctx.enter_context(nc.sbuf_tensor(name, shape, dt))

        def sem(name):
            return ctx.enter_context(nc.semaphore(name))

        ident = sb("ident", [P, P])
        identb = sb("identb", [P, P], BF16)
        ones_col = sb("ones_col", [P, 1])
        power = sb("power", [P, 2, NB])
        mask_edge = sb("mask_edge", [P, 2, GQ], BF16)
        mask_first = sb("mask_first", [P, BAND], BF16)
        lat_mask = sb("lat_mask", [P, NB, LAT], BF16)
        diag_mask = sb("diag_mask", [P, LH, LAT])
        dead = sb("dead", [P, NB, H])
        live = sb("live", [P, NB, LH])
        wqk = sb("wqk", [P, KT, 2 * D])
        wv = sb("wv", [P, KT, H, VW])
        wrq = sb("wrq", [P, KT, LD])
        wrkv = sb("wrkv", [P, KT, 2 * LD])
        wout = sb("wout", [P, KT, D])
        wro = sb("wro", [P, RW])
        bqk = sb("bqk", [P, 4])
        brq = sb("brq", [LD, 1])
        brkv = sb("brkv", [P, 1])
        bv = sb("bv", [P, H, VW])
        brem = sb("brem", [P, RW])
        bout = sb("bout", [P, D])
        glb = sb("glb", [P, HD])
        grb = sb("grb", [P, HD])
        wup_t = sb("wup_t", [P, KT, F], F16)
        wdn_t = sb("wdn_t", [P, FT, D], F16)
        alpha = sb("alpha", [P, 8])
        xtok = sb("xtok", [P, NB, D])
        xb = sb("xb", [P, 2, NB, D])
        xT = sb("xT", [P, KT, S])
        pooled = sb("pooled", [P, KT, LAT])
        parts = sb("parts", [P, 3, 4, S], BF16)
        Qs = [sb(f"Qs{k}", [P, H, S], BF16) for k in range(2)]
        Ks = [sb(f"Ks{k}", [P, H, P + S], BF16) for k in range(2)]
        Vp = sb("Vp", [P, 2, NB, H * VW + PVW - VW])
        rqT = sb("rqT", [LD, S])
        rkv_sb = sb("rkv_sb", [P, LAT])
        lat_bd = sb("lat_bd", [P, LH, LAT])
        rvr = sb("rvr", [P, 2, RW])
        lat_st = sb("lat_st", [P, 3, NB, LH])
        rem = sb("rem", [P, 2, NB, RW])
        nmax = sb("nmax", [P, NB, H])
        nmaxT = sb("nmaxT", [H, 2, S], BF16)
        Pt = sb("Pt", [P, NPT, 4, 2 * P])
        oT = sb("oT", [P, S])
        o_tok = sb("o_tok", [P, NB, H, VW])
        gate = sb("gate", [P, 5, NB, H])
        ytok = sb("ytok", [P, NB, D])
        stats = sb("stats", [P, NB, 6])
        mv = sb("mv", [P, NB, 2])
        rs = sb("rs", [P, 4, NB])
        x1 = sb("x1", [P, NB, D])
        mixT = sb("mixT", [P, KT, S])
        xnT = sb("xnT", [P, 2, KT, S], F16)
        hbuf = sb("hbuf", [P, 2, S])
        h_hi = sb("h_hi", [P, FT, S], F16)
        h_lo = sb("h_lo", [P, FT, S], F16)
        mixed = x1
        lat_p = x1[:, :, :].rearrange("p b (h l) -> p b h l", h=LH)
        lat_pT = mixT[:, :, :].rearrange("p t n -> p (t n)").rearrange("p (b t n) -> p b t n", b=NB, t=2)
        qk_rest = hbuf
        hsq = oT
        ssq_row = rqT[0:1, :]

        work = ctx.enter_context(nc.psum_tensor("work", [P, 2, 512], F32))
        scores = ctx.enter_context(nc.psum_tensor("scores", [P, 2, 2, 512], F32))
        oacc = ctx.enter_context(nc.psum_tensor("oacc", [P, 2, 512], F32))

        parts_dram = nc.dram_tensor("parts_scratch", [3, 2 * D, S], BF16, kind="Internal").ap()
        nmax_dram = nc.dram_tensor("nmax_scratch", [2, H, S], BF16, kind="Internal").ap()

        passed = sem("passed")
        w_in = sem("w_in")
        consts = sem("consts")
        alpha_part = sem("alpha_part")
        alpha_all = sem("alpha_all")
        tern = sem("tern")
        tern_T = sem("tern_T")
        wt_done = sem("wt_done")
        prep_done = sem("prep_done")
        q_consts = sem("q_consts")
        pool_chain = sem("pool_chain")
        vec_chain = sem("vec_chain")
        x_in = sem("x_in")
        xb_done = sem("xb_done")
        w_full = [sem(f"w_full{k}") for k in range(2)]
        w_taken = [sem(f"w_taken{k}") for k in range(2)]
        p_vec = sem("p_vec")
        bd_ready = sem("bd_ready")
        part0 = sem("part0")
        part1 = sem("part1")
        part2 = sem("part2")
        parts_out = sem("parts_out")
        stacks_in = [sem(f"stacks_in{k}") for k in range(2)]
        lat_exp = sem("lat_exp")
        lat_norm = sem("lat_norm")
        s_full = [sem(f"s_full{k}") for k in range(2)]
        s_taken = [sem(f"s_taken{k}") for k in range(2)]
        nmax_hi = sem("nmax_hi")
        nmax_out = sem("nmax_out")
        nmax_in = [sem(f"nmax_in{k}") for k in range(2)]
        masked = sem("masked")
        pv_done = sem("pv_done")
        oT_ready = sem("oT_ready")
        f_vec = sem("f_vec")
        gate_z = sem("gate_z")
        gate_e = sem("gate_e")
        gate_g = sem("gate_g")
        rem_part = sem("rem_part")
        mixed_ready = sem("mixed_ready")
        var_ready = sem("var_ready")
        rstd_ready = sem("rstd_ready")
        var2_ready = sem("var2_ready")
        rstd2_ready = sem("rstd2_ready")
        xn_ready = sem("xn_ready")
        xn_hi = sem("xn_hi")
        h_sq = sem("h_sq")
        h_hi_ready = sem("h_hi_ready")
        h_lo_ready = sem("h_lo_ready")
        sq_read = sem("sq_read")
        ssq_ready = sem("ssq_ready")
        ssqT = sem("ssqT")
        ssq_mean = sem("ssq_mean")
        hroot = sem("hroot")
        y_ready = sem("y_ready")
        y_out = sem("y_out")

        block = ctx.enter_context(nc.Block())

        def natural(stack, k):
            v = stack[:, :, :].rearrange("p h n -> p (h n)").bitcast(F32)
            if k == 0:
                return v[:, 0:FT * D]
            return v[:, FT * D:FT * D + KT * F]

        nat = [natural(Qs[0], k) for k in range(2)]
        ternary = [natural(Qs[1], k) for k in range(2)]
        below = h_hi[:, :, :].rearrange("p t n -> p (t n)").bitcast(F32)

        def rows_of_all(v, n):
            return bass.AP(v.tensor, v.offset, [[0, P], [1, n]])

        loads = [
            (nat[0].rearrange("p (t d) -> p t d", t=FT), w_up.rearrange("(t p) d -> p t d", p=P)),
            (nat[1].rearrange("p (t f) -> p t f", t=KT), w_down.rearrange("(t p) f -> p t f", p=P)),
            (wqk[:, :, :], qkv_w[:, 0:2 * D].rearrange("(t p) n -> p t n", p=P)),
            (wrq[:, :, :], rq_w.rearrange("(t p) n -> p t n", p=P)),
            (wrkv[:, :, :], rkv_w.rearrange("(t p) n -> p t n", p=P)),
            (wout[:, :, :], out_w.rearrange("(t p) n -> p t n", p=P)),
            (wro[LD:2 * LD, 0:D], rout_w),
            (bqk[:, :], qkv_b[0:2 * D].rearrange("(t p) -> p t", p=P)),
            (brq[:, :], rq_b.rearrange("(p a) -> p a", a=1)),
            (brkv[:, :], rkv_b.rearrange("(p a) -> p a", a=1)),
            (bv[:, :, 0:HD], bass.AP(qkv_b.tensor, qkv_b.offset + 2 * D, [[0, P], [HD, H], [1, HD]])),
            (brem[:, 0:D], rows_of_all(rout_b, D)),
            (bout[:, :], rows_of_all(out_b, D)),
            (glb[:, :], rows_of_all(gl_w, HD)),
            (grb[:, :], rows_of_all(gr_w, HD)),
        ] + [(wv[:, t, :, 0:HD], qkv_w[t * P:(t + 1) * P, 2 * D:3 * D].rearrange("p (h d) -> p h d", h=H))
             for t in range(KT)]
        W_ALL = 16 * len(loads)

        def wait_alone(eng, semaphore, value):
            eng.wait_ge(semaphore, value)
            eng.sem_inc(passed, 1)

        @block.sync
        def _(sp):
            xs = x.rearrange("s (b p) d -> s p b d", p=P)
            outs = out.rearrange("s (b p) d -> s p b d", p=P)

            def of_seq(t, i):
                return t[i] if isinstance(i, int) else t[bass.ds(i, 1)].squeeze(0)

            def load_x(s, before=None):
                if before is not None:
                    for t in range(KT):
                        slot, k = work_use(before, "P", t)
                        wait_alone(sp, w_full[slot], k + 1)
                    wait_alone(sp, xb_done, count(before, 1, 0))
                sp.dma_start(xtok[:, :, :], of_seq(xs, s.i)).then_inc(x_in, 16)

            def restack(s):
                if not s.first:
                    wait_alone(sp, stacks_in[1 - s.par], (s.half + s.par) * (16 * 2 * len(QPART)))
                for j in range(3):
                    wait_alone(sp, (part0, part1, part2)[j], count(s, 4, 3))
                    sp.dma_start(parts_dram[j].rearrange("(t p) n -> p t n", p=P), parts[:, j, :, :]
                                 ).then_inc(parts_out, 16)
                if isinstance(s.i, int) and s.i < 2:
                    wait_alone(sp, q_consts, 1)
                else:
                    wait_alone(sp, pv_done, count(s, NU, -NU - 1))
                wait_alone(sp, parts_out, count(s, 1, 0) * 48)
                for r in range(len(QPART)):
                    rows = slice(HD * r, HD * r + HD)
                    sp.dma_start(Qs[s.par][rows, :, :],
                                 parts_dram[QPART[r], 0:D].rearrange("(h d) n -> d h n", d=HD)
                                 ).then_inc(stacks_in[s.par], 16)
                    sp.dma_start(Ks[s.par][rows, :, P:P + S],
                                 parts_dram[KPART[r], D:2 * D].rearrange("(h d) n -> d h n", d=HD)
                                 ).then_inc(stacks_in[s.par], 16)

            def move_max(s):
                for t in range(NA_):
                    slot, k = work_use(s, "A", t)
                    wait_alone(sp, w_taken[slot], k + 1)
                if not s.first:
                    wait_alone(sp, nmax_in[1 - s.par], (s.half + s.par) * 16)
                sp.dma_start(nmax_dram.rearrange("j h n -> h j n"), nmaxT[:, :, :]).then_inc(nmax_out, 16)
                wait_alone(sp, nmax_out, count(s, 1, 0) * 16)
                sp.dma_start(Qs[s.par][MAXR:MAXR + 2, :, :], nmax_dram).then_inc(nmax_in[s.par], 16)

            def body(s):
                if not s.last:
                    restack(s.next())
                    move_max(s.next())
                    if not s.next().last:
                        load_x(s.next().next(), s.next())
                wait_alone(sp, y_ready, count(s, NB, NB - 1))
                sp.dma_start(of_seq(outs, s.i), ytok[:, :, :]).then_inc(y_out, 16)

            with nc.allow_non_contiguous_dma(reason="bias columns, a few hundred elements"):
                for dst, src in loads:
                    sp.dma_start(dst, src).then_inc(w_in, 16)
            load_x(Seq(0, 0, 0))
            restack(Seq(0, 0, 0))
            move_max(Seq(0, 0, 0))
            load_x(Seq(1, 1, 0), Seq(0, 0, 0))
            over_sequences(sp, body)
            sp.wait_ge(y_out, 16 * B)

        @block.gpsimd
        def _(pool):
            links = [0]

            def link(ins):
                links[0] += 1
                ins.then_inc(pool_chain, 1)
                pool.wait_ge(pool_chain, links[0])

            pool.wait_ge(w_in, W_ALL)
            link(pool.memset(ones_col[:, :], 1.0))
            link(pool.memset(power[:, 0, :], -0.5))
            link(pool.memset(power[:, 1, :], 0.5))
            link(pool.memset(ident[:, :], 0.0))
            link(pool.memset(mask_edge[:, :, :], 0.0))
            link(pool.memset(mask_first[:, :], 0.0))
            link(pool.memset(lat_mask[:, :, :], 0.0))
            link(pool.memset(diag_mask[:, :, :], 1.0))
            link(pool.memset(dead[:, :, :], 0.0))
            link(pool.memset(live[:, :, :], 1.0))
            link(pool.memset(Vp[:, :, :, :], 0.0))
            link(pool.memset(wv[:, :, :, HD:VW], 0.0))
            link(pool.memset(bv[:, :, HD:VW], 1.0))
            for k in range(2):
                link(pool.memset(Ks[k][0:ROWS, :, 0:P], 0.0))
                link(pool.memset(Ks[k][ROWS:P, :, :], 1.0))
                link(pool.memset(Ks[k][EXC:EXC + 1, :, :], 0.0))
                link(pool.memset(Ks[k][EXC:EXC + 1, :, :].rearrange("p h (b c) -> p h b c", c=P)[:, :, :, 0:1],
                                 NEG))
            link(pool.affine_select(out=ident[:, :], in_=ident[:, :], compare_op=ALU.not_equal, fill=1.0,
                                    base=0, pattern=[[-1, P]], channel_multiplier=1))
            link(pool.tensor_copy(identb[:, :], ident[:, :]))
            for g in range(P // GQ):
                rows = slice(g * GQ, (g + 1) * GQ)
                link(pool.affine_select(out=mask_edge[rows, 0, :], in_=mask_edge[rows, 0, :],
                                        compare_op=ALU.is_ge, fill=NEG, base=0,
                                        pattern=[[1, GQ]], channel_multiplier=-1))
                link(pool.affine_select(out=mask_edge[rows, 1, :], in_=mask_edge[rows, 1, :],
                                        compare_op=ALU.is_gt, fill=NEG, base=0,
                                        pattern=[[-1, GQ]], channel_multiplier=1))
                link(pool.affine_select(out=mask_first[rows, :], in_=mask_first[rows, :],
                                        compare_op=ALU.is_gt, fill=NEG, base=P,
                                        pattern=[[-1, BAND]], channel_multiplier=1))
                link(pool.affine_select(out=mask_first[rows, :], in_=mask_first[rows, :],
                                        compare_op=ALU.is_ge, fill=NEG, base=g * GQ - P,
                                        pattern=[[1, BAND]], channel_multiplier=0))
            link(pool.memset(mask_first[0:1, 1:2], 0.0))
            link(pool.affine_select(out=lat_mask[:, :, :], in_=lat_mask[:, :, :], compare_op=ALU.is_ge,
                                    fill=NEG, base=-CHUNK, pattern=[[P, NB], [-CHUNK, LAT]],
                                    channel_multiplier=1))
            for half in range(2):
                rows = slice(half * LD, half * LD + LD)
                link(pool.affine_select(out=diag_mask[rows, :, :], in_=diag_mask[rows, :, :],
                                        compare_op=ALU.is_ge, fill=0.0, base=0,
                                        pattern=[[-LHD, LH], [0, LAT]], channel_multiplier=1))
                link(pool.affine_select(out=diag_mask[rows, :, :], in_=diag_mask[rows, :, :],
                                        compare_op=ALU.is_ge, fill=0.0, base=LHD - 1,
                                        pattern=[[LHD, LH], [0, LAT]], channel_multiplier=-1))
            link(pool.memset(dead[0:1, 0, :], 1.0))
            pool.memset(live[0:CHUNK, 0, :], 0.0).then_inc(consts, 1)
            pool.wait_ge(alpha_part, 1)
            pool.partition_all_reduce(alpha[:, 4:6], alpha[:, 2:4], P, RADD).then_inc(alpha_all, 1)
            pool.wait_ge(wt_done, 2)
            for k in range(2):
                link(pool.memset(Qs[k][ROWS:P, :, :], 0.0))
                link(pool.memset(Qs[k][EXC:EXC + 1, :, :].rearrange("p h (b c) -> p h b c", c=P)[:, :, :, 0:1],
                                 1.0))
            pool.sem_inc(q_consts, 1)

            def phase_p(s):
                pool.wait_ge(x_in, count(s, 1, 0) * 16)
                for b in range(NB):
                    ins = pool.tensor_tensor(xb[:, s.par, b, :], xtok[:, b, :], bout[:, :], ALU.add)
                ins.then_inc(xb_done, 1)
                for t in range(4):
                    pool.wait_ge(part1, count(s, 4, t))
                    if t == 0 and not s.first:
                        pool.wait_ge(parts_out, count(s, 1, -1) * 48)
                    pool.tensor_tensor(parts[:, 2, t, :], qk_rest[:, t % 2, :], parts[:, 1, t, :],
                                       ALU.subtract).then_inc(part2, 1)

            def phase_b(s):
                for u in range(NU):
                    pt = Pt[:, u % NPT, :, :]
                    slot, k = score_use(s, "B", u)
                    wait_alone(pool, s_taken[slot], k + 1)
                    ins = pool.affine_select(out=pt[:, :, 0:P], in_=pt[:, :, 0:P], compare_op=ALU.is_gt,
                                             fill=0.0, base=0, pattern=[[0, 4], [1, P]], channel_multiplier=-1)
                    if u % NB < NB - 1:
                        ins = pool.affine_select(out=pt[:, :, P:2 * P], in_=pt[:, :, P:2 * P],
                                                 compare_op=ALU.is_ge, fill=0.0, base=0,
                                                 pattern=[[0, 4], [-1, P]], channel_multiplier=1)
                    ins.then_inc(masked, 1)

            def phase_f(s):
                pool.wait_ge(gate_g, count(s, 1, 0))
                for b in range(NB):
                    rv = rem[:, s.par, b, 0:D].rearrange("p (h d) -> p h d", h=H)
                    ins = pool.tensor_tensor(rv, rv, gate[:, 2, b, :].unsqueeze(2).to_broadcast([P, H, HD]),
                                             ALU.mult)
                ins.then_inc(rem_part, 1)
                pool.wait_ge(var_ready, count(s, 1, 0))
                pool.tensor_tensor(rs[:, 0, :], rs[:, 3, :], power[:, 0, :], ALU.pow)
                pool.tensor_tensor(rs[:, 1, :], mv[:, :, 1], power[:, 1, :], ALU.pow).then_inc(rstd_ready, 1)
                for t in range(FT):
                    pool.wait_ge(h_hi_ready, count(s, FT, t))
                    pool.tensor_tensor(h_lo[:, t, :], hbuf[:, t % 2, :], h_hi[:, t, :],
                                       ALU.subtract).then_inc(h_lo_ready, 1)
                pool.wait_ge(ssq_mean, count(s, 1, 0))
                pool.tensor_tensor(rs[:, 2, :], rs[:, 3, :], power[:, 1, :], ALU.pow).then_inc(hroot, 1)
                pool.wait_ge(var2_ready, count(s, 1, 0))
                pool.tensor_tensor(rs[:, 0, :], rs[:, 3, :], power[:, 0, :], ALU.pow).then_inc(rstd2_ready, 1)

            def body(s):
                if not s.last:
                    phase_p(s.next())
                phase_b(s)
                phase_f(s)

            phase_p(Seq(0, 0, 0))
            over_sequences(pool, body)

        @block.scalar
        def _(act):
            def phase_p(s):
                for t in range(4):
                    slot, k = work_use(s, "P", 4 + t)
                    act.wait_ge(w_full[slot], k + 1)
                    if t == 0 and not s.first:
                        act.wait_ge(parts_out, count(s, 1, -1) * 48)
                    nc.scalar.activation(parts[:, 0, t, :], work[:, slot, :], ACT.Identity,
                                         bias=bqk[:, t:t + 1]).then_inc(part0, 1)
                for b2 in range(NB // 2):
                    slot, k = work_use(s, "P", 8 + b2)
                    act.wait_ge(w_taken[slot], k + 1)
                    lp = lat_p[:, 2 * b2:2 * b2 + 2, :, :].rearrange("p b h l -> p (b h l)")
                    nc.scalar.activation(lp, lp, ACT.Exp, scale=LSCALE).then_inc(lat_exp, 1)
                for t in range(2):
                    slot, k = work_use(s, "P", 14 + t)
                    act.wait_ge(w_full[slot], k + 1)
                    nc.scalar.activation(rvr[:, t, :], work[:, slot, 0:RW], ACT.Copy
                                         ).then_inc(w_taken[slot], 1)
                for t in range(2):
                    slot, k = work_use(s, "P", 16 + t)
                    act.wait_ge(w_full[slot], k + 1)
                    nc.scalar.activation(lat_pT[:, 2 * t:2 * t + 2, :, :].rearrange("p b t n -> p (b t n)"),
                                         work[:, slot, :], ACT.Copy).then_inc(w_taken[slot], 1)

            def phase_a(s):
                for t in range(NA_):
                    slot, k = work_use(s, "A", t)
                    act.wait_ge(w_full[slot], k + 1)
                    if t == 0 and not s.first:
                        act.wait_ge(nmax_out, count(s, 1, -1) * 16)
                    nc.scalar.activation(nmaxT[:, 0, 2 * P * t:2 * P * (t + 1)], work[0:H, slot, 0:2 * P],
                                         ACT.Copy).then_inc(nmax_hi, 1)

            def copy_o(s, hg):
                act.wait_ge(pv_done, count(s, NU, NB * hg + NB - 1))
                if hg > 0:
                    slot, k = work_use(s, "B", hg - 1)
                    act.wait_ge(w_full[slot], k + 1)
                nc.scalar.activation(oT[:, :], oacc[:, hg % 2, :], ACT.Copy).then_inc(oT_ready, 1)

            def phase_b(s):
                for u in range(NU + 3):
                    if u < NU:
                        slot, k = score_use(s, "B", u)
                        act.wait_ge(s_full[slot], k + 1)
                        if u >= NPT:
                            act.wait_ge(pv_done, count(s, NU, u - NPT))
                        w = 2 * P if u % NB < NB - 1 else P
                        nc.scalar.activation(
                            Pt[:, u % NPT, :, 0:w],
                            scores[:, slot, :, :].rearrange("p k (h q) -> p (k h) q", h=2)[:, :, 0:w],
                            ACT.Exp, scale=SCALE).then_inc(s_taken[slot], 1)
                    if u >= 6 and (u - 6) % NB == 0:
                        copy_o(s, (u - 6) // NB)

            def phase_f(s):
                act.wait_ge(gate_z, count(s, 1, 0))
                nc.scalar.activation(gate[:, 1, :, :], gate[:, 0, :, :], ACT.Exp, scale=-1.0
                                     ).then_inc(gate_e, 1)
                for t in range(KT):
                    slot, k = work_use(s, "F", t)
                    act.wait_ge(w_full[slot], k + 1)
                    nc.scalar.activation(mixT[:, t, :], work[:, slot, :], ACT.Copy).then_inc(w_taken[slot], 1)
                for t in range(KT):
                    slot, k = work_use(s, "F", 4 + t)
                    act.wait_ge(w_full[slot], k + 1)
                    nc.scalar.activation(xnT[:, 0, t, :], work[:, slot, :], ACT.Copy).then_inc(xn_hi, 1)
                for t in range(FT):
                    slot, k = work_use(s, "F", 6 + t)
                    act.wait_ge(w_full[slot], k + 1)
                    if t >= 2:
                        act.wait_ge(h_lo_ready, count(s, FT, t - 2))
                        act.wait_ge(h_sq, count(s, FT, t - 2))
                    nc.scalar.activation(hbuf[:, t % 2, :], work[:, slot, :], ACT.Gelu
                                         ).then_inc(w_taken[slot], 1)

            def body(s):
                if not s.last:
                    phase_p(s.next())
                phase_b(s)
                if not s.last:
                    phase_a(s.next())
                phase_f(s)

            act.wait_ge(w_in, W_ALL)
            phase_p(Seq(0, 0, 0))
            phase_a(Seq(0, 0, 0))
            over_sequences(act, body)

        @block.vector
        def _(dve):
            links = [0]

            def link(ins):
                links[0] += 1
                ins.then_inc(vec_chain, 1)
                dve.wait_ge(vec_chain, links[0])

            dve.wait_ge(w_in, W_ALL)
            for k in range(2):
                ins = nc.vector.tensor_reduce(alpha[:, 2 + k:3 + k], nat[k], X, ALU.add,
                                              apply_absolute_value=True)
            ins.then_inc(alpha_part, 1)
            dve.wait_ge(alpha_all, 1)
            nc.vector.tensor_scalar(alpha[:, 0:2], alpha[:, 4:6], 0.5 / (F * D), None, ALU.mult)
            link(nc.vector.tensor_scalar(alpha[:, 6:8], alpha[:, 4:6], -0.5 / (F * D), None, ALU.mult))
            for k in range(2):
                link(nc.vector.tensor_scalar(below, nat[k], alpha[:, 6 + k:7 + k], None, ALU.is_lt))
                nc.vector.scalar_tensor_tensor(out=ternary[k], in0=nat[k], scalar=alpha[:, k:k + 1],
                                               in1=below, op0=ALU.is_gt, op1=ALU.subtract).then_inc(tern, 1)
                dve.wait_ge(tern, k + 1)
            dve.wait_ge(consts, 1)
            tmp = ytok[:, 0, :].rearrange("p (h d) -> p h d", h=H)
            gl3 = glb[:, :].unsqueeze(1).to_broadcast([P, H, HD])
            gr3 = grb[:, :].unsqueeze(1).to_broadcast([P, H, HD])
            rem3 = brem[:, 0:D].rearrange("p (h d) -> p h d", h=H)
            wro3 = wro[LD:2 * LD, 0:D].rearrange("p (h d) -> p h d", h=H)
            for w3, o in [(wv[:, t, :, 0:HD], wv[:, t, :, HD + 1:VW]) for t in range(KT)] + \
                         [(bv[:, :, 0:HD], bv[:, :, HD + 1:VW])]:
                link(nc.vector.tensor_tensor(tmp, w3, gl3, ALU.mult))
                link(nc.vector.tensor_reduce(o, tmp, X, ALU.add))
            link(nc.vector.tensor_tensor(tmp, rem3, gr3, ALU.mult))
            link(nc.vector.tensor_reduce(brem[:, D:RW], tmp, X, ALU.add))
            link(nc.vector.tensor_tensor(tmp[LD:2 * LD], wro3, gr3[LD:2 * LD], ALU.mult))
            nc.vector.tensor_reduce(wro[LD:2 * LD, D:RW], tmp[LD:2 * LD], X, ALU.add).then_inc(prep_done, 1)
            for k in range(2):
                dve.wait_ge(tern_T, k + 1)
                for a in range(2):
                    for b in range(2):
                        if k == 0:
                            ins = nc.vector.tensor_copy(wup_t[:, a, 512 * b:512 * b + 512], scores[:, a, b, :])
                        else:
                            ins = nc.vector.tensor_copy(wdn_t[:, 4 * b:4 * b + 4, a * P:(a + 1) * P],
                                                        scores[:, a, b, :].rearrange("p (t n) -> p t n", n=P))
                ins.then_inc(wt_done, 1)

            def phase_p(s):
                N = 9
                step = [0]

                def done(ins):
                    step[0] += 1
                    assert step[0] <= N
                    ins.then_inc(p_vec, 1)
                    dve.wait_ge(p_vec, count(s, N, step[0] - 1))

                def take(u):
                    slot, k = work_use(s, "P", u)
                    dve.wait_ge(w_full[slot], k + 1)
                    return slot, k

                for t in range(KT):
                    slot, k = take(t)
                    nc.vector.tensor_copy(xT[:, t, :], work[:, slot, :]).then_inc(w_taken[slot], 1)
                for t in range(KT):
                    slot, k = work_use(s, "P", t)
                    dve.wait_ge(w_taken[slot], k + 1)
                done(nc.vector.tensor_reduce(pooled[:, :, :].rearrange("p t l -> p (t l)"),
                                             xT[:, :, :].rearrange("p t n -> p (t n)").rearrange(
                                                 "p (l c) -> p l c", c=CHUNK), X, ALU.add))
                slot, k = take(2)
                nc.vector.tensor_scalar(rqT[:, :], work[0:LD, slot, :], brq[:, :], None, ALU.add
                                        ).then_inc(w_taken[slot], 1)
                slot, k = take(3)
                nc.vector.tensor_scalar(rkv_sb[:, :], work[:, slot, 0:LAT], 1.0 / CHUNK, brkv[:, :],
                                        ALU.mult, ALU.add).then_inc(w_taken[slot], 1)
                dve.wait_ge(w_taken[slot], k + 1)
                nc.vector.tensor_tensor(lat_bd[:, :, :], rkv_sb[:, :].unsqueeze(1).to_broadcast([P, LH, LAT]),
                                        diag_mask[:, :, :], ALU.mult).then_inc(bd_ready, 1)
                for t in range(4):
                    slot, k = take(4 + t)
                    dve.wait_ge(part0, count(s, 4, t))
                    if t >= 2:
                        dve.wait_ge(part2, count(s, 4, t - 2))
                    nc.vector.scalar_tensor_tensor(out=qk_rest[:, t % 2, :], in0=work[:, slot, :],
                                                   scalar=bqk[:, t:t + 1], in1=parts[:, 0, t, :],
                                                   op0=ALU.add, op1=ALU.subtract).then_inc(w_taken[slot], 1)
                    dve.wait_ge(w_taken[slot], k + 1)
                    if t == 0 and not s.first:
                        dve.wait_ge(parts_out, count(s, 1, -1) * 48)
                    nc.vector.tensor_copy(parts[:, 1, t, :], qk_rest[:, t % 2, :]).then_inc(part1, 1)
                for b2 in range(NB // 2):
                    slot, k = take(8 + b2)
                    blocks = slice(2 * b2, 2 * b2 + 2)
                    done(nc.vector.tensor_reduce(lat_st[:, 0, blocks, :].rearrange("p b h -> p (b h)"),
                                                 work[:, slot, :].rearrange("p (g l) -> p g l", l=LAT),
                                                 X, ALU.max, negate=True))
                    nc.vector.tensor_tensor(
                        lat_p[:, blocks, :, :].rearrange("p b h l -> p (b h) l"),
                        work[:, slot, :].rearrange("p (g l) -> p g l", l=LAT),
                        lat_st[:, 0, blocks, :].rearrange("p b h -> p (b h)").unsqueeze(2).to_broadcast(
                            [P, 2 * LH, LAT]), ALU.add).then_inc(w_taken[slot], 1)
                for b in range(NB):
                    slot, k = take(10 + b)
                    nc.vector.tensor_tensor(Vp[:, s.par, b, 0:H * VW], work[:, slot, 0:H * VW],
                                            bv[:, :, :].rearrange("p h d -> p (h d)"), ALU.add
                                            ).then_inc(w_taken[slot], 1)
                dve.wait_ge(lat_exp, count(s, 2, 1))
                flat = lat_p[:, :, :, :].rearrange("p b h l -> p (b h) l")
                st = [lat_st[:, j, :, :].rearrange("p b h -> p (b h)") for j in range(3)]
                done(nc.vector.tensor_reduce(st[1], flat, X, ALU.add))
                done(nc.vector.reciprocal(st[2], st[1]))
                done(nc.vector.tensor_tensor(st[1], st[2], live[:, :, :].rearrange("p b h -> p (b h)"), ALU.mult))
                nc.vector.tensor_tensor(flat, flat, st[1].unsqueeze(2).to_broadcast([P, NB * LH, LAT]),
                                        ALU.mult).then_inc(lat_norm, 1)
                for b in range(NB):
                    slot, k = take(18 + b)
                    nc.vector.tensor_tensor(rem[:, s.par, b, :], work[:, slot, 0:RW], brem[:, :], ALU.add
                                            ).then_inc(w_taken[slot], 1)
                while step[0] < N:
                    step[0] += 1
                    dve.sem_inc(p_vec, 1)

            def phase_a(s):
                def low_part(t):
                    slot, k = work_use(s, "A", t)
                    dve.wait_ge(nmax_hi, count(s, NA_, t))
                    cols = slice(2 * P * t, 2 * P * (t + 1))
                    nc.vector.tensor_tensor(nmaxT[:, 1, cols], work[0:H, slot, 0:2 * P], nmaxT[:, 0, cols],
                                            ALU.subtract).then_inc(w_taken[slot], 1)

                for u in range(NU):
                    slot, k = score_use(s, "A", u)
                    dve.wait_ge(s_full[slot], k + 1)
                    nc.vector.tensor_reduce(
                        nmax[:, u // HG, 4 * (u % HG):4 * (u % HG) + 4],
                        scores[:, slot, :, 0:2 * BAND].rearrange("p k (h c) -> p k h c", h=2),
                        X, ALU.max, negate=True).then_inc(s_taken[slot], 1)
                    if u == 12:
                        low_part(0)
                low_part(1)

            def phase_b(s):
                for hg in range(HG):
                    slot, k = work_use(s, "B", hg)
                    dve.wait_ge(w_full[slot], k + 1)
                    nc.vector.tensor_copy(
                        o_tok[:, :, 4 * hg:4 * hg + 4, :],
                        work[:, slot, :].rearrange("p (b h d) -> p b h d", b=NB, h=4)[:, :, :, 0:VW]
                    ).then_inc(w_taken[slot], 1)

            def phase_f(s):
                N = 23
                step = [0]

                def mark(ins):
                    step[0] += 1
                    assert step[0] <= N
                    ins.then_inc(f_vec, 1)

                def sync():
                    dve.wait_ge(f_vec, count(s, N, step[0] - 1))

                def done(ins):
                    mark(ins)
                    sync()

                def take(u):
                    slot, k = work_use(s, "F", u)
                    dve.wait_ge(w_full[slot], k + 1)
                    return slot, k

                for hg in range(2, 4):
                    slot, k = work_use(s, "B", hg)
                    dve.wait_ge(w_taken[slot], k + 1)
                z, e, ng, r, a = (gate[:, j, :, :] for j in range(5))
                done(nc.vector.tensor_tensor(e, o_tok[:, :, :, HD], dead[:, :, :], ALU.add))
                done(nc.vector.reciprocal(r, e))
                done(nc.vector.tensor_tensor(a, o_tok[:, :, :, HD + 1], r, ALU.mult))
                nc.vector.tensor_tensor(z, a, rem[:, s.par, :, D:RW], ALU.add).then_inc(gate_z, 1)
                dve.wait_ge(gate_e, count(s, 1, 0))
                done(nc.vector.tensor_scalar(z, e, 1.0, None, ALU.add))
                done(nc.vector.reciprocal(e, z))
                mark(nc.vector.tensor_tensor(a, e, r, ALU.mult))
                nc.vector.tensor_scalar(ng, e, -1.0, 1.0, ALU.mult, ALU.add).then_inc(gate_g, 1)
                sync()
                for b in range(NB):
                    ins = nc.vector.tensor_tensor(mixed[:, b, :].rearrange("p (h d) -> p h d", h=H),
                                                  o_tok[:, b, :, 0:HD],
                                                  a[:, b, :].unsqueeze(2).to_broadcast([P, H, HD]), ALU.mult)
                done(ins)
                dve.wait_ge(rem_part, count(s, 1, 0))
                nc.vector.tensor_tensor(mixed[:, :, :], mixed[:, :, :], rem[:, s.par, :, 0:D], ALU.add
                                        ).then_inc(mixed_ready, 1)
                if not s.first:
                    dve.wait_ge(y_out, count(s, 1, -1) * 16)
                for t in range(2):
                    slot, k = take(2 + t)
                    blocks = slice(2 * t, 2 * t + 2)
                    nc.vector.tensor_tensor(ytok[:, blocks, :].rearrange("p b d -> p (b d)"), work[:, slot, :],
                                            xb[:, s.par, blocks, :].rearrange("p b d -> p (b d)"), ALU.add
                                            ).then_inc(w_taken[slot], 1)
                    dve.wait_ge(w_taken[slot], k + 1)
                    for b in range(2 * t, 2 * t + 2):
                        ins = nc.vector.bn_stats(stats[:, b, :], ytok[:, b, :])
                mark(ins)
                wait_alone(dve, f_vec, count(s, N, step[0] - 1))
                for b in range(NB):
                    ins = nc.vector.bn_aggr(mv[:, b, :], stats[:, b, :])
                done(ins)
                nc.vector.tensor_scalar(rs[:, 3, :], mv[:, :, 1], EPS, None, ALU.add).then_inc(var_ready, 1)
                dve.wait_ge(rstd_ready, count(s, 1, 0))
                done(nc.vector.tensor_tensor(rs[:, 2, :], rs[:, 0, :], rs[:, 1, :], ALU.mult))
                done(nc.vector.tensor_scalar(rs[:, 3, :], rs[:, 2, :], 1e-8, None, ALU.add))
                done(nc.vector.reciprocal(rs[:, 2, :], rs[:, 3, :]))
                done(nc.vector.tensor_tensor(rs[:, 1, :], rs[:, 2, :], rs[:, 0, :], ALU.mult))
                for b in range(NB):
                    nc.vector.tensor_scalar(x1[:, b, :], ytok[:, b, :], mv[:, b, 0:1], rs[:, 0, b:b + 1],
                                            ALU.subtract, ALU.mult)
                    ins = nc.vector.tensor_scalar(ytok[:, b, :], ytok[:, b, :], mv[:, b, 0:1], rs[:, 1, b:b + 1],
                                                  ALU.subtract, ALU.mult)
                ins.then_inc(xn_ready, 1)
                for t in range(KT):
                    slot, k = take(4 + t)
                    dve.wait_ge(xn_hi, count(s, KT, t))
                    nc.vector.tensor_tensor(xnT[:, 1, t, :], work[:, slot, :], xnT[:, 0, t, :], ALU.subtract
                                            ).then_inc(w_taken[slot], 1)
                for t in range(FT):
                    slot, k = work_use(s, "F", 6 + t)
                    dve.wait_ge(w_taken[slot], k + 1)
                    nc.vector.tensor_copy(h_hi[:, t, :], hbuf[:, t % 2, :]).then_inc(h_hi_ready, 1)
                    if t > 0:
                        dve.wait_ge(sq_read, count(s, FT, t - 1))
                    nc.vector.tensor_tensor(hsq[:, :], hbuf[:, t % 2, :], hbuf[:, t % 2, :], ALU.mult
                                            ).then_inc(h_sq, 1)
                dve.wait_ge(sq_read, count(s, FT, FT - 1))
                nc.vector.tensor_copy(ssq_row[:, :], oacc[0:1, 0, :]).then_inc(ssq_ready, 1)
                dve.wait_ge(ssqT, count(s, 1, 0))
                nc.vector.tensor_scalar(rs[:, 3, :], oacc[:, 1, 0:NB], 1.0 / F, None, ALU.mult
                                        ).then_inc(ssq_mean, 1)
                dve.wait_ge(hroot, count(s, 1, 0))
                done(nc.vector.tensor_scalar(rs[:, 3, :], rs[:, 2, :], 1e-8, None, ALU.add))
                done(nc.vector.reciprocal(rs[:, 2, :], rs[:, 3, :]))
                for t in range(2):
                    slot, k = take(14 + t)
                    for b in range(2 * t, 2 * t + 2):
                        ins = nc.vector.scalar_tensor_tensor(
                            out=ytok[:, b, :], in0=work[:, slot, (b % 2) * D:(b % 2 + 1) * D],
                            scalar=rs[:, 2, b:b + 1], in1=x1[:, b, :], op0=ALU.mult, op1=ALU.add)
                    ins.then_inc(w_taken[slot], 1)
                    dve.wait_ge(w_taken[slot], k + 1)
                    for b in range(2 * t, 2 * t + 2):
                        ins = nc.vector.bn_stats(stats[:, b, :], ytok[:, b, :])
                mark(ins)
                wait_alone(dve, f_vec, count(s, N, step[0] - 1))
                for b in range(NB):
                    ins = nc.vector.bn_aggr(mv[:, b, :], stats[:, b, :])
                done(ins)
                nc.vector.tensor_scalar(rs[:, 3, :], mv[:, :, 1], EPS, None, ALU.add).then_inc(var2_ready, 1)
                dve.wait_ge(rstd2_ready, count(s, 1, 0))
                for b in range(NB):
                    nc.vector.tensor_scalar(ytok[:, b, :], ytok[:, b, :], mv[:, b, 0:1], rs[:, 0, b:b + 1],
                                            ALU.subtract, ALU.mult).then_inc(y_ready, 1)
                while step[0] < N:
                    step[0] += 1
                    dve.sem_inc(f_vec, 1)

            def body(s):
                if not s.last:
                    phase_p(s.next())
                phase_b(s)
                if not s.last:
                    phase_a(s.next())
                phase_f(s)

            phase_p(Seq(0, 0, 0))
            phase_a(Seq(0, 0, 0))
            over_sequences(dve, body)

        @block.tensor
        def _(pe):
            pe.wait_ge(w_in, W_ALL)
            pe.wait_ge(consts, 1)
            for k in range(2):
                pe.wait_ge(tern, k + 1)
                if k:
                    pe.wait_ge(wt_done, 1)
                for a in range(2):
                    for b in range(2):
                        for c in range(4):
                            t = 4 * b + c
                            src = ternary[0][:, t * D + a * P:t * D + (a + 1) * P] if k == 0 else \
                                ternary[1][:, a * F + t * P:a * F + (t + 1) * P]
                            mm = nc.tensor.transpose(scores[:, a, b, c * P:(c + 1) * P], src, ident[:, :])
                mm.then_inc(tern_T, 1)
            pe.wait_ge(wt_done, 2)
            pe.wait_ge(prep_done, 1)

            def bank(s, phase, u):
                slot, k = work_use(s, phase, u)
                if not (isinstance(k, int) and k == 0):
                    pe.wait_ge(w_taken[slot], k)
                return slot

            def taken(s, phase, *us):
                for u in us:
                    slot, k = work_use(s, phase, u)
                    pe.wait_ge(w_taken[slot], k + 1)

            def product(out, lhs, rhs, n=KT):
                for t in range(n):
                    mm = nc.tensor.matmul(out, lhs(t), rhs(t), start=(t == 0), stop=(t == n - 1))
                return mm

            def phase_p(s):
                pe.wait_ge(x_in, count(s, 1, 0) * 16)
                for t in range(KT):
                    slot = bank(s, "P", t)
                    for b in range(NB):
                        mm = nc.tensor.transpose(work[:, slot, b * P:(b + 1) * P],
                                                 xtok[:, b, t * P:(t + 1) * P], ident[:, :])
                    mm.then_inc(w_full[slot], 1)
                taken(s, "P", 0, 1)
                slot = bank(s, "P", 2)
                product(work[0:LD, slot, :], lambda t: wrq[:, t, :], lambda t: xT[:, t, :]
                        ).then_inc(w_full[slot], 1)
                slot = bank(s, "P", 3)
                pe.wait_ge(p_vec, count(s, 9, 0))
                product(work[:, slot, 0:LAT], lambda t: wrkv[:, t, :], lambda t: pooled[:, t, :]
                        ).then_inc(w_full[slot], 1)
                for c in range(4):
                    slot = bank(s, "P", 4 + c)
                    product(work[:, slot, :], lambda t: wqk[:, t, c * P:(c + 1) * P], lambda t: xT[:, t, :]
                            ).then_inc(w_full[slot], 1)
                taken(s, "P", 2)
                pe.wait_ge(bd_ready, count(s, 1, 0))
                for b2 in range(NB // 2):
                    slot = bank(s, "P", 8 + b2)
                    for b in range(2 * b2, 2 * b2 + 2):
                        o = work[:, slot, (b % 2) * LH * LAT:(b % 2 + 1) * LH * LAT]
                        nc.tensor.matmul(o, rqT[:, b * P:(b + 1) * P],
                                         lat_bd[0:LD, :, :].rearrange("p h l -> p (h l)"),
                                         start=(b % 2 == 0), stop=False, skip_group_check=True)
                        mm = nc.tensor.matmul(o.rearrange("p (h l) -> p h l", h=LH), identb[:, :],
                                              lat_mask[:, b, :].unsqueeze(1).to_broadcast([P, LH, LAT]),
                                              start=False, stop=(b % 2 == 1), skip_group_check=True)
                    mm.then_inc(w_full[slot], 1)
                for b in range(NB):
                    slot = bank(s, "P", 10 + b)
                    product(work[:, slot, 0:H * VW], lambda t: xT[:, t, b * P:(b + 1) * P],
                            lambda t: wv[:, t, :, :].rearrange("p h d -> p (h d)")).then_inc(w_full[slot], 1)
                for t in range(2):
                    slot = bank(s, "P", 14 + t)
                    nc.tensor.matmul(work[:, slot, 0:RW],
                                     lat_bd[LD:2 * LD, 2 * t:2 * t + 2, :].rearrange("p h l -> p (h l)"),
                                     wro[LD:2 * LD, :], start=True, stop=True).then_inc(w_full[slot], 1)
                pe.wait_ge(lat_norm, count(s, 1, 0))
                for t in range(2):
                    slot = bank(s, "P", 16 + t)
                    for b in range(2 * t, 2 * t + 2):
                        for c in range(2):
                            q = (b % 2) * 2 + c
                            mm = nc.tensor.transpose(
                                work[:, slot, q * P:(q + 1) * P],
                                lat_p[:, b, 2 * c:2 * c + 2, :].rearrange("p h l -> p (h l)"), ident[:, :])
                    mm.then_inc(w_full[slot], 1)
                taken(s, "P", 14, 15, 16, 17)
                for b in range(NB):
                    slot = bank(s, "P", 18 + b)
                    product(work[:, slot, 0:RW], lambda t: lat_pT[:, b, t, :], lambda t: rvr[:, t, :], 2
                            ).then_inc(w_full[slot], 1)

            def maxima_T(s, t):
                slot, k = score_use(s, "A", 8 * t + 7)
                pe.wait_ge(s_taken[slot], k + 1)
                slot = bank(s, "A", t)
                for b in range(2):
                    mm = nc.tensor.transpose(work[0:H, slot, b * P:(b + 1) * P], nmax[:, 2 * t + b, :],
                                             ident[:, :])
                mm.then_inc(w_full[slot], 1)

            def phase_a(s):
                pe.wait_ge(stacks_in[s.par], (s.half + 1) * (16 * 2 * len(QPART)))
                q, kk = Qs[s.par], Ks[s.par]
                for u in range(NU):
                    b, hg = u // HG, u % HG
                    slot, k = score_use(s, "A", u)
                    if not (isinstance(k, int) and k == 0):
                        pe.wait_ge(s_taken[slot], k)
                    for j in range(2):
                        for hh in range(2):
                            for g in range(P // GQ):
                                h, at = 4 * hg + 2 * j + hh, b * P + g * GQ
                                nc.tensor.matmul(scores[g * GQ:(g + 1) * GQ, slot, j, hh * BAND:(hh + 1) * BAND],
                                                 q[0:KA, h, at:at + GQ], kk[0:KA, h, at:at + BAND],
                                                 start=(hh == 0), stop=False, skip_group_check=True)
                        o = scores[:, slot, j, 0:2 * BAND]
                        if b:
                            o = o.rearrange("p (h c w) -> p h c w", h=2, w=GQ)[:, :, 0:3:2, :]
                            m = mask_edge[:, :, :].unsqueeze(1).to_broadcast([P, 2, 2, GQ])
                        else:
                            o = o.rearrange("p (h c) -> p h c", h=2)
                            m = mask_first[:, :].unsqueeze(1).to_broadcast([P, 2, BAND])
                        mm = nc.tensor.matmul(o, identb[:, :], m, start=False, stop=True, skip_group_check=True)
                    mm.then_inc(s_full[slot], 1)
                    if u == 10:
                        maxima_T(s, 0)
                maxima_T(s, 1)

            def phase_b(s):
                pe.wait_ge(nmax_in[s.par], (s.half + 1) * 16)
                q, kk = Qs[s.par], Ks[s.par]
                for u in range(NU + 5):
                    if u < NU:
                        hg, j = u // NB, u % NB
                        slot, k = score_use(s, "B", u)
                        pe.wait_ge(s_taken[slot], k)
                        w = 2 * P if j < NB - 1 else P
                        for c in range(4):
                            mm = nc.tensor.matmul(scores[:, slot, c // 2, (c % 2) * 2 * P:(c % 2) * 2 * P + w],
                                                  kk[0:KB, 4 * hg + c, P + j * P:2 * P + j * P],
                                                  q[0:KB, 4 * hg + c, j * P:j * P + w], start=True, stop=True)
                        mm.then_inc(s_full[slot], 1)
                    if 2 <= u < NU + 2:
                        v = u - 2
                        hg, j = v // NB, v % NB
                        if j == 0 and (hg >= 2 or not s.first):
                            pe.wait_ge(oT_ready, count(s, HG, hg - 2))
                        pe.wait_ge(masked, count(s, NU, v))
                        w = 2 * P if j < NB - 1 else P
                        for c in range(4):
                            h = 4 * hg + c
                            mm = nc.tensor.matmul(oacc[c * PVW:(c + 1) * PVW, hg % 2, j * P:j * P + w],
                                                  Vp[:, s.par, j, h * VW:h * VW + PVW],
                                                  Pt[:, v % NPT, c, 0:w], start=(j == 0), stop=(j == NB - 1),
                                                  skip_group_check=True)
                        mm.then_inc(pv_done, 1)
                    if u >= 8 and (u - 8) % NB == 0:
                        hg = (u - 8) // NB
                        pe.wait_ge(oT_ready, count(s, HG, hg))
                        slot = bank(s, "B", hg)
                        for b in range(NB):
                            mm = nc.tensor.transpose(work[:, slot, b * P:(b + 1) * P], oT[:, b * P:(b + 1) * P],
                                                     ident[:, :])
                        mm.then_inc(w_full[slot], 1)

            def phase_f(s):
                pe.wait_ge(mixed_ready, count(s, 1, 0))
                for t in range(KT):
                    slot = bank(s, "F", t)
                    for b in range(NB):
                        mm = nc.tensor.transpose(work[:, slot, b * P:(b + 1) * P],
                                                 mixed[:, b, t * P:(t + 1) * P], ident[:, :])
                    mm.then_inc(w_full[slot], 1)
                taken(s, "F", 0, 1)
                for c in range(2):
                    slot = bank(s, "F", 2 + c)
                    for b in range(2 * c, 2 * c + 2):
                        mm = product(work[:, slot, (b % 2) * D:(b % 2 + 1) * D],
                                     lambda t: mixT[:, t, b * P:(b + 1) * P], lambda t: wout[:, t, :])
                    mm.then_inc(w_full[slot], 1)
                pe.wait_ge(xn_ready, count(s, 1, 0))
                for t in range(KT):
                    slot = bank(s, "F", 4 + t)
                    for b in range(NB):
                        mm = nc.tensor.transpose(work[:, slot, b * P:(b + 1) * P],
                                                 ytok[:, b, t * P:(t + 1) * P], ident[:, :])
                    mm.then_inc(w_full[slot], 1)
                taken(s, "F", 4, 5)
                for f in range(FT + 2):
                    if f < FT:
                        slot = bank(s, "F", 6 + f)
                        product(work[:, slot, :], lambda t: wup_t[:, t % KT, f * P:(f + 1) * P],
                                lambda t: xnT[:, t // KT, t % KT, :], 2 * KT).then_inc(w_full[slot], 1)
                    if f >= 2:
                        pe.wait_ge(h_sq, count(s, FT, f - 2))
                        if f == 2:
                            pe.wait_ge(oT_ready, count(s, HG, HG - 1))
                        nc.tensor.matmul(oacc[0:1, 0, :], ones_col[:, :], hsq[:, :], start=(f == 2),
                                         stop=(f == FT + 1)).then_inc(sq_read, 1)
                pe.wait_ge(h_hi_ready, count(s, FT, FT - 1))
                pe.wait_ge(h_lo_ready, count(s, FT, FT - 1))
                for c in range(2):
                    slot = bank(s, "F", 14 + c)
                    for b in range(2 * c, 2 * c + 2):
                        mm = product(work[:, slot, (b % 2) * D:(b % 2 + 1) * D],
                                     lambda t: (h_hi, h_lo)[t % 2][:, t // 2, b * P:(b + 1) * P],
                                     lambda t: wdn_t[:, t // 2, :], 2 * FT)
                    mm.then_inc(w_full[slot], 1)
                    if c == 0:
                        pe.wait_ge(ssq_ready, count(s, 1, 0))
                        for b in range(NB):
                            mm = nc.tensor.matmul(oacc[:, 1, b:b + 1], ssq_row[:, b * P:(b + 1) * P],
                                                  ones_col[0:1, :], start=True, stop=True)
                        mm.then_inc(ssqT, 1)

            def body(s):
                if not s.last:
                    phase_p(s.next())
                phase_b(s)
                if not s.last:
                    phase_a(s.next())
                phase_f(s)

            phase_p(Seq(0, 0, 0))
            phase_a(Seq(0, 0, 0))
            over_sequences(pe, body)


INPUTS = ["L0_attn_x", "L0_attn_qkv_w", "L0_attn_qkv_b", "L0_attn_rq_w", "L0_attn_rq_b", "L0_attn_rkv_w",
          "L0_attn_rkv_b", "L0_attn_rout_w", "L0_attn_rout_b", "L0_attn_out_w", "L0_attn_out_b",
          "L0_attn_gl_w", "L0_attn_gr_w", "L0_ffn_w_up", "L0_ffn_w_down"]


def kernel(**inputs):
    import numpy as np
    import concourse.bacc as bacc
    from concourse.bass_utils import run_bass_kernel_spmd

    nc = bacc.Bacc("TRN2", target_bir_lowering=False, num_devices=1)
    arrays, args = {}, []
    for name in INPUTS:
        a = np.ascontiguousarray(inputs[name])
        arrays[name] = a
        args.append(nc.dram_tensor(name, a.shape, mybir.dt.from_np(a.dtype), kind="ExternalInput").ap())
    out = nc.dram_tensor("y", (B, S, D), F32, kind="ExternalOutput").ap()
    build(nc, *args, out)
    r = run_bass_kernel_spmd(nc, [arrays], core_ids=[0])
    return r.results[0]["y"]
```

```python
from contextlib import ExitStack

import concourse.bass as bass
from concourse import mybir

ALU = mybir.AluOpType
ACT = mybir.ActivationFunctionType
F32 = mybir.dt.float32
BF16 = mybir.dt.bfloat16
F16 = mybir.dt.float16
X = mybir.AxisListType.X
RADD = bass.bass_isa.ReduceOp.add

P = 128
NEG = -1.0e30
EPS = 1e-5

B, S, D = 16, 512, 256
H, HD = 16, 16
LH, LHD, LAT = 4, 16, 64
LD = LH * LHD
F = 1024
NB = S // P
KT = D // P
FT = F // P
CHUNK = S // LAT
SCALE = float(HD) ** -0.5
LSCALE = float(LHD) ** -0.5
VW = HD + 2
RW = D + H
PVW = 32

QPART = (0, 0, 0, 1, 1, 2)
KPART = (0, 1, 2, 0, 1, 0)
ROWS = HD * len(QPART)
EXC = ROWS
MAXR = ROWS + 1
KA, KB = ROWS + 1, ROWS + 3
GQ = 64
BAND = GQ + P

HG = H // 4
NU = HG * NB
NPT = 3
NM = NB * H // 2
NR = 3
TRAIL = 2
NP_VEC, NF_VEC = 6, 15

SECOND_HALF = (
    ("P", 0), ("F", 0), ("P", 1), ("P", 2), ("P", 3), ("F", 1), ("P", 4), ("P", 5), ("F", 2), ("P", 6),
    ("P", 7), ("P", 8), ("P", 9), ("P", 10), ("P", 11), ("F", 3), ("F", 4), ("F", 5), ("P", 12), ("F", 6),
    ("P", 13), ("F", 7), ("P", 14), ("F", 8), ("P", 15), ("F", 9), ("P", 16), ("F", 10), ("P", 17),
    ("F", 11), ("P", 18), ("F", 12))
NSTEP_P = 19
assert [k for phase, k in SECOND_HALF if phase == "P"] == list(range(NSTEP_P))
STAT_AT = 1
FIRST_HALF = NU + 2

PUSES = 22
P_PER = [len(range(b, PUSES, 4)) for b in range(4)]


def order_of_work():
    order = []
    for u in range(FIRST_HALF):
        for v in (2 * u, 2 * u + 1):
            if v < NM:
                order.append(("A", v))
        if u >= 7 and (u - 7) % NB == 0:
            order.append(("O", (u - 7) // NB))
        if u == 9:
            order.append(("T", 0))
        if u == NM // 2:
            order.append(("T", 1))
    return order + [("O", HG - 1)] + [("F", k) for k in range(15)]


WORK_ALL = order_of_work()
WORK_A = [x for x in WORK_ALL if x[0] in "AT"]
WORK_LAST = [x for x in WORK_ALL if x[0] in "OF"]
WORK_PER = [len(WORK_ALL[b::2]) for b in range(2)]


class Seq:

    def __init__(self, i, par, half):
        self.i, self.par, self.half = i, par, half
        self.known = isinstance(i, int)
        self.first = self.known and i == 0
        self.last = self.known and i == B - 1
        self.exists = not self.known or i < B

    def next(self):
        return Seq(self.i + 1, 1 - self.par, self.half + self.par)

    def before(self):
        return Seq(self.i - 1, 1 - self.par, self.half - (1 - self.par))

    def second_next(self):
        return Seq(self.i + 2, self.par, self.half + 1)


def count(s, per, k):
    return s.i * per + (k + 1)


def work_use(s, phase, k):
    if phase in "AT" and s.first:
        at = WORK_A.index((phase, k))
        return at % 2, at // 2
    at = (WORK_LAST if s.last and phase in "OF" else WORK_ALL).index((phase, k))
    slot = at % 2
    before = len(WORK_A[slot::2])
    if phase in "AT":
        before -= WORK_PER[slot]
    return slot, s.i * WORK_PER[slot] + (before + at // 2)


def p_use(s, u):
    return u % 4, s.i * P_PER[u % 4] + u // 4


def score_use(s, u):
    return u % 2, s.i * (NU // 2) + u // 2


def over_sequences(eng, body):
    body(Seq(0, 0, 0))
    body(Seq(1, 1, 0))
    with eng.Fori(1, B // 2 - 1) as pair:
        body(Seq(pair * 2, 0, pair))
        body(Seq(pair * 2 + 1, 1, pair))
    body(Seq(B - 2, 0, B // 2 - 1))
    body(Seq(B - 1, 1, B // 2 - 1))


def build(nc, x, qkv_w, qkv_b, rq_w, rq_b, rkv_w, rkv_b, rout_w, rout_b, out_w, out_b, gl_w, gr_w,
          w_up, w_down, out):
    with ExitStack() as ctx:
        def sb(name, shape, dt=F32):
            return ctx.enter_context(nc.sbuf_tensor(name, shape, dt))

        def sem(name):
            return ctx.enter_context(nc.semaphore(name))

        ident = sb("ident", [P, P])
        identb = sb("identb", [P, P], BF16)
        ones_col = sb("ones_col", [P, 1])
        power = sb("power", [P, 2, NB])
        mask_edge = sb("mask_edge", [P, 2, GQ], BF16)
        mask_first = sb("mask_first", [P, BAND], BF16)
        lat_mask = sb("lat_mask", [P, NB, LAT], BF16)
        diag_mask = sb("diag_mask", [P, LH, LAT])
        dead = sb("dead", [P, NB, H])
        live = sb("live", [P, NB, LH])
        wqk = sb("wqk", [P, KT, 2 * D])
        wv = sb("wv", [P, KT, H, VW])
        wrq = sb("wrq", [P, KT, LD])
        wrkv = sb("wrkv", [P, KT, 2 * LD])
        wout = sb("wout", [P, KT, D])
        wro = sb("wro", [P, RW])
        bqk = sb("bqk", [P, 4])
        brq = sb("brq", [LD, 1])
        brkv = sb("brkv", [P, 1])
        bv = sb("bv", [P, H, VW])
        brem = sb("brem", [P, RW])
        bout = sb("bout", [P, D])
        glb = sb("glb", [P, HD])
        grb = sb("grb", [P, HD])
        wup_t = sb("wup_t", [P, KT, F], F16)
        wdn_t = sb("wdn_t", [P, FT, D], F16)
        alpha = sb("alpha", [P, 8])
        xtok = sb("xtok", [P, NB, D])
        xres = sb("xres", [P, NB, D])
        xT = sb("xT", [P, KT, S])
        pooled = sb("pooled", [P, KT, LAT])
        parts = sb("parts", [P, 3, 4, S], BF16)
        Qs = [sb(f"Qs{k}", [P, H, S], BF16) for k in range(2)]
        Ks = [sb(f"Ks{k}", [P, H, P + S], BF16) for k in range(2)]
        Vp = sb("Vp", [P, 2, NB, H * VW + PVW - VW])
        rqT = sb("rqT", [LD, S])
        rkv_sb = sb("rkv_sb", [P, LAT])
        lat_bd = sb("lat_bd", [P, LH, LAT])
        rvr = sb("rvr", [P, 2, RW])
        lat_st = sb("lat_st", [P, 3, NB, LH])
        rem = sb("rem", [P, 2, NB, RW])
        nmax = sb("nmax", [P, NB, H])
        nmaxT = sb("nmaxT", [H, 2, S], BF16)
        Pt = sb("Pt", [P, NPT, 4, 2 * P])
        oT = sb("oT", [P, S])
        o_tok = sb("o_tok", [P, NB, H, VW])
        gate = sb("gate", [P, 5, NB, H])
        ytok = sb("ytok", [P, NB, D])
        stats = sb("stats", [P, NB, 6])
        mv = sb("mv", [P, NB, 2])
        rs = sb("rs", [P, 4, NB])
        x1 = sb("x1", [P, NB, D])
        mixT = sb("mixT", [P, KT, S])
        xnT = sb("xnT", [P, 2, KT, S], F16)
        hbuf = sb("hbuf", [P, 2, S])
        hsq = sb("hsq", [P, 2, S])
        h_hi = sb("h_hi", [P, NR, S], F16)
        h_lo = sb("h_lo", [P, NR, S], F16)
        mixed = x1
        lat_p = Pt[:, 0, :, :].rearrange("p b (h l) -> p b h l", h=LH)
        qk_rest = Pt[:, 1, :, :].rearrange("p a b -> p (a b)").rearrange("p (t n) -> p t n", t=2)
        lat_pT = Pt[:, 2, :, :].rearrange("p b (t n) -> p b t n", t=2)
        h_sum = oT

        work = ctx.enter_context(nc.psum_tensor("work", [P, 2, 512], F32))
        scores = ctx.enter_context(nc.psum_tensor("scores", [P, 2, 2, 512], F32))
        oacc = ctx.enter_context(nc.psum_tensor("oacc", [P, 2, 512], F32))

        parts_dram = nc.dram_tensor("parts_scratch", [3, 2 * D, S], BF16, kind="Internal").ap()
        nmax_dram = nc.dram_tensor("nmax_scratch", [2, H, S], BF16, kind="Internal").ap()

        passed = sem("passed")
        w_in = sem("w_in")
        consts = sem("consts")
        alpha_part = sem("alpha_part")
        alpha_all = sem("alpha_all")
        tern = sem("tern")
        tern_T = sem("tern_T")
        wt_done = sem("wt_done")
        prep_done = sem("prep_done")
        q_consts = sem("q_consts")
        pool_chain = sem("pool_chain")
        vec_chain = sem("vec_chain")
        x_in = sem("x_in")
        xres_in = sem("xres_in")
        xres_done = sem("xres_done")
        w_full = [sem(f"w_full{k}") for k in range(2)]
        w_taken = [sem(f"w_taken{k}") for k in range(2)]
        p_full = [sem(f"p_full{k}") for k in range(4)]
        p_taken = [sem(f"p_taken{k}") for k in range(4)]
        p_vec = sem("p_vec")
        bd_ready = sem("bd_ready")
        part0 = sem("part0")
        part1 = sem("part1")
        part2 = sem("part2")
        parts_out = sem("parts_out")
        stacks_in = [sem(f"stacks_in{k}") for k in range(2)]
        lat_exp = sem("lat_exp")
        lat_norm = sem("lat_norm")
        s_full = [sem(f"s_full{k}") for k in range(2)]
        s_taken = [sem(f"s_taken{k}") for k in range(2)]
        nmax_hi = sem("nmax_hi")
        nmax_out = sem("nmax_out")
        nmax_in = [sem(f"nmax_in{k}") for k in range(2)]
        masked = sem("masked")
        pv_done = sem("pv_done")
        oT_ready = sem("oT_ready")
        f_vec = sem("f_vec")
        gate_z = sem("gate_z")
        gate_e = sem("gate_e")
        gate_g = sem("gate_g")
        rem_part = sem("rem_part")
        mixed_ready = sem("mixed_ready")
        var_ready = sem("var_ready")
        rstd_ready = sem("rstd_ready")
        var2_ready = sem("var2_ready")
        rstd2_ready = sem("rstd2_ready")
        xn_ready = sem("xn_ready")
        xn_hi = sem("xn_hi")
        h_sq = sem("h_sq")
        h_hi_ready = sem("h_hi_ready")
        h_lo_ready = sem("h_lo_ready")
        h_added = sem("h_added")
        down_done = sem("down_done")
        y2_ready = sem("y2_ready")
        y2_vec = sem("y2_vec")
        ssq_mean = sem("ssq_mean")
        hroot = sem("hroot")
        y_ready = sem("y_ready")
        y_out = sem("y_out")

        block = ctx.enter_context(nc.Block())

        def p_bank(bank):
            return scores[:, bank // 2, bank % 2, :]

        def natural(stack, k):
            v = stack[:, :, :].rearrange("p h n -> p (h n)").bitcast(F32)
            if k == 0:
                return v[:, 0:FT * D]
            return v[:, FT * D:FT * D + KT * F]

        nat = [natural(Qs[0], k) for k in range(2)]
        ternary = [natural(Qs[1], k) for k in range(2)]
        below = parts[:, :, :, :].rearrange("p j t n -> p (j t n)").bitcast(F32)[:, 0:FT * D]

        def rows_of_all(v, n):
            return bass.AP(v.tensor, v.offset, [[0, P], [1, n]])

        loads = [
            (nat[0].rearrange("p (t d) -> p t d", t=FT), w_up.rearrange("(t p) d -> p t d", p=P)),
            (nat[1].rearrange("p (t f) -> p t f", t=KT), w_down.rearrange("(t p) f -> p t f", p=P)),
            (wqk[:, :, :], qkv_w[:, 0:2 * D].rearrange("(t p) n -> p t n", p=P)),
            (wrq[:, :, :], rq_w.rearrange("(t p) n -> p t n", p=P)),
            (wrkv[:, :, :], rkv_w.rearrange("(t p) n -> p t n", p=P)),
            (wout[:, :, :], out_w.rearrange("(t p) n -> p t n", p=P)),
            (wro[LD:2 * LD, 0:D], rout_w),
            (bqk[:, :], qkv_b[0:2 * D].rearrange("(t p) -> p t", p=P)),
            (brq[:, :], rq_b.rearrange("(p a) -> p a", a=1)),
            (brkv[:, :], rkv_b.rearrange("(p a) -> p a", a=1)),
            (bv[:, :, 0:HD], bass.AP(qkv_b.tensor, qkv_b.offset + 2 * D, [[0, P], [HD, H], [1, HD]])),
            (brem[:, 0:D], rows_of_all(rout_b, D)),
            (bout[:, :], rows_of_all(out_b, D)),
            (glb[:, :], rows_of_all(gl_w, HD)),
            (grb[:, :], rows_of_all(gr_w, HD)),
        ] + [(wv[:, t, :, 0:HD], qkv_w[t * P:(t + 1) * P, 2 * D:3 * D].rearrange("p (h d) -> p h d", h=H))
             for t in range(KT)]
        W_ALL = 16 * len(loads)

        def wait_alone(eng, semaphore, value):
            eng.wait_ge(semaphore, value)
            eng.sem_inc(passed, 1)

        @block.sync
        def _(sp):
            xs = x.rearrange("s (b p) d -> s p b d", p=P)
            outs = out.rearrange("s (b p) d -> s p b d", p=P)

            def of_seq(t, i):
                return t[i] if isinstance(i, int) else t[bass.ds(i, 1)].squeeze(0)

            def load_x(s):
                if not s.first:
                    for t in range(KT):
                        bank, k = p_use(s.before(), t)
                        wait_alone(sp, p_full[bank], k + 1)
                sp.dma_start(xtok[:, :, :], of_seq(xs, s.i)).then_inc(x_in, 16)

            def load_xres(s):
                if not s.first:
                    for t in range(2):
                        slot, k = work_use(s.before(), "F", 2 + t)
                        wait_alone(sp, w_taken[slot], k + 1)
                sp.dma_start(xres[:, :, :], of_seq(xs, s.i)).then_inc(xres_in, 16)

            def restack(s):
                if not s.first:
                    wait_alone(sp, stacks_in[1 - s.par], (s.half + s.par) * (16 * 2 * len(QPART)))
                for j in range(3):
                    wait_alone(sp, (part0, part1, part2)[j], count(s, 4, 3))
                    sp.dma_start(parts_dram[j].rearrange("(t p) n -> p t n", p=P), parts[:, j, :, :]
                                 ).then_inc(parts_out, 16)
                if isinstance(s.i, int) and s.i < 2:
                    wait_alone(sp, q_consts, 1)
                else:
                    wait_alone(sp, pv_done, count(s, NU, -NU - 1))
                wait_alone(sp, parts_out, count(s, 1, 0) * 48)
                for r in range(len(QPART)):
                    rows = slice(HD * r, HD * r + HD)
                    sp.dma_start(Qs[s.par][rows, :, :],
                                 parts_dram[QPART[r], 0:D].rearrange("(h d) n -> d h n", d=HD)
                                 ).then_inc(stacks_in[s.par], 16)
                    sp.dma_start(Ks[s.par][rows, :, P:P + S],
                                 parts_dram[KPART[r], D:2 * D].rearrange("(h d) n -> d h n", d=HD)
                                 ).then_inc(stacks_in[s.par], 16)

            def move_max(s):
                for t in range(2):
                    slot, k = work_use(s, "T", t)
                    wait_alone(sp, w_taken[slot], k + 1)
                if not s.first:
                    wait_alone(sp, nmax_in[1 - s.par], (s.half + s.par) * 16)
                sp.dma_start(nmax_dram.rearrange("j h n -> h j n"), nmaxT[:, :, :]).then_inc(nmax_out, 16)
                wait_alone(sp, nmax_out, count(s, 1, 0) * 16)
                sp.dma_start(Qs[s.par][MAXR:MAXR + 2, :, :], nmax_dram).then_inc(nmax_in[s.par], 16)

            def store_before(s):
                wait_alone(sp, y_ready, count(s, NB, -1))
                sp.dma_start(of_seq(outs, s.i - 1), ytok[:, :, :]).then_inc(y_out, 16)

            def body(s):
                later = s.second_next()
                if later.exists:
                    load_x(later)
                load_xres(s)
                if not s.first:
                    store_before(s)
                if not s.last:
                    move_max(s.next())
                if later.exists:
                    restack(later)

            with nc.allow_non_contiguous_dma(reason="bias columns, a few hundred elements"):
                for dst, src in loads:
                    sp.dma_start(dst, src).then_inc(w_in, 16)
            load_x(Seq(0, 0, 0))
            load_x(Seq(1, 1, 0))
            restack(Seq(0, 0, 0))
            restack(Seq(1, 1, 0))
            move_max(Seq(0, 0, 0))
            over_sequences(sp, body)
            store_before(Seq(B, 0, B // 2))
            sp.wait_ge(y_out, 16 * B)

        @block.gpsimd
        def _(pool):
            links = [0]

            def link(ins):
                links[0] += 1
                ins.then_inc(pool_chain, 1)
                pool.wait_ge(pool_chain, links[0])

            pool.wait_ge(w_in, W_ALL)
            link(pool.memset(ones_col[:, :], 1.0))
            link(pool.memset(power[:, 0, :], -0.5))
            link(pool.memset(power[:, 1, :], 0.5))
            link(pool.memset(ident[:, :], 0.0))
            link(pool.memset(mask_edge[:, :, :], 0.0))
            link(pool.memset(mask_first[:, :], 0.0))
            link(pool.memset(lat_mask[:, :, :], 0.0))
            link(pool.memset(diag_mask[:, :, :], 1.0))
            link(pool.memset(dead[:, :, :], 0.0))
            link(pool.memset(live[:, :, :], 1.0))
            link(pool.memset(Vp[:, :, :, :], 0.0))
            link(pool.memset(wv[:, :, :, HD:VW], 0.0))
            link(pool.memset(bv[:, :, HD:VW], 1.0))
            for k in range(2):
                link(pool.memset(Ks[k][0:ROWS, :, 0:P], 0.0))
                link(pool.memset(Ks[k][ROWS:P, :, :], 1.0))
                link(pool.memset(Ks[k][EXC:EXC + 1, :, :], 0.0))
                link(pool.memset(Ks[k][EXC:EXC + 1, :, :].rearrange("p h (b c) -> p h b c", c=P)[:, :, :, 0:1],
                                 NEG))
            link(pool.affine_select(out=ident[:, :], in_=ident[:, :], compare_op=ALU.not_equal, fill=1.0,
                                    base=0, pattern=[[-1, P]], channel_multiplier=1))
            link(pool.tensor_copy(identb[:, :], ident[:, :]))
            for g in range(P // GQ):
                rows = slice(g * GQ, (g + 1) * GQ)
                link(pool.affine_select(out=mask_edge[rows, 0, :], in_=mask_edge[rows, 0, :],
                                        compare_op=ALU.is_ge, fill=NEG, base=0,
                                        pattern=[[1, GQ]], channel_multiplier=-1))
                link(pool.affine_select(out=mask_edge[rows, 1, :], in_=mask_edge[rows, 1, :],
                                        compare_op=ALU.is_gt, fill=NEG, base=0,
                                        pattern=[[-1, GQ]], channel_multiplier=1))
                link(pool.affine_select(out=mask_first[rows, :], in_=mask_first[rows, :],
                                        compare_op=ALU.is_gt, fill=NEG, base=P,
                                        pattern=[[-1, BAND]], channel_multiplier=1))
                link(pool.affine_select(out=mask_first[rows, :], in_=mask_first[rows, :],
                                        compare_op=ALU.is_ge, fill=NEG, base=g * GQ - P,
                                        pattern=[[1, BAND]], channel_multiplier=0))
            link(pool.memset(mask_first[0:1, 1:2], 0.0))
            link(pool.affine_select(out=lat_mask[:, :, :], in_=lat_mask[:, :, :], compare_op=ALU.is_ge,
                                    fill=NEG, base=-CHUNK, pattern=[[P, NB], [-CHUNK, LAT]],
                                    channel_multiplier=1))
            for half in range(2):
                rows = slice(half * LD, half * LD + LD)
                link(pool.affine_select(out=diag_mask[rows, :, :], in_=diag_mask[rows, :, :],
                                        compare_op=ALU.is_ge, fill=0.0, base=0,
                                        pattern=[[-LHD, LH], [0, LAT]], channel_multiplier=1))
                link(pool.affine_select(out=diag_mask[rows, :, :], in_=diag_mask[rows, :, :],
                                        compare_op=ALU.is_ge, fill=0.0, base=LHD - 1,
                                        pattern=[[LHD, LH], [0, LAT]], channel_multiplier=-1))
            link(pool.memset(dead[0:1, 0, :], 1.0))
            pool.memset(live[0:CHUNK, 0, :], 0.0).then_inc(consts, 1)
            pool.wait_ge(alpha_part, 1)
            pool.partition_all_reduce(alpha[:, 4:6], alpha[:, 2:4], P, RADD).then_inc(alpha_all, 1)
            pool.wait_ge(wt_done, 2)
            for k in range(2):
                link(pool.memset(Qs[k][ROWS:P, :, :], 0.0))
                link(pool.memset(Qs[k][EXC:EXC + 1, :, :].rearrange("p h (b c) -> p h b c", c=P)[:, :, :, 0:1],
                                 1.0))
            pool.sem_inc(q_consts, 1)

            def p_step(s, k):
                if 1 <= k <= 4:
                    t = k - 1
                    pool.wait_ge(part1, count(s, 4, t))
                    if t == 0 and not s.first:
                        pool.wait_ge(parts_out, count(s, 1, -1) * 48)
                    pool.tensor_tensor(parts[:, 2, t, :], qk_rest[:, t % 2, :], parts[:, 1, t, :],
                                       ALU.subtract).then_inc(part2, 1)

            def mask(s, u):
                pt = Pt[:, u % NPT, :, :]
                slot, k = score_use(s, u)
                wait_alone(pool, s_taken[slot], k + 1)
                ins = pool.affine_select(out=pt[:, :, 0:P], in_=pt[:, :, 0:P], compare_op=ALU.is_gt,
                                         fill=0.0, base=0, pattern=[[0, 4], [1, P]], channel_multiplier=-1)
                if u % NB < NB - 1:
                    ins = pool.affine_select(out=pt[:, :, P:2 * P], in_=pt[:, :, P:2 * P],
                                             compare_op=ALU.is_ge, fill=0.0, base=0,
                                             pattern=[[0, 4], [-1, P]], channel_multiplier=1)
                ins.then_inc(masked, 1)

            def f_step(s, k):
                if k == 0:
                    pool.wait_ge(gate_g, count(s, 1, 0))
                    for b in range(NB):
                        rv = rem[:, s.par, b, 0:D].rearrange("p (h d) -> p h d", h=H)
                        ins = pool.tensor_tensor(rv, rv, gate[:, 2, b, :].unsqueeze(2).to_broadcast([P, H, HD]),
                                                 ALU.mult)
                    ins.then_inc(rem_part, 1)
                if k == 1:
                    pool.wait_ge(xres_in, count(s, 1, 0) * 16)
                    for b in range(NB):
                        ins = pool.tensor_tensor(xres[:, b, :], xres[:, b, :], bout[:, :], ALU.add)
                    ins.then_inc(xres_done, 1)
                if k == 2:
                    pool.wait_ge(var_ready, count(s, 1, 0))
                    pool.tensor_tensor(rs[:, 0, :], rs[:, 3, :], power[:, 0, :], ALU.pow)
                    pool.tensor_tensor(rs[:, 1, :], mv[:, :, 1], power[:, 1, :], ALU.pow).then_inc(rstd_ready, 1)
                if 4 <= k < 4 + FT:
                    t = k - 4
                    pool.wait_ge(h_hi_ready, count(s, FT, t))
                    if t >= NR:
                        pool.wait_ge(down_done, count(s, FT, t - NR))
                    pool.tensor_tensor(h_lo[:, t % NR, :], hbuf[:, t % 2, :], h_hi[:, t % NR, :],
                                       ALU.subtract).then_inc(h_lo_ready, 1)
                if k == 12:
                    pool.wait_ge(ssq_mean, count(s, 1, 0))
                    pool.tensor_tensor(rs[:, 2, :], rs[:, 3, :], power[:, 1, :], ALU.pow).then_inc(hroot, 1)

            def finish_before(s):
                pool.wait_ge(var2_ready, count(s, 1, -1))
                pool.tensor_tensor(rs[:, 0, :], rs[:, 3, :], power[:, 0, :], ALU.pow).then_inc(rstd2_ready, 1)

            def body(s):
                for u in range(NU):
                    mask(s, u)
                    if u == STAT_AT and not s.first:
                        finish_before(s)
                later = s.second_next()
                for phase, k in SECOND_HALF:
                    if phase == "F":
                        f_step(s, k)
                    elif later.exists:
                        p_step(later, k)

            for s in (Seq(0, 0, 0), Seq(1, 1, 0)):
                for k in range(NSTEP_P):
                    p_step(s, k)
            over_sequences(pool, body)
            finish_before(Seq(B, 0, B // 2))

        @block.scalar
        def _(act):
            def p_step(s, k):
                if 1 <= k <= 4:
                    t = k - 1
                    bank, n = p_use(s, 2 + t)
                    act.wait_ge(p_full[bank], n + 1)
                    if t == 0 and not s.first:
                        act.wait_ge(parts_out, count(s, 1, -1) * 48)
                    nc.scalar.activation(parts[:, 0, t, :], p_bank(bank), ACT.Identity,
                                         bias=bqk[:, t:t + 1]).then_inc(part0, 1)
                    act.wait_ge(p_taken[bank], n + 1)
                    nc.scalar.activation(parts[:, 1, t, :], qk_rest[:, t % 2, :], ACT.Copy).then_inc(part1, 1)
                if k == 6 or k == 7:
                    b2 = k - 6
                    bank, n = p_use(s, 8 + b2)
                    act.wait_ge(p_taken[bank], n + 1)
                    lp = lat_p[:, 2 * b2:2 * b2 + 2, :, :].rearrange("p b h l -> p (b h l)")
                    nc.scalar.activation(lp, lp, ACT.Exp, scale=LSCALE).then_inc(lat_exp, 1)
                if k == 12:
                    for t in range(2):
                        bank, n = p_use(s, 14 + t)
                        act.wait_ge(p_full[bank], n + 1)
                        nc.scalar.activation(rvr[:, t, :], p_bank(bank)[:, 0:RW], ACT.Copy
                                             ).then_inc(p_taken[bank], 1)
                if k == 13 or k == 14:
                    t = k - 13
                    bank, n = p_use(s, 16 + t)
                    act.wait_ge(p_full[bank], n + 1)
                    nc.scalar.activation(lat_pT[:, 2 * t:2 * t + 2, :, :].rearrange("p b t n -> p (b t n)"),
                                         p_bank(bank), ACT.Copy).then_inc(p_taken[bank], 1)

            def max_high(s, t):
                slot, k = work_use(s, "T", t)
                act.wait_ge(w_full[slot], k + 1)
                if t == 0 and not s.first:
                    act.wait_ge(nmax_out, count(s, 1, -1) * 16)
                nc.scalar.activation(nmaxT[:, 0, 2 * P * t:2 * P * (t + 1)], work[0:H, slot, 0:2 * P],
                                     ACT.Copy).then_inc(nmax_hi, 1)

            def copy_o(s, hg):
                act.wait_ge(pv_done, count(s, NU, NB * hg + NB - 1))
                if hg > 0:
                    slot, k = work_use(s, "O", hg - 1)
                    act.wait_ge(w_full[slot], k + 1)
                nc.scalar.activation(oT[:, :], oacc[:, hg % 2, :], ACT.Copy).then_inc(oT_ready, 1)

            def weights(s, u):
                slot, k = score_use(s, u)
                act.wait_ge(s_full[slot], k + 1)
                if u >= NPT:
                    act.wait_ge(pv_done, count(s, NU, u - NPT))
                if u == 1 and not s.last:
                    act.wait_ge(part2, count(s.next(), 4, 3))
                w = 2 * P if u % NB < NB - 1 else P
                nc.scalar.activation(
                    Pt[:, u % NPT, :, 0:w],
                    scores[:, slot, :, :].rearrange("p k (h q) -> p (k h) q", h=2)[:, :, 0:w],
                    ACT.Exp, scale=SCALE).then_inc(s_taken[slot], 1)

            def f_step(s, k):
                if k == 0:
                    copy_o(s, HG - 1)
                    act.wait_ge(gate_z, count(s, 1, 0))
                    nc.scalar.activation(gate[:, 1, :, :], gate[:, 0, :, :], ACT.Exp, scale=-1.0
                                         ).then_inc(gate_e, 1)
                if k == 1:
                    for t in range(KT):
                        slot, n = work_use(s, "F", t)
                        act.wait_ge(w_full[slot], n + 1)
                        nc.scalar.activation(mixT[:, t, :], work[:, slot, :], ACT.Copy
                                             ).then_inc(w_taken[slot], 1)
                if k == 3:
                    for t in range(KT):
                        slot, n = work_use(s, "F", 4 + t)
                        act.wait_ge(w_full[slot], n + 1)
                        nc.scalar.activation(xnT[:, 0, t, :], work[:, slot, :], ACT.Copy).then_inc(xn_hi, 1)
                if 4 <= k < 4 + FT:
                    t = k - 4
                    slot, n = work_use(s, "F", 6 + t)
                    act.wait_ge(w_full[slot], n + 1)
                    if t >= 2:
                        act.wait_ge(h_lo_ready, count(s, FT, t - 2))
                        act.wait_ge(h_sq, count(s, FT, t - 2))
                    nc.scalar.activation(hbuf[:, t % 2, :], work[:, slot, :], ACT.Gelu
                                         ).then_inc(w_taken[slot], 1)
                    act.wait_ge(w_taken[slot], n + 1)
                    if t >= 3:
                        act.wait_ge(h_added, count(s, FT - 1, t - 3))
                    nc.scalar.activation(h_sum[:, :] if t == 0 else hsq[:, t % 2, :], hbuf[:, t % 2, :],
                                         ACT.Square).then_inc(h_sq, 1)

            def body(s):
                for u in range(FIRST_HALF):
                    if u < NU:
                        weights(s, u)
                    if u >= 6 and (u - 6) % NB == 0 and (u - 6) // NB < HG - 1:
                        copy_o(s, (u - 6) // NB)
                    if not s.last:
                        for t in range(2):
                            if u == (9, NM // 2)[t]:
                                max_high(s.next(), t)
                later = s.second_next()
                for phase, k in SECOND_HALF:
                    if phase == "F":
                        f_step(s, k)
                    elif later.exists:
                        p_step(later, k)

            act.wait_ge(w_in, W_ALL)
            for s in (Seq(0, 0, 0), Seq(1, 1, 0)):
                for k in range(NSTEP_P):
                    p_step(s, k)
            for t in range(2):
                max_high(Seq(0, 0, 0), t)
            over_sequences(act, body)

        @block.vector
        def _(dve):
            links = [0]

            def link(ins):
                links[0] += 1
                ins.then_inc(vec_chain, 1)
                dve.wait_ge(vec_chain, links[0])

            dve.wait_ge(w_in, W_ALL)
            sums = gate[:, 0:2, :, :].rearrange("p k b h -> p k (b h)")
            for k in range(2):
                link(nc.vector.tensor_reduce(sums[:, k, :], nat[k].rearrange("p (a n) -> p a n", a=NB * H), X,
                                             ALU.add, apply_absolute_value=True))
            nc.vector.tensor_reduce(alpha[:, 2:4], sums, X, ALU.add).then_inc(alpha_part, 1)
            dve.wait_ge(alpha_all, 1)
            nc.vector.tensor_scalar(alpha[:, 0:2], alpha[:, 4:6], 0.5 / (F * D), None, ALU.mult)
            link(nc.vector.tensor_scalar(alpha[:, 6:8], alpha[:, 4:6], -0.5 / (F * D), None, ALU.mult))
            for k in range(2):
                link(nc.vector.tensor_scalar(below, nat[k], alpha[:, 6 + k:7 + k], None, ALU.is_lt))
                nc.vector.scalar_tensor_tensor(out=ternary[k], in0=nat[k], scalar=alpha[:, k:k + 1],
                                               in1=below, op0=ALU.is_gt, op1=ALU.subtract).then_inc(tern, 1)
                dve.wait_ge(tern, k + 1)
            dve.wait_ge(consts, 1)
            tmp = ytok[:, 0, :].rearrange("p (h d) -> p h d", h=H)
            gl3 = glb[:, :].unsqueeze(1).to_broadcast([P, H, HD])
            gr3 = grb[:, :].unsqueeze(1).to_broadcast([P, H, HD])
            rem3 = brem[:, 0:D].rearrange("p (h d) -> p h d", h=H)
            wro3 = wro[LD:2 * LD, 0:D].rearrange("p (h d) -> p h d", h=H)
            for w3, o in [(wv[:, t, :, 0:HD], wv[:, t, :, HD + 1:VW]) for t in range(KT)] + \
                         [(bv[:, :, 0:HD], bv[:, :, HD + 1:VW])]:
                link(nc.vector.tensor_tensor(tmp, w3, gl3, ALU.mult))
                link(nc.vector.tensor_reduce(o, tmp, X, ALU.add))
            link(nc.vector.tensor_tensor(tmp, rem3, gr3, ALU.mult))
            link(nc.vector.tensor_reduce(brem[:, D:RW], tmp, X, ALU.add))
            link(nc.vector.tensor_tensor(tmp[LD:2 * LD], wro3, gr3[LD:2 * LD], ALU.mult))
            nc.vector.tensor_reduce(wro[LD:2 * LD, D:RW], tmp[LD:2 * LD], X, ALU.add).then_inc(prep_done, 1)
            for k in range(2):
                dve.wait_ge(tern_T, k + 1)
                for a in range(2):
                    for b in range(2):
                        if k == 0:
                            ins = nc.vector.tensor_copy(wup_t[:, a, 512 * b:512 * b + 512], scores[:, a, b, :])
                        else:
                            ins = nc.vector.tensor_copy(wdn_t[:, 4 * b:4 * b + 4, a * P:(a + 1) * P],
                                                        scores[:, a, b, :].rearrange("p (t n) -> p t n", n=P))
                ins.then_inc(wt_done, 1)

            p_links = [0]
            f_links = [0]

            def p_mark(ins):
                p_links[0] += 1
                ins.then_inc(p_vec, 1)

            def p_done(s, ins):
                p_mark(ins)
                dve.wait_ge(p_vec, count(s, NP_VEC, p_links[0] - 1))

            def p_step(s, k):
                def take(u):
                    bank, n = p_use(s, u)
                    dve.wait_ge(p_full[bank], n + 1)
                    return bank, n

                if k == 0:
                    p_links[0] = 0
                    for t in range(KT):
                        bank, n = take(t)
                        nc.vector.tensor_copy(xT[:, t, :], p_bank(bank)).then_inc(p_taken[bank], 1)
                if 1 <= k <= 4:
                    t = k - 1
                    bank, n = take(2 + t)
                    dve.wait_ge(part0, count(s, 4, t))
                    if t >= 2:
                        dve.wait_ge(part2, count(s, 4, t - 2))
                    nc.vector.scalar_tensor_tensor(out=qk_rest[:, t % 2, :], in0=p_bank(bank),
                                                   scalar=bqk[:, t:t + 1], in1=parts[:, 0, t, :],
                                                   op0=ALU.add, op1=ALU.subtract).then_inc(p_taken[bank], 1)
                if k == 4:
                    for t in range(KT):
                        bank, n = p_use(s, t)
                        dve.wait_ge(p_taken[bank], n + 1)
                    p_done(s, nc.vector.tensor_reduce(pooled[:, :, :].rearrange("p t l -> p (t l)"),
                                                      xT[:, :, :].rearrange("p t n -> p (t n)").rearrange(
                                                          "p (l c) -> p l c", c=CHUNK), X, ALU.add))
                if k == 5:
                    bank, n = take(6)
                    nc.vector.tensor_scalar(rqT[:, :], p_bank(bank)[0:LD, :], brq[:, :], None, ALU.add
                                            ).then_inc(p_taken[bank], 1)
                    bank, n = take(7)
                    nc.vector.tensor_scalar(rkv_sb[:, :], p_bank(bank)[:, 0:LAT], 1.0 / CHUNK, brkv[:, :],
                                            ALU.mult, ALU.add).then_inc(p_taken[bank], 1)
                    dve.wait_ge(p_taken[bank], n + 1)
                    nc.vector.tensor_tensor(lat_bd[:, :, :],
                                            rkv_sb[:, :].unsqueeze(1).to_broadcast([P, LH, LAT]),
                                            diag_mask[:, :, :], ALU.mult).then_inc(bd_ready, 1)
                if k == 6 or k == 7:
                    b2 = k - 6
                    bank, n = take(8 + b2)
                    blocks = slice(2 * b2, 2 * b2 + 2)
                    p_done(s, nc.vector.tensor_reduce(lat_st[:, 0, blocks, :].rearrange("p b h -> p (b h)"),
                                                      p_bank(bank).rearrange("p (g l) -> p g l", l=LAT),
                                                      X, ALU.max, negate=True))
                    nc.vector.tensor_tensor(
                        lat_p[:, blocks, :, :].rearrange("p b h l -> p (b h) l"),
                        p_bank(bank).rearrange("p (g l) -> p g l", l=LAT),
                        lat_st[:, 0, blocks, :].rearrange("p b h -> p (b h)").unsqueeze(2).to_broadcast(
                            [P, 2 * LH, LAT]), ALU.add).then_inc(p_taken[bank], 1)
                if 8 <= k <= 11:
                    b = k - 8
                    bank, n = take(10 + b)
                    nc.vector.tensor_tensor(Vp[:, s.par, b, 0:H * VW], p_bank(bank)[:, 0:H * VW],
                                            bv[:, :, :].rearrange("p h d -> p (h d)"), ALU.add
                                            ).then_inc(p_taken[bank], 1)
                if k == 12:
                    dve.wait_ge(lat_exp, count(s, 2, 1))
                    flat = lat_p[:, :, :, :].rearrange("p b h l -> p (b h) l")
                    st = [lat_st[:, j, :, :].rearrange("p b h -> p (b h)") for j in range(3)]
                    p_done(s, nc.vector.tensor_reduce(st[1], flat, X, ALU.add))
                    p_done(s, nc.vector.reciprocal(st[2], st[1]))
                    p_done(s, nc.vector.tensor_tensor(st[1], st[2], live[:, :, :].rearrange("p b h -> p (b h)"),
                                                      ALU.mult))
                    nc.vector.tensor_tensor(flat, flat, st[1].unsqueeze(2).to_broadcast([P, NB * LH, LAT]),
                                            ALU.mult).then_inc(lat_norm, 1)
                    assert p_links[0] == NP_VEC
                if 15 <= k <= 18:
                    b = k - 15
                    bank, n = take(18 + b)
                    nc.vector.tensor_tensor(rem[:, s.par, b, :], p_bank(bank)[:, 0:RW], brem[:, :], ALU.add
                                            ).then_inc(p_taken[bank], 1)

            def maxima(s, v):
                slot, k = work_use(s, "A", v)
                dve.wait_ge(w_full[slot], k + 1)
                b, pair = v // (H // 2), v % (H // 2)
                nc.vector.tensor_reduce(nmax[:, b, 2 * pair:2 * pair + 2],
                                        work[:, slot, 0:2 * BAND].rearrange("p (h c) -> p h c", h=2),
                                        X, ALU.max, negate=True).then_inc(w_taken[slot], 1)

            def max_low(s, t):
                slot, k = work_use(s, "T", t)
                dve.wait_ge(nmax_hi, count(s, 2, t))
                cols = slice(2 * P * t, 2 * P * (t + 1))
                nc.vector.tensor_tensor(nmaxT[:, 1, cols], work[0:H, slot, 0:2 * P], nmaxT[:, 0, cols],
                                        ALU.subtract).then_inc(w_taken[slot], 1)

            def take_o(s, hg):
                slot, k = work_use(s, "O", hg)
                dve.wait_ge(w_full[slot], k + 1)
                nc.vector.tensor_copy(
                    o_tok[:, :, 4 * hg:4 * hg + 4, :],
                    work[:, slot, :].rearrange("p (b h d) -> p b h d", b=NB, h=4)[:, :, :, 0:VW]
                ).then_inc(w_taken[slot], 1)

            def f_step(s, k):
                def mark(ins):
                    f_links[0] += 1
                    ins.then_inc(f_vec, 1)

                def sync():
                    dve.wait_ge(f_vec, count(s, NF_VEC, f_links[0] - 1))

                def done(ins):
                    mark(ins)
                    sync()

                def take(u):
                    slot, n = work_use(s, "F", u)
                    dve.wait_ge(w_full[slot], n + 1)
                    return slot, n

                if k == 0:
                    f_links[0] = 0
                    take_o(s, HG - 1)
                    for hg in range(2, 4):
                        slot, n = work_use(s, "O", hg)
                        dve.wait_ge(w_taken[slot], n + 1)
                    z, e, ng, r, a = (gate[:, j, :, :] for j in range(5))
                    done(nc.vector.tensor_tensor(e, o_tok[:, :, :, HD], dead[:, :, :], ALU.add))
                    done(nc.vector.reciprocal(r, e))
                    done(nc.vector.tensor_tensor(a, o_tok[:, :, :, HD + 1], r, ALU.mult))
                    nc.vector.tensor_tensor(z, a, rem[:, s.par, :, D:RW], ALU.add).then_inc(gate_z, 1)
                    dve.wait_ge(gate_e, count(s, 1, 0))
                    done(nc.vector.tensor_scalar(z, e, 1.0, None, ALU.add))
                    done(nc.vector.reciprocal(e, z))
                    mark(nc.vector.tensor_tensor(a, e, r, ALU.mult))
                    nc.vector.tensor_scalar(ng, e, -1.0, 1.0, ALU.mult, ALU.add).then_inc(gate_g, 1)
                    sync()
                    for b in range(NB):
                        ins = nc.vector.tensor_tensor(mixed[:, b, :].rearrange("p (h d) -> p h d", h=H),
                                                      o_tok[:, b, :, 0:HD],
                                                      a[:, b, :].unsqueeze(2).to_broadcast([P, H, HD]), ALU.mult)
                    done(ins)
                    dve.wait_ge(rem_part, count(s, 1, 0))
                    nc.vector.tensor_tensor(mixed[:, :, :], mixed[:, :, :], rem[:, s.par, :, 0:D], ALU.add
                                            ).then_inc(mixed_ready, 1)
                if k == 2:
                    dve.wait_ge(xres_done, count(s, 1, 0))
                    if not s.first:
                        dve.wait_ge(y_out, count(s, 1, -1) * 16)
                    for t in range(2):
                        slot, n = take(2 + t)
                        blocks = slice(2 * t, 2 * t + 2)
                        nc.vector.tensor_tensor(ytok[:, blocks, :].rearrange("p b d -> p (b d)"),
                                                work[:, slot, :],
                                                xres[:, blocks, :].rearrange("p b d -> p (b d)"), ALU.add
                                                ).then_inc(w_taken[slot], 1)
                        dve.wait_ge(w_taken[slot], n + 1)
                        for b in range(2 * t, 2 * t + 2):
                            last_stats = nc.vector.bn_stats(stats[:, b, :], ytok[:, b, :])
                    mark(last_stats)
                    wait_alone(dve, f_vec, count(s, NF_VEC, f_links[0] - 1))
                    for b in range(NB):
                        ins = nc.vector.bn_aggr(mv[:, b, :], stats[:, b, :])
                    done(ins)
                    nc.vector.tensor_scalar(rs[:, 3, :], mv[:, :, 1], EPS, None, ALU.add).then_inc(var_ready, 1)
                    dve.wait_ge(rstd_ready, count(s, 1, 0))
                    done(nc.vector.tensor_tensor(rs[:, 2, :], rs[:, 0, :], rs[:, 1, :], ALU.mult))
                    done(nc.vector.tensor_scalar(rs[:, 3, :], rs[:, 2, :], 1e-8, None, ALU.add))
                    done(nc.vector.reciprocal(rs[:, 2, :], rs[:, 3, :]))
                    done(nc.vector.tensor_tensor(rs[:, 1, :], rs[:, 2, :], rs[:, 0, :], ALU.mult))
                    for b in range(NB):
                        nc.vector.tensor_scalar(x1[:, b, :], ytok[:, b, :], mv[:, b, 0:1], rs[:, 0, b:b + 1],
                                                ALU.subtract, ALU.mult)
                        ins = nc.vector.tensor_scalar(ytok[:, b, :], ytok[:, b, :], mv[:, b, 0:1],
                                                      rs[:, 1, b:b + 1], ALU.subtract, ALU.mult)
                    ins.then_inc(xn_ready, 1)
                if k == 3:
                    for t in range(KT):
                        slot, n = take(4 + t)
                        dve.wait_ge(xn_hi, count(s, KT, t))
                        nc.vector.tensor_tensor(xnT[:, 1, t, :], work[:, slot, :], xnT[:, 0, t, :], ALU.subtract
                                                ).then_inc(w_taken[slot], 1)
                if 4 <= k < 4 + FT:
                    t = k - 4
                    slot, n = work_use(s, "F", 6 + t)
                    dve.wait_ge(w_taken[slot], n + 1)
                    if t >= NR:
                        dve.wait_ge(down_done, count(s, FT, t - NR))
                    nc.vector.tensor_copy(h_hi[:, t % NR, :], hbuf[:, t % 2, :]).then_inc(h_hi_ready, 1)
                    if t > 0:
                        dve.wait_ge(h_sq, count(s, FT, t))
                        if t > 1:
                            dve.wait_ge(h_added, count(s, FT - 1, t - 2))
                        nc.vector.tensor_tensor(h_sum[:, :], h_sum[:, :], hsq[:, t % 2, :], ALU.add
                                                ).then_inc(h_added, 1)
                if k == 12:
                    slot, n = take(14)
                    nc.vector.tensor_scalar(rs[:, 3, :], work[:, slot, 0:NB], 1.0 / F, None, ALU.mult
                                            ).then_inc(w_taken[slot], 1)
                    dve.wait_ge(w_taken[slot], n + 1)
                    dve.sem_inc(ssq_mean, 1)
                    dve.wait_ge(hroot, count(s, 1, 0))
                    done(nc.vector.tensor_scalar(rs[:, 3, :], rs[:, 2, :], 1e-8, None, ALU.add))
                    done(nc.vector.reciprocal(rs[:, 2, :], rs[:, 3, :]))
                    dve.wait_ge(down_done, count(s, FT, FT - 1))
                    for b in range(NB):
                        ins = nc.vector.scalar_tensor_tensor(
                            out=ytok[:, b, :], in0=oacc[:, b // 2, (b % 2) * D:(b % 2 + 1) * D],
                            scalar=rs[:, 2, b:b + 1], in1=x1[:, b, :], op0=ALU.mult, op1=ALU.add)
                    ins.then_inc(y2_ready, 1)
                    assert f_links[0] == NF_VEC, f_links

            def statistics_before(s):
                dve.wait_ge(y2_ready, count(s, 1, -1))
                for b in range(NB):
                    ins = nc.vector.bn_stats(stats[:, b, :], ytok[:, b, :])
                ins.then_inc(y2_vec, 1)
                wait_alone(dve, y2_vec, count(s, 2, -2))
                for b in range(NB):
                    ins = nc.vector.bn_aggr(mv[:, b, :], stats[:, b, :])
                ins.then_inc(y2_vec, 1)
                dve.wait_ge(y2_vec, count(s, 2, -1))
                nc.vector.tensor_scalar(rs[:, 3, :], mv[:, :, 1], EPS, None, ALU.add).then_inc(var2_ready, 1)

            def finish_before(s):
                dve.wait_ge(rstd2_ready, count(s, 1, -1))
                for b in range(NB):
                    nc.vector.tensor_scalar(ytok[:, b, :], ytok[:, b, :], mv[:, b, 0:1], rs[:, 0, b:b + 1],
                                            ALU.subtract, ALU.mult).then_inc(y_ready, 1)

            def body(s):
                for u in range(FIRST_HALF):
                    if u == STAT_AT and not s.first:
                        statistics_before(s)
                    if u == STAT_AT + 2 and not s.first:
                        finish_before(s)
                    for v in (2 * u, 2 * u + 1):
                        if v < NM and not s.last:
                            maxima(s.next(), v)
                    if u >= 7 and (u - 7) % NB == 0 and (u - 7) // NB < HG - 1:
                        take_o(s, (u - 7) // NB)
                    if not s.last:
                        for t in range(2):
                            if u == (9, NM // 2)[t]:
                                max_low(s.next(), t)
                later = s.second_next()
                for phase, k in SECOND_HALF:
                    if phase == "F":
                        f_step(s, k)
                    elif later.exists:
                        p_step(later, k)

            for s in (Seq(0, 0, 0), Seq(1, 1, 0)):
                for k in range(NSTEP_P):
                    p_step(s, k)
            for phase, k in WORK_A:
                (maxima if phase == "A" else max_low)(Seq(0, 0, 0), k)
            over_sequences(dve, body)
            statistics_before(Seq(B, 0, B // 2))
            finish_before(Seq(B, 0, B // 2))

        @block.tensor
        def _(pe):
            pe.wait_ge(w_in, W_ALL)
            pe.wait_ge(consts, 1)
            for k in range(2):
                pe.wait_ge(tern, k + 1)
                if k:
                    pe.wait_ge(wt_done, 1)
                for a in range(2):
                    for b in range(2):
                        for c in range(4):
                            t = 4 * b + c
                            src = ternary[0][:, t * D + a * P:t * D + (a + 1) * P] if k == 0 else \
                                ternary[1][:, a * F + t * P:a * F + (t + 1) * P]
                            mm = nc.tensor.transpose(scores[:, a, b, c * P:(c + 1) * P], src, ident[:, :])
                mm.then_inc(tern_T, 1)
            pe.wait_ge(wt_done, 2)
            pe.wait_ge(prep_done, 1)

            def work_bank(s, phase, u):
                slot, k = work_use(s, phase, u)
                if not (isinstance(k, int) and k == 0):
                    pe.wait_ge(w_taken[slot], k)
                return slot

            def bank_p(s, u):
                bank, k = p_use(s, u)
                if u < 4 and not (s.known and s.i < 2):
                    pe.wait_ge(s_taken[bank // 2], (s.i - 1) * (NU // 2))
                if not (isinstance(k, int) and k == 0):
                    pe.wait_ge(p_taken[bank], k)
                return bank

            def product(out, lhs, rhs, n=KT):
                for t in range(n):
                    mm = nc.tensor.matmul(out, lhs(t), rhs(t), start=(t == 0), stop=(t == n - 1))
                return mm

            def p_taken_by(s, *us):
                for u in us:
                    bank, n = p_use(s, u)
                    pe.wait_ge(p_taken[bank], n + 1)

            def p_step(s, k):
                if k == 0:
                    pe.wait_ge(x_in, count(s, 1, 0) * 16)
                    for t in range(KT):
                        bank = bank_p(s, t)
                        for b in range(NB):
                            mm = nc.tensor.transpose(p_bank(bank)[:, b * P:(b + 1) * P],
                                                     xtok[:, b, t * P:(t + 1) * P], ident[:, :])
                        mm.then_inc(p_full[bank], 1)
                if k == 1:
                    p_taken_by(s, 0, 1)
                if 1 <= k <= 4:
                    c = k - 1
                    bank = bank_p(s, 2 + c)
                    product(p_bank(bank), lambda t: wqk[:, t, c * P:(c + 1) * P], lambda t: xT[:, t, :]
                            ).then_inc(p_full[bank], 1)
                if k == 5:
                    bank = bank_p(s, 6)
                    product(p_bank(bank)[0:LD, :], lambda t: wrq[:, t, :], lambda t: xT[:, t, :]
                            ).then_inc(p_full[bank], 1)
                    bank = bank_p(s, 7)
                    pe.wait_ge(p_vec, count(s, NP_VEC, 0))
                    product(p_bank(bank)[:, 0:LAT], lambda t: wrkv[:, t, :], lambda t: pooled[:, t, :]
                            ).then_inc(p_full[bank], 1)
                if k == 6:
                    p_taken_by(s, 6)
                    pe.wait_ge(bd_ready, count(s, 1, 0))
                if k == 6 or k == 7:
                    b2 = k - 6
                    bank = bank_p(s, 8 + b2)
                    for b in range(2 * b2, 2 * b2 + 2):
                        o = p_bank(bank)[:, (b % 2) * LH * LAT:(b % 2 + 1) * LH * LAT]
                        nc.tensor.matmul(o, rqT[:, b * P:(b + 1) * P],
                                         lat_bd[0:LD, :, :].rearrange("p h l -> p (h l)"),
                                         start=(b % 2 == 0), stop=False, skip_group_check=True)
                        mm = nc.tensor.matmul(o.rearrange("p (h l) -> p h l", h=LH), identb[:, :],
                                              lat_mask[:, b, :].unsqueeze(1).to_broadcast([P, LH, LAT]),
                                              start=False, stop=(b % 2 == 1), skip_group_check=True)
                    mm.then_inc(p_full[bank], 1)
                if 8 <= k <= 11:
                    b = k - 8
                    bank = bank_p(s, 10 + b)
                    product(p_bank(bank)[:, 0:H * VW], lambda t: xT[:, t, b * P:(b + 1) * P],
                            lambda t: wv[:, t, :, :].rearrange("p h d -> p (h d)")).then_inc(p_full[bank], 1)
                if k == 12:
                    for t in range(2):
                        bank = bank_p(s, 14 + t)
                        nc.tensor.matmul(p_bank(bank)[:, 0:RW],
                                         lat_bd[LD:2 * LD, 2 * t:2 * t + 2, :].rearrange("p h l -> p (h l)"),
                                         wro[LD:2 * LD, :], start=True, stop=True).then_inc(p_full[bank], 1)
                if k == 13:
                    pe.wait_ge(lat_norm, count(s, 1, 0))
                if k == 13 or k == 14:
                    t = k - 13
                    bank = bank_p(s, 16 + t)
                    for b in range(2 * t, 2 * t + 2):
                        for c in range(2):
                            q = (b % 2) * 2 + c
                            mm = nc.tensor.transpose(
                                p_bank(bank)[:, q * P:(q + 1) * P],
                                lat_p[:, b, 2 * c:2 * c + 2, :].rearrange("p h l -> p (h l)"), ident[:, :])
                    mm.then_inc(p_full[bank], 1)
                if k == 15:
                    p_taken_by(s, 14, 15, 16, 17)
                if 15 <= k <= 18:
                    b = k - 15
                    bank = bank_p(s, 18 + b)
                    product(p_bank(bank)[:, 0:RW], lambda t: lat_pT[:, b, t, :], lambda t: rvr[:, t, :], 2
                            ).then_inc(p_full[bank], 1)

            def max_scores(s, v):
                b, pair = v // (H // 2), v % (H // 2)
                if v == 0:
                    pe.wait_ge(stacks_in[s.par], (s.half + 1) * (16 * 2 * len(QPART)))
                q, kk = Qs[s.par], Ks[s.par]
                slot = work_bank(s, "A", v)
                for hh in range(2):
                    for g in range(P // GQ):
                        h, at = 2 * pair + hh, b * P + g * GQ
                        nc.tensor.matmul(work[g * GQ:(g + 1) * GQ, slot, hh * BAND:(hh + 1) * BAND],
                                         q[0:KA, h, at:at + GQ], kk[0:KA, h, at:at + BAND],
                                         start=(hh == 0), stop=False, skip_group_check=True)
                o = work[:, slot, 0:2 * BAND]
                if b:
                    o = o.rearrange("p (h c w) -> p h c w", h=2, w=GQ)[:, :, 0:3:2, :]
                    m = mask_edge[:, :, :].unsqueeze(1).to_broadcast([P, 2, 2, GQ])
                else:
                    o = o.rearrange("p (h c) -> p h c", h=2)
                    m = mask_first[:, :].unsqueeze(1).to_broadcast([P, 2, BAND])
                nc.tensor.matmul(o, identb[:, :], m, start=False, stop=True, skip_group_check=True
                                 ).then_inc(w_full[slot], 1)

            def maxima_T(s, t):
                slot, k = work_use(s, "A", NM // 2 * (t + 1) - 1)
                pe.wait_ge(w_taken[slot], k + 1)
                slot = work_bank(s, "T", t)
                for b in range(2):
                    mm = nc.tensor.transpose(work[0:H, slot, b * P:(b + 1) * P], nmax[:, 2 * t + b, :],
                                             ident[:, :])
                mm.then_inc(w_full[slot], 1)

            def scores_T(s, u):
                q, kk = Qs[s.par], Ks[s.par]
                hg, j = u // NB, u % NB
                slot, k = score_use(s, u)
                if u < 2 and not s.last:
                    for bank in (2 * slot, 2 * slot + 1):
                        pe.wait_ge(p_taken[bank], count(s.next(), P_PER[bank], P_PER[bank] - 1))
                if not (isinstance(k, int) and k == 0):
                    pe.wait_ge(s_taken[slot], k)
                w = 2 * P if j < NB - 1 else P
                for c in range(4):
                    mm = nc.tensor.matmul(scores[:, slot, c // 2, (c % 2) * 2 * P:(c % 2) * 2 * P + w],
                                          kk[0:KB, 4 * hg + c, P + j * P:2 * P + j * P],
                                          q[0:KB, 4 * hg + c, j * P:j * P + w], start=True, stop=True)
                mm.then_inc(s_full[slot], 1)

            def weigh(s, v):
                hg, j = v // NB, v % NB
                if j == 0 and hg < 2 and not s.first:
                    pe.wait_ge(y2_ready, count(s, 1, -1))
                if j == 0 and hg >= 2:
                    pe.wait_ge(oT_ready, count(s, HG, hg - 2))
                pe.wait_ge(masked, count(s, NU, v))
                w = 2 * P if j < NB - 1 else P
                for c in range(4):
                    h = 4 * hg + c
                    mm = nc.tensor.matmul(oacc[c * PVW:(c + 1) * PVW, hg % 2, j * P:j * P + w],
                                          Vp[:, s.par, j, h * VW:h * VW + PVW],
                                          Pt[:, v % NPT, c, 0:w], start=(j == 0), stop=(j == NB - 1),
                                          skip_group_check=True)
                mm.then_inc(pv_done, 1)

            def transpose_o(s, hg):
                pe.wait_ge(oT_ready, count(s, HG, hg))
                slot = work_bank(s, "O", hg)
                for b in range(NB):
                    mm = nc.tensor.transpose(work[:, slot, b * P:(b + 1) * P], oT[:, b * P:(b + 1) * P],
                                             ident[:, :])
                mm.then_inc(w_full[slot], 1)

            def down(s, f):
                pe.wait_ge(h_lo_ready, count(s, FT, f))
                for b in range(NB):
                    for j in range(2):
                        mm = nc.tensor.matmul(oacc[:, b // 2, (b % 2) * D:(b % 2 + 1) * D],
                                              (h_hi, h_lo)[j][:, f % NR, b * P:(b + 1) * P], wdn_t[:, f, :],
                                              start=(f == 0 and b % 2 == 0 and j == 0),
                                              stop=(f == FT - 1 and b % 2 == 1 and j == 1),
                                              skip_group_check=True)
                mm.then_inc(down_done, 1)

            def f_step(s, k):
                if k == 0:
                    transpose_o(s, HG - 1)
                if k == 1:
                    pe.wait_ge(mixed_ready, count(s, 1, 0))
                    for t in range(KT):
                        slot = work_bank(s, "F", t)
                        for b in range(NB):
                            mm = nc.tensor.transpose(work[:, slot, b * P:(b + 1) * P],
                                                     mixed[:, b, t * P:(t + 1) * P], ident[:, :])
                        mm.then_inc(w_full[slot], 1)
                if k == 2:
                    for t in range(KT):
                        slot, n = work_use(s, "F", t)
                        pe.wait_ge(w_taken[slot], n + 1)
                    for c in range(2):
                        slot = work_bank(s, "F", 2 + c)
                        for b in range(2 * c, 2 * c + 2):
                            mm = product(work[:, slot, (b % 2) * D:(b % 2 + 1) * D],
                                         lambda t: mixT[:, t, b * P:(b + 1) * P], lambda t: wout[:, t, :])
                        mm.then_inc(w_full[slot], 1)
                if k == 3:
                    pe.wait_ge(xn_ready, count(s, 1, 0))
                    for t in range(KT):
                        slot = work_bank(s, "F", 4 + t)
                        for b in range(NB):
                            mm = nc.tensor.transpose(work[:, slot, b * P:(b + 1) * P],
                                                     ytok[:, b, t * P:(t + 1) * P], ident[:, :])
                        mm.then_inc(w_full[slot], 1)
                if k == 4:
                    for t in range(KT):
                        slot, n = work_use(s, "F", 4 + t)
                        pe.wait_ge(w_taken[slot], n + 1)
                    pe.wait_ge(oT_ready, count(s, HG, HG - 1))
                if 4 <= k < 4 + FT:
                    f = k - 4
                    slot = work_bank(s, "F", 6 + f)
                    product(work[:, slot, :], lambda t: wup_t[:, t % KT, f * P:(f + 1) * P],
                            lambda t: xnT[:, t // KT, t % KT, :], 2 * KT).then_inc(w_full[slot], 1)
                    if f >= TRAIL:
                        down(s, f - TRAIL)
                if k == 12:
                    for f in range(FT - TRAIL, FT):
                        if f == FT - 1:
                            pe.wait_ge(h_added, count(s, FT - 1, FT - 2))
                            slot = work_bank(s, "F", 14)
                            for b in range(NB):
                                mm = nc.tensor.matmul(work[:, slot, b:b + 1], h_sum[:, b * P:(b + 1) * P],
                                                      ones_col[:, :], start=True, stop=True)
                            mm.then_inc(w_full[slot], 1)
                        down(s, f)

            def body(s):
                pe.wait_ge(nmax_in[s.par], (s.half + 1) * 16)
                for u in range(FIRST_HALF):
                    if u < NU:
                        scores_T(s, u)
                    if 2 * u < NM and not s.last:
                        max_scores(s.next(), 2 * u)
                    if u >= 2:
                        weigh(s, u - 2)
                    if 2 * u < NM and not s.last:
                        max_scores(s.next(), 2 * u + 1)
                    if u >= 7 and (u - 7) % NB == 0 and (u - 7) // NB < HG - 1:
                        transpose_o(s, (u - 7) // NB)
                    if not s.last:
                        for t in range(2):
                            if u == (9, NM // 2)[t]:
                                maxima_T(s.next(), t)
                later = s.second_next()
                for phase, k in SECOND_HALF:
                    if phase == "F":
                        f_step(s, k)
                    elif later.exists:
                        p_step(later, k)

            for s in (Seq(0, 0, 0), Seq(1, 1, 0)):
                for k in range(NSTEP_P):
                    p_step(s, k)
            for phase, k in WORK_A:
                (max_scores if phase == "A" else maxima_T)(Seq(0, 0, 0), k)
            over_sequences(pe, body)


INPUTS = ["L0_attn_x", "L0_attn_qkv_w", "L0_attn_qkv_b", "L0_attn_rq_w", "L0_attn_rq_b", "L0_attn_rkv_w",
          "L0_attn_rkv_b", "L0_attn_rout_w", "L0_attn_rout_b", "L0_attn_out_w", "L0_attn_out_b",
          "L0_attn_gl_w", "L0_attn_gr_w", "L0_ffn_w_up", "L0_ffn_w_down"]


def kernel(**inputs):
    import numpy as np
    import concourse.bacc as bacc
    from concourse.bass_utils import run_bass_kernel_spmd

    nc = bacc.Bacc("TRN2", target_bir_lowering=False, num_devices=1)
    arrays, args = {}, []
    for name in INPUTS:
        a = np.ascontiguousarray(inputs[name])
        arrays[name] = a
        args.append(nc.dram_tensor(name, a.shape, mybir.dt.from_np(a.dtype), kind="ExternalInput").ap())
    out = nc.dram_tensor("y", (B, S, D), F32, kind="ExternalOutput").ap()
    build(nc, *args, out)
    r = run_bass_kernel_spmd(nc, [arrays], core_ids=[0])
    return r.results[0]["y"]
```

```python
from contextlib import ExitStack

import numpy as np

import concourse.bass as bass
from concourse import mybir

ALU = mybir.AluOpType
ACT = mybir.ActivationFunctionType
F32 = mybir.dt.float32
BF16 = mybir.dt.bfloat16
F16 = mybir.dt.float16
X = mybir.AxisListType.X
RADD = bass.bass_isa.ReduceOp.add

P = 128
NEG = -1.0e30
EPS = 1e-5

B, S, D = 16, 512, 256
H, HD = 16, 16
LH, LHD, LAT = 4, 16, 64
LD = LH * LHD
F = 1024
NB = S // P
KT = D // P
FT = F // P
CHUNK = S // LAT
SCALE = float(HD) ** -0.5
LSCALE = float(LHD) ** -0.5
VW = HD + 2
RW = D + H
PVW = 32

QPART = (0, 0, 0, 1, 1, 2)
KPART = (0, 1, 2, 0, 1, 0)
ROWS = HD * len(QPART)
EXC = ROWS
MAXR = ROWS + 1
KA, KB = ROWS + 1, ROWS + 3
GQ = 64
BAND = GQ + P

HG = H // 4
NU = HG * NB
NPT = 3
NM = NB * H // 2
NR = 3
TRAIL = 2
NP_VEC, NF_VEC = 6, 14

X_T, QK, LAT_IN, LAT_SCORES, VALUES, LAT_V, LAT_T, REMOTE = 0, 1, 5, 6, 8, 12, 13, 15
NSTEP_P = REMOTE + NB
GATE, MIX, MIX_T, OUT, NORM, XN_T, UP = 0, 1, 2, 3, 4, 5, 6
END = UP + FT
SECOND_HALF = (
    ("P", X_T), ("F", GATE), ("P", QK), ("F", MIX), ("P", QK + 1), ("P", QK + 2), ("P", QK + 3),
    ("F", MIX_T), ("P", LAT_IN), ("F", OUT), ("P", VALUES), ("P", VALUES + 1), ("P", LAT_SCORES),
    ("F", NORM), ("P", LAT_SCORES + 1), ("P", VALUES + 2), ("P", VALUES + 3), ("F", XN_T),
    ("P", LAT_V), ("F", UP), ("F", UP + 1), ("P", LAT_T), ("F", UP + 2), ("P", LAT_T + 1),
    ("F", UP + 3), ("P", REMOTE), ("F", UP + 4), ("P", REMOTE + 1), ("F", UP + 5), ("P", REMOTE + 2),
    ("F", UP + 6), ("P", REMOTE + 3), ("F", UP + 7), ("F", END))
STEPS_P = [k for phase, k in SECOND_HALF if phase == "P"]
STEPS_P_FIRST = [X_T, QK, QK + 1, QK + 2, QK + 3, LAT_IN, VALUES, VALUES + 1, VALUES + 2, LAT_SCORES,
                 LAT_SCORES + 1, LAT_V, VALUES + 3, LAT_T, LAT_T + 1] + [REMOTE + b for b in range(NB)]
assert sorted(STEPS_P) == sorted(STEPS_P_FIRST) == list(range(NSTEP_P))
assert [k for phase, k in SECOND_HALF if phase == "F"] == list(range(END + 1))
STAT_AT = 3
FIRST_HALF = NU + 2

P_RESULTS = {X_T: [0, 1], LAT_IN: [6, 7], LAT_V: [14, 15]}
P_RESULTS |= {QK + c: [2 + c] for c in range(4)} | {LAT_SCORES + c: [8 + c] for c in range(2)}
P_RESULTS |= {VALUES + b: [10 + b] for b in range(NB)} | {LAT_T + t: [16 + t] for t in range(2)}
P_RESULTS |= {REMOTE + b: [18 + b] for b in range(NB)}
P_ORDER = [r for k in STEPS_P for r in P_RESULTS[k]]
P_ORDER_FIRST = [r for k in STEPS_P_FIRST for r in P_RESULTS[k]]
P_PER = [len(P_ORDER[b::4]) for b in range(4)]


def order_of_work():
    order = []
    for u in range(FIRST_HALF):
        for v in (2 * u, 2 * u + 1):
            if v < NM:
                order.append(("A", v))
        if u >= 7 and (u - 7) % NB == 0:
            order.append(("O", (u - 7) // NB))
        if u == 9:
            order.append(("T", 0))
        if u == NM // 2:
            order.append(("T", 1))
    return order + [("O", HG - 1)] + [("F", k) for k in range(15)]


WORK_ALL = order_of_work()
WORK_A = [x for x in WORK_ALL if x[0] in "AT"]
WORK_LAST = [x for x in WORK_ALL if x[0] in "OF"]
WORK_PER = [len(WORK_ALL[b::2]) for b in range(2)]


def order_of_prologue():
    order = []
    for k in STEPS_P_FIRST:
        order.append(("P0", k))
        order += [("W", j) for j, after in enumerate(TERNARY_AFTER) if after == k]
    order += [("W", 2), ("W", 3)]
    rest = list(WORK_A)
    for n, k in enumerate(STEPS_P_FIRST):
        order.append(("P1", k))
        if n >= 4:
            order, rest = order + rest[:3], rest[3:]
    return order + rest


TERNARY_AFTER = (QK + 3, VALUES + 3)
PROLOGUE = order_of_prologue()


class Seq:

    def __init__(self, i, par, half):
        self.i, self.par, self.half = i, par, half
        self.known = isinstance(i, int)
        self.first = self.known and i == 0
        self.last = self.known and i == B - 1
        self.exists = not self.known or i < B

    def next(self):
        return Seq(self.i + 1, 1 - self.par, self.half + self.par)

    def before(self):
        return Seq(self.i - 1, 1 - self.par, self.half - (1 - self.par))

    def second_next(self):
        return Seq(self.i + 2, self.par, self.half + 1)


def count(s, per, k):
    return s.i * per + (k + 1)


def work_use(s, phase, k):
    if phase in "AT" and s.first:
        at = WORK_A.index((phase, k))
        return at % 2, at // 2
    at = (WORK_LAST if s.last and phase in "OF" else WORK_ALL).index((phase, k))
    slot = at % 2
    before = len(WORK_A[slot::2])
    if phase in "AT":
        before -= WORK_PER[slot]
    return slot, s.i * WORK_PER[slot] + (before + at // 2)


def p_use(s, result):
    at = (P_ORDER_FIRST if s.known and s.i < 2 else P_ORDER).index(result)
    return at % 4, s.i * P_PER[at % 4] + at // 4


def score_use(s, u):
    return u % 2, s.i * (NU // 2) + u // 2


def over_sequences(eng, body):
    body(Seq(0, 0, 0))
    body(Seq(1, 1, 0))
    with eng.Fori(1, B // 2 - 1) as pair:
        body(Seq(pair * 2, 0, pair))
        body(Seq(pair * 2 + 1, 1, pair))
    body(Seq(B - 2, 0, B // 2 - 1))
    body(Seq(B - 1, 1, B // 2 - 1))


def build(nc, x, qkv_w, qkv_b, rq_w, rq_b, rkv_w, rkv_b, rout_w, rout_b, out_w, out_b, gl_w, gr_w,
          w_up, w_down, out):
    with ExitStack() as ctx:
        def sb(name, shape, dt=F32):
            return ctx.enter_context(nc.sbuf_tensor(name, shape, dt))

        def sem(name):
            return ctx.enter_context(nc.semaphore(name))

        ident = sb("ident", [P, P])
        identb = sb("identb", [P, P], BF16)
        ones_col = sb("ones_col", [P, 1])
        power = sb("power", [P, 2, NB])
        mask_edge = sb("mask_edge", [P, 2, GQ], BF16)
        mask_first = sb("mask_first", [P, BAND], BF16)
        lat_mask = sb("lat_mask", [P, NB, LAT], BF16)
        diag_mask = sb("diag_mask", [P, LH, LAT])
        dead = sb("dead", [P, NB, H])
        live = sb("live", [P, NB, LH])
        wqk = sb("wqk", [P, KT, 2 * D])
        wv = sb("wv", [P, KT, H, VW])
        wrq = sb("wrq", [P, KT, LD])
        wrkv = sb("wrkv", [P, KT, 2 * LD])
        wout = sb("wout", [P, KT, D])
        wro = sb("wro", [P, RW])
        bqk = sb("bqk", [P, 4])
        brq = sb("brq", [LD, 1])
        brkv = sb("brkv", [P, 1])
        bv = sb("bv", [P, H, VW])
        brem = sb("brem", [P, RW])
        bout = sb("bout", [P, D])
        glb = sb("glb", [P, HD])
        grb = sb("grb", [P, HD])
        wup_t = sb("wup_t", [P, KT, F], F16)
        wdn_t = sb("wdn_t", [P, FT, D], F16)
        alpha = sb("alpha", [P, 8])
        xtok = sb("xtok", [P, NB, D])
        xres = sb("xres", [P, NB, D])
        xT = sb("xT", [P, KT, S])
        pooled = sb("pooled", [P, KT, LAT])
        parts = sb("parts", [P, 3, 4, S], BF16)
        Qs = [sb(f"Qs{k}", [P, H, S], BF16) for k in range(2)]
        Ks = [sb(f"Ks{k}", [P, H, P + S], BF16) for k in range(2)]
        Vp = sb("Vp", [P, 2, NB, H * VW + PVW - VW])
        rqT = sb("rqT", [LD, S])
        rkv_sb = sb("rkv_sb", [P, LAT])
        lat_bd = sb("lat_bd", [P, LH, LAT])
        rvr = sb("rvr", [P, 2, RW])
        lat_st = sb("lat_st", [P, 3, NB, LH])
        rem = sb("rem", [P, 2, NB, RW])
        nmax = sb("nmax", [P, NB, H])
        nmaxT = sb("nmaxT", [H, 2, S], BF16)
        Pt = sb("Pt", [P, NPT, 4, 2 * P])
        oT = sb("oT", [P, S])
        o_tok = sb("o_tok", [P, NB, H, VW])
        gate = sb("gate", [P, 5, NB, H])
        ytok = sb("ytok", [P, NB, D])
        stats = sb("stats", [P, NB, 6])
        mv = sb("mv", [P, NB, 2])
        rs = sb("rs", [P, 5, NB])
        x1 = sb("x1", [P, NB, D])
        mixT = sb("mixT", [P, KT, S])
        xnT = sb("xnT", [P, 2, KT, S], F16)
        hbuf = sb("hbuf", [P, 2, S])
        hsq = sb("hsq", [P, 2, S])
        h_hi = sb("h_hi", [P, NR, S], F16)
        h_lo = sb("h_lo", [P, NR, S], F16)
        mixed = x1
        xn = mixT[:, :, :].rearrange("p t n -> p (t n)").rearrange("p (b d) -> p b d", b=NB)
        lat_p = Pt[:, 0, :, :].rearrange("p b (h l) -> p b h l", h=LH)
        qk_rest = Pt[:, 1, :, :].rearrange("p a b -> p (a b)").rearrange("p (t n) -> p t n", t=2)
        lat_pT = Pt[:, 2, :, :].rearrange("p b (t n) -> p b t n", t=2)
        h_sum = oT

        work = ctx.enter_context(nc.psum_tensor("work", [P, 2, 512], F32))
        scores = ctx.enter_context(nc.psum_tensor("scores", [P, 2, 2, 512], F32))
        oacc = ctx.enter_context(nc.psum_tensor("oacc", [P, 2, 512], F32))

        parts_dram = nc.dram_tensor("parts_scratch", [3, 2 * D, S], BF16, kind="Internal").ap()
        nmax_dram = nc.dram_tensor("nmax_scratch", [2, H, S], BF16, kind="Internal").ap()

        passed = sem("passed")
        w_in = sem("w_in")
        ff_in = sem("ff_in")
        ones_set = sem("ones_set")
        consts = sem("consts")
        alpha_part = sem("alpha_part")
        alpha_all = sem("alpha_all")
        tern = sem("tern")
        tern_T = sem("tern_T")
        wt_done = sem("wt_done")
        prep_done = sem("prep_done")
        q_consts = sem("q_consts")
        pool_chain = sem("pool_chain")
        vec_chain = sem("vec_chain")
        x_in = sem("x_in")
        xres_in = sem("xres_in")
        xres_done = sem("xres_done")
        w_full = [sem(f"w_full{k}") for k in range(2)]
        w_taken = [sem(f"w_taken{k}") for k in range(2)]
        p_full = [sem(f"p_full{k}") for k in range(4)]
        p_taken = [sem(f"p_taken{k}") for k in range(4)]
        p_vec = sem("p_vec")
        bd_ready = sem("bd_ready")
        part0 = sem("part0")
        part1 = sem("part1")
        part2 = sem("part2")
        parts_out = sem("parts_out")
        stacks_in = [sem(f"stacks_in{k}") for k in range(2)]
        lat_exp = sem("lat_exp")
        lat_norm = sem("lat_norm")
        s_full = [sem(f"s_full{k}") for k in range(2)]
        s_taken = [sem(f"s_taken{k}") for k in range(2)]
        nmax_hi = sem("nmax_hi")
        nmax_out = sem("nmax_out")
        nmax_in = [sem(f"nmax_in{k}") for k in range(2)]
        masked = sem("masked")
        pv_done = sem("pv_done")
        oT_ready = sem("oT_ready")
        f_vec = sem("f_vec")
        gate_z = sem("gate_z")
        gate_e = sem("gate_e")
        gate_g = sem("gate_g")
        rem_part = sem("rem_part")
        mixed_ready = sem("mixed_ready")
        var_ready = sem("var_ready")
        rstd_ready = sem("rstd_ready")
        var2_ready = sem("var2_ready")
        rstd2_ready = sem("rstd2_ready")
        x1_ready = sem("x1_ready")
        xn_ready = sem("xn_ready")
        xn_hi = sem("xn_hi")
        h_sq = sem("h_sq")
        h_hi_ready = sem("h_hi_ready")
        h_lo_ready = sem("h_lo_ready")
        h_added = sem("h_added")
        down_done = sem("down_done")
        y2_ready = sem("y2_ready")
        y2_vec = sem("y2_vec")
        ssq_mean = sem("ssq_mean")
        hroot = sem("hroot")
        y_ready = sem("y_ready")
        y_out = sem("y_out")

        START = {"P0": Seq(0, 0, 0), "P1": Seq(1, 1, 0)}
        block = ctx.enter_context(nc.Block())

        def p_bank(bank):
            return scores[:, bank // 2, bank % 2, :]

        nat_all = Qs[1][:, :, :].rearrange("p h n -> p (h n)").bitcast(F32)
        nat = nat_all[:, 0:FT * D], nat_all[:, FT * D:FT * D + KT * F]
        ternary = [t[:, :, :].rearrange("p k n -> p (k n)").bitcast(BF16) for t in (hbuf, hsq)]
        below = Vp[:, 1, :, :].rearrange("p b n -> p (b n)").bitcast(BF16)[:, 0:FT * D]

        def in_pairs(stack):
            return stack[:, :, :].bitcast(F32)

        ONE_PAIR = float(np.array([0x3F803F80], np.uint32).view(np.float32)[0])

        def rows_of_all(v, n):
            return bass.AP(v.tensor, v.offset, [[0, P], [1, n]])

        loads = [
            (nat[0].rearrange("p (t d) -> p t d", t=FT), w_up.rearrange("(t p) d -> p t d", p=P)),
            (nat[1].rearrange("p (t f) -> p t f", t=KT), w_down.rearrange("(t p) f -> p t f", p=P)),
            (wqk[:, :, :], qkv_w[:, 0:2 * D].rearrange("(t p) n -> p t n", p=P)),
            (wrq[:, :, :], rq_w.rearrange("(t p) n -> p t n", p=P)),
            (wrkv[:, :, :], rkv_w.rearrange("(t p) n -> p t n", p=P)),
            (wout[:, :, :], out_w.rearrange("(t p) n -> p t n", p=P)),
            (wro[LD:2 * LD, 0:D], rout_w),
            (bqk[:, :], qkv_b[0:2 * D].rearrange("(t p) -> p t", p=P)),
            (brq[:, :], rq_b.rearrange("(p a) -> p a", a=1)),
            (brkv[:, :], rkv_b.rearrange("(p a) -> p a", a=1)),
            (bv[:, :, 0:HD], bass.AP(qkv_b.tensor, qkv_b.offset + 2 * D, [[0, P], [HD, H], [1, HD]])),
            (brem[:, 0:D], rows_of_all(rout_b, D)),
            (bout[:, :], rows_of_all(out_b, D)),
            (glb[:, :], rows_of_all(gl_w, HD)),
            (grb[:, :], rows_of_all(gr_w, HD)),
        ] + [(wv[:, t, :, 0:HD], qkv_w[t * P:(t + 1) * P, 2 * D:3 * D].rearrange("p (h d) -> p h d", h=H))
             for t in range(KT)]
        ff_loads, loads = loads[:2], loads[2:]
        W_ALL, W_FF = 16 * len(loads), 16 * len(ff_loads)

        def wait_alone(eng, semaphore, value):
            eng.wait_ge(semaphore, value)
            eng.sem_inc(passed, 1)

        @block.sync
        def _(sp):
            xs = x.rearrange("s (b p) d -> s p b d", p=P)
            outs = out.rearrange("s (b p) d -> s p b d", p=P)

            def of_seq(t, i):
                return t[i] if isinstance(i, int) else t[bass.ds(i, 1)].squeeze(0)

            def load_x(s):
                if not s.first:
                    for t in range(KT):
                        bank, k = p_use(s.before(), t)
                        wait_alone(sp, p_full[bank], k + 1)
                sp.dma_start(xtok[:, :, :], of_seq(xs, s.i)).then_inc(x_in, 16)

            def load_xres(s):
                if not s.first:
                    for t in range(2):
                        slot, k = work_use(s.before(), "F", 2 + t)
                        wait_alone(sp, w_taken[slot], k + 1)
                sp.dma_start(xres[:, :, :], of_seq(xs, s.i)).then_inc(xres_in, 16)

            def restack(s):
                if not s.first:
                    wait_alone(sp, stacks_in[1 - s.par], (s.half + s.par) * (16 * 2 * len(QPART)))
                for j in range(3):
                    wait_alone(sp, (part0, part1, part2)[j], count(s, 4, 3))
                    sp.dma_start(parts_dram[j].rearrange("(t p) n -> p t n", p=P), parts[:, j, :, :]
                                 ).then_inc(parts_out, 16)
                if s.known and s.i < 2:
                    wait_alone(sp, q_consts, s.i + 1)
                else:
                    wait_alone(sp, pv_done, count(s, NU, -NU - 1))
                wait_alone(sp, parts_out, count(s, 1, 0) * 48)
                for r in range(len(QPART)):
                    rows = slice(HD * r, HD * r + HD)
                    sp.dma_start(Qs[s.par][rows, :, :],
                                 parts_dram[QPART[r], 0:D].rearrange("(h d) n -> d h n", d=HD)
                                 ).then_inc(stacks_in[s.par], 16)
                    sp.dma_start(Ks[s.par][rows, :, P:P + S],
                                 parts_dram[KPART[r], D:2 * D].rearrange("(h d) n -> d h n", d=HD)
                                 ).then_inc(stacks_in[s.par], 16)

            def move_max(s):
                for t in range(2):
                    slot, k = work_use(s, "T", t)
                    wait_alone(sp, w_taken[slot], k + 1)
                if not s.first:
                    wait_alone(sp, nmax_in[1 - s.par], (s.half + s.par) * 16)
                sp.dma_start(nmax_dram.rearrange("j h n -> h j n"), nmaxT[:, :, :]).then_inc(nmax_out, 16)
                wait_alone(sp, nmax_out, count(s, 1, 0) * 16)
                sp.dma_start(Qs[s.par][MAXR:MAXR + 2, :, :], nmax_dram).then_inc(nmax_in[s.par], 16)

            def store_before(s):
                wait_alone(sp, y_ready, count(s, NB, -1))
                sp.dma_start(of_seq(outs, s.i - 1), ytok[:, :, :]).then_inc(y_out, 16)

            def body(s):
                later = s.second_next()
                if later.exists:
                    load_x(later)
                load_xres(s)
                if not s.first:
                    store_before(s)
                if not s.last:
                    move_max(s.next())
                if later.exists:
                    restack(later)

            with nc.allow_non_contiguous_dma(reason="bias columns, a few hundred elements"):
                load_x(Seq(0, 0, 0))
                for dst, src in loads:
                    sp.dma_start(dst, src).then_inc(w_in, 16)
                for dst, src in ff_loads:
                    sp.dma_start(dst, src).then_inc(ff_in, 16)
            load_x(Seq(1, 1, 0))
            restack(Seq(0, 0, 0))
            restack(Seq(1, 1, 0))
            move_max(Seq(0, 0, 0))
            over_sequences(sp, body)
            store_before(Seq(B, 0, B // 2))
            sp.wait_ge(y_out, 16 * B)

        @block.gpsimd
        def _(pool):
            links = [0]

            def link(ins):
                links[0] += 1
                ins.then_inc(pool_chain, 1)
                pool.wait_ge(pool_chain, links[0])

            link(pool.memset(ident[:, :], 0.0))
            link(pool.affine_select(out=ident[:, :], in_=ident[:, :], compare_op=ALU.not_equal, fill=1.0,
                                    base=0, pattern=[[-1, P]], channel_multiplier=1))
            link(pool.tensor_copy(identb[:, :], ident[:, :]))
            pool.sem_inc(consts, 1)
            link(pool.memset(ones_col[:, :], 1.0))
            link(pool.memset(power[:, 0, :], -0.5))
            link(pool.memset(power[:, 1, :], 0.5))
            link(pool.memset(mask_edge[:, :, :], 0.0))
            link(pool.memset(mask_first[:, :], 0.0))
            link(pool.memset(lat_mask[:, :, :], 0.0))
            link(pool.memset(diag_mask[:, :, :], 1.0))
            link(pool.memset(dead[:, :, :], 0.0))
            link(pool.memset(live[:, :, :], 1.0))
            link(pool.memset(wv[:, :, :, HD:VW], 0.0))
            link(pool.memset(bv[:, :, HD:VW], 1.0))
            for g in range(P // GQ):
                rows = slice(g * GQ, (g + 1) * GQ)
                link(pool.affine_select(out=mask_edge[rows, 0, :], in_=mask_edge[rows, 0, :],
                                        compare_op=ALU.is_ge, fill=NEG, base=0,
                                        pattern=[[1, GQ]], channel_multiplier=-1))
                link(pool.affine_select(out=mask_edge[rows, 1, :], in_=mask_edge[rows, 1, :],
                                        compare_op=ALU.is_gt, fill=NEG, base=0,
                                        pattern=[[-1, GQ]], channel_multiplier=1))
                link(pool.affine_select(out=mask_first[rows, :], in_=mask_first[rows, :],
                                        compare_op=ALU.is_gt, fill=NEG, base=P,
                                        pattern=[[-1, BAND]], channel_multiplier=1))
                link(pool.affine_select(out=mask_first[rows, :], in_=mask_first[rows, :],
                                        compare_op=ALU.is_ge, fill=NEG, base=g * GQ - P,
                                        pattern=[[1, BAND]], channel_multiplier=0))
            link(pool.memset(mask_first[0:1, 1:2], 0.0))
            link(pool.affine_select(out=lat_mask[:, :, :], in_=lat_mask[:, :, :], compare_op=ALU.is_ge,
                                    fill=NEG, base=-CHUNK, pattern=[[P, NB], [-CHUNK, LAT]],
                                    channel_multiplier=1))
            for half in range(2):
                rows = slice(half * LD, half * LD + LD)
                link(pool.affine_select(out=diag_mask[rows, :, :], in_=diag_mask[rows, :, :],
                                        compare_op=ALU.is_ge, fill=0.0, base=0,
                                        pattern=[[-LHD, LH], [0, LAT]], channel_multiplier=1))
                link(pool.affine_select(out=diag_mask[rows, :, :], in_=diag_mask[rows, :, :],
                                        compare_op=ALU.is_ge, fill=0.0, base=LHD - 1,
                                        pattern=[[LHD, LH], [0, LAT]], channel_multiplier=-1))
            link(pool.memset(dead[0:1, 0, :], 1.0))
            pool.memset(live[0:CHUNK, 0, :], 0.0).then_inc(consts, 1)

            def exclude_k(k):
                link(pool.memset(in_pairs(Ks[k])[EXC:EXC + 1], 0.0))
                link(pool.memset(Ks[k][EXC:EXC + 1, :, :].rearrange("p h (b c) -> p h b c", c=P)[:, :, :, 0:1],
                                 NEG))

            def exclude_q(k):
                link(pool.memset(Qs[k][EXC:EXC + 1, :, :].rearrange("p h (b c) -> p h b c", c=P)[:, :, :, 0:1],
                                 1.0))

            pool.wait_ge(ones_set, 1)
            exclude_k(0)
            exclude_q(0)
            pool.sem_inc(q_consts, 1)

            def p_step(s, k):
                if QK <= k < QK + 4:
                    t = k - QK
                    pool.wait_ge(part1, count(s, 4, t))
                    if t == 0 and not s.first:
                        pool.wait_ge(parts_out, count(s, 1, -1) * 48)
                    pool.tensor_tensor(parts[:, 2, t, :], qk_rest[:, t % 2, :], parts[:, 1, t, :],
                                       ALU.subtract).then_inc(part2, 1)

            def mask(s, u):
                pt = Pt[:, u % NPT, :, :]
                slot, k = score_use(s, u)
                wait_alone(pool, s_taken[slot], k + 1)
                ins = pool.affine_select(out=pt[:, :, 0:P], in_=pt[:, :, 0:P], compare_op=ALU.is_gt,
                                         fill=0.0, base=0, pattern=[[0, 4], [1, P]], channel_multiplier=-1)
                if u % NB < NB - 1:
                    ins = pool.affine_select(out=pt[:, :, P:2 * P], in_=pt[:, :, P:2 * P],
                                             compare_op=ALU.is_ge, fill=0.0, base=0,
                                             pattern=[[0, 4], [-1, P]], channel_multiplier=1)
                ins.then_inc(masked, 1)

            def f_step(s, k):
                if k == GATE:
                    pool.wait_ge(gate_g, count(s, 1, 0))
                    for b in range(NB):
                        rv = rem[:, s.par, b, 0:D].rearrange("p (h d) -> p h d", h=H)
                        pool.tensor_tensor(rv, rv, gate[:, 2, b, :].unsqueeze(2).to_broadcast([P, H, HD]),
                                           ALU.mult).then_inc(rem_part, 1)
                if k == OUT:
                    pool.wait_ge(var_ready, count(s, 1, 0))
                    pool.tensor_tensor(rs[:, 0:2, :], rs[:, 3:5, :], power[:, :, :], ALU.pow
                                       ).then_inc(rstd_ready, 1)
                if UP <= k < END:
                    t = k - UP
                    pool.wait_ge(h_hi_ready, count(s, FT, t))
                    if t >= NR:
                        pool.wait_ge(down_done, count(s, FT, t - NR))
                    pool.tensor_tensor(h_lo[:, t % NR, :], hbuf[:, t % 2, :], h_hi[:, t % NR, :],
                                       ALU.subtract).then_inc(h_lo_ready, 1)
                if k == END:
                    pool.wait_ge(ssq_mean, count(s, 1, 0))
                    pool.tensor_tensor(rs[:, 2, :], rs[:, 3, :], power[:, 1, :], ALU.pow).then_inc(hroot, 1)

            def w_step(j):
                if j == 0:
                    pool.wait_ge(alpha_part, 1)
                    pool.partition_all_reduce(alpha[:, 4:6], alpha[:, 2:4], P, RADD).then_inc(alpha_all, 1)
                    pool.wait_ge(alpha_all, 1)
                if j == 1:
                    pool.wait_ge(ones_set, 2)
                    exclude_k(1)
                    pool.wait_ge(tern, 2)
                    link(pool.memset(Vp[:, :, :, H * VW:], 0.0))
                    link(pool.memset(in_pairs(Qs[1])[ROWS:P], 0.0))
                    exclude_q(1)
                    pool.sem_inc(q_consts, 1)

            def add_bias(s, b):
                if b == 0:
                    pool.wait_ge(xres_in, count(s, 1, 0) * 16)
                pool.tensor_tensor(xres[:, b, :], xres[:, b, :], bout[:, :], ALU.add).then_inc(xres_done, 1)

            def finish_before(s):
                pool.wait_ge(var2_ready, count(s, 1, -1))
                pool.tensor_tensor(rs[:, 0, :], rs[:, 3, :], power[:, 0, :], ALU.pow).then_inc(rstd2_ready, 1)

            def body(s):
                for u in range(NU):
                    mask(s, u)
                    if u == STAT_AT + NB and not s.first:
                        finish_before(s)
                    if u % NB == NB - 1:
                        add_bias(s, u // NB)
                later = s.second_next()
                for phase, k in SECOND_HALF:
                    if phase == "F":
                        f_step(s, k)
                    elif later.exists:
                        p_step(later, k)

            for phase, k in PROLOGUE:
                if phase == "W":
                    w_step(k)
                elif phase in ("P0", "P1"):
                    p_step(START[phase], k)
            over_sequences(pool, body)
            finish_before(Seq(B, 0, B // 2))

        @block.scalar
        def _(act):
            def p_step(s, k):
                if k == X_T:
                    for t in range(KT):
                        bank, n = p_use(s, t)
                        act.wait_ge(p_full[bank], n + 1)
                        if not s.first:
                            for b in range(NB):
                                last, m = p_use(s.before(), 10 + b)
                                act.wait_ge(p_full[last], m + 1)
                        nc.scalar.activation(xT[:, t, :], p_bank(bank), ACT.Copy).then_inc(p_taken[bank], 1)
                if QK <= k < QK + 4:
                    t = k - QK
                    bank, n = p_use(s, 2 + t)
                    act.wait_ge(p_full[bank], n + 1)
                    if t == 0 and not s.first:
                        act.wait_ge(parts_out, count(s, 1, -1) * 48)
                    nc.scalar.activation(parts[:, 0, t, :], p_bank(bank), ACT.Identity,
                                         bias=bqk[:, t:t + 1]).then_inc(part0, 1)
                if QK < k <= QK + 4:
                    t = k - QK - 1
                    bank, n = p_use(s, 2 + t)
                    act.wait_ge(p_taken[bank], n + 1)
                    nc.scalar.activation(parts[:, 1, t, :], qk_rest[:, t % 2, :], ACT.Copy).then_inc(part1, 1)
                if LAT_SCORES <= k < LAT_SCORES + 2:
                    b2 = k - LAT_SCORES
                    bank, n = p_use(s, 8 + b2)
                    act.wait_ge(p_taken[bank], n + 1)
                    lp = lat_p[:, 2 * b2:2 * b2 + 2, :, :].rearrange("p b h l -> p (b h l)")
                    nc.scalar.activation(lp, lp, ACT.Exp, scale=LSCALE).then_inc(lat_exp, 1)
                if k == LAT_V:
                    for t in range(2):
                        bank, n = p_use(s, 14 + t)
                        act.wait_ge(p_full[bank], n + 1)
                        nc.scalar.activation(rvr[:, t, :], p_bank(bank)[:, 0:RW], ACT.Copy
                                             ).then_inc(p_taken[bank], 1)
                if LAT_T <= k < LAT_T + 2:
                    t = k - LAT_T
                    bank, n = p_use(s, 16 + t)
                    act.wait_ge(p_full[bank], n + 1)
                    nc.scalar.activation(lat_pT[:, 2 * t:2 * t + 2, :, :].rearrange("p b t n -> p (b t n)"),
                                         p_bank(bank), ACT.Copy).then_inc(p_taken[bank], 1)

            def max_high(s, t):
                slot, k = work_use(s, "T", t)
                act.wait_ge(w_full[slot], k + 1)
                if t == 0 and not s.first:
                    act.wait_ge(nmax_out, count(s, 1, -1) * 16)
                nc.scalar.activation(nmaxT[:, 0, 2 * P * t:2 * P * (t + 1)], work[0:H, slot, 0:2 * P],
                                     ACT.Copy).then_inc(nmax_hi, 1)

            def copy_o(s, hg):
                act.wait_ge(pv_done, count(s, NU, NB * hg + NB - 1))
                if hg > 0:
                    slot, k = work_use(s, "O", hg - 1)
                    act.wait_ge(w_full[slot], k + 1)
                nc.scalar.activation(oT[:, :], oacc[:, hg % 2, :], ACT.Copy).then_inc(oT_ready, 1)

            def weights(s, u):
                slot, k = score_use(s, u)
                act.wait_ge(s_full[slot], k + 1)
                if u >= NPT:
                    act.wait_ge(pv_done, count(s, NU, u - NPT))
                if u == 1 and not s.last:
                    act.wait_ge(part2, count(s.next(), 4, 3))
                w = 2 * P if u % NB < NB - 1 else P
                nc.scalar.activation(
                    Pt[:, u % NPT, :, 0:w],
                    scores[:, slot, :, :].rearrange("p k (h q) -> p (k h) q", h=2)[:, :, 0:w],
                    ACT.Exp, scale=SCALE).then_inc(s_taken[slot], 1)

            def f_step(s, k):
                if k == GATE:
                    act.wait_ge(gate_z, count(s, 1, 0))
                    nc.scalar.activation(gate[:, 1, :, :], gate[:, 0, :, :], ACT.Exp, scale=-1.0
                                         ).then_inc(gate_e, 1)
                if k == MIX_T:
                    for t in range(KT):
                        slot, n = work_use(s, "F", t)
                        act.wait_ge(w_full[slot], n + 1)
                        nc.scalar.activation(mixT[:, t, :], work[:, slot, :], ACT.Copy
                                             ).then_inc(w_taken[slot], 1)
                if k == NORM:
                    for b in range(NB):
                        act.wait_ge(x1_ready, count(s, NB, b))
                        nc.scalar.activation(xn[:, b, :], x1[:, b, :], ACT.Copy, scale=rs[:, 2, b:b + 1]
                                             ).then_inc(xn_ready, 1)
                if k == XN_T:
                    for t in range(KT):
                        slot, n = work_use(s, "F", 4 + t)
                        act.wait_ge(w_full[slot], n + 1)
                        nc.scalar.activation(xnT[:, 0, t, :], work[:, slot, :], ACT.Copy).then_inc(xn_hi, 1)
                if UP <= k < END:
                    t = k - UP
                    slot, n = work_use(s, "F", 6 + t)
                    act.wait_ge(w_full[slot], n + 1)
                    if t >= 2:
                        act.wait_ge(h_lo_ready, count(s, FT, t - 2))
                        act.wait_ge(h_sq, count(s, FT, t - 2))
                    nc.scalar.activation(hbuf[:, t % 2, :], work[:, slot, :], ACT.Gelu
                                         ).then_inc(w_taken[slot], 1)
                    act.wait_ge(w_taken[slot], n + 1)
                    if t >= 3:
                        act.wait_ge(h_added, count(s, FT - 1, t - 3))
                    nc.scalar.activation(h_sum[:, :] if t == 0 else hsq[:, t % 2, :], hbuf[:, t % 2, :],
                                         ACT.Square).then_inc(h_sq, 1)

            def body(s):
                for u in range(FIRST_HALF):
                    if u < NU:
                        weights(s, u)
                    if u >= 6 and (u - 6) % NB == 0 and (u - 6) // NB < HG - 1:
                        copy_o(s, (u - 6) // NB)
                    if not s.last:
                        for t in range(2):
                            if u == (9, NM // 2)[t]:
                                max_high(s.next(), t)
                copy_o(s, HG - 1)
                later = s.second_next()
                for phase, k in SECOND_HALF:
                    if phase == "F":
                        f_step(s, k)
                    elif later.exists:
                        p_step(later, k)

            act.wait_ge(w_in, W_ALL)
            for phase, k in PROLOGUE:
                if phase == "T":
                    max_high(Seq(0, 0, 0), k)
                elif phase in ("P0", "P1"):
                    p_step(START[phase], k)
            over_sequences(act, body)

        @block.vector
        def _(dve):
            links = [0]

            def link(ins):
                links[0] += 1
                ins.then_inc(vec_chain, 1)
                dve.wait_ge(vec_chain, links[0])

            nc.vector.memset(in_pairs(Qs[0])[ROWS:P], 0.0)
            for k in range(2):
                nc.vector.memset(in_pairs(Ks[k])[0:ROWS, :, 0:P // 2], 0.0)
                nc.vector.memset(in_pairs(Ks[k])[ROWS:P], ONE_PAIR).then_inc(ones_set, 1)
            dve.wait_ge(w_in, W_ALL)
            dve.wait_ge(consts, 2)
            tmp = ytok[:, 0, :].rearrange("p (h d) -> p h d", h=H)
            gl3 = glb[:, :].unsqueeze(1).to_broadcast([P, H, HD])
            gr3 = grb[:, :].unsqueeze(1).to_broadcast([P, H, HD])
            rem3 = brem[:, 0:D].rearrange("p (h d) -> p h d", h=H)
            wro3 = wro[LD:2 * LD, 0:D].rearrange("p (h d) -> p h d", h=H)
            for w3, o in [(wv[:, t, :, 0:HD], wv[:, t, :, HD + 1:VW]) for t in range(KT)] + \
                         [(bv[:, :, 0:HD], bv[:, :, HD + 1:VW])]:
                link(nc.vector.tensor_tensor(tmp, w3, gl3, ALU.mult))
                link(nc.vector.tensor_reduce(o, tmp, X, ALU.add))
            link(nc.vector.tensor_tensor(tmp, rem3, gr3, ALU.mult))
            link(nc.vector.tensor_reduce(brem[:, D:RW], tmp, X, ALU.add))
            link(nc.vector.tensor_tensor(tmp[LD:2 * LD], wro3, gr3[LD:2 * LD], ALU.mult))
            nc.vector.tensor_reduce(wro[LD:2 * LD, D:RW], tmp[LD:2 * LD], X, ALU.add).then_inc(prep_done, 1)

            def w_step(j):
                if j == 0:
                    dve.wait_ge(ff_in, W_FF)
                    sums = gate[:, 0:2, :, :].rearrange("p k b h -> p k (b h)")
                    for k in range(2):
                        link(nc.vector.tensor_reduce(sums[:, k, :],
                                                     nat[k].rearrange("p (a n) -> p a n", a=NB * H), X,
                                                     ALU.add, apply_absolute_value=True))
                    nc.vector.tensor_reduce(alpha[:, 2:4], sums, X, ALU.add).then_inc(alpha_part, 1)
                if j == 1:
                    dve.wait_ge(alpha_all, 1)
                    nc.vector.tensor_scalar(alpha[:, 0:2], alpha[:, 4:6], 0.5 / (F * D), None, ALU.mult)
                    link(nc.vector.tensor_scalar(alpha[:, 6:8], alpha[:, 4:6], -0.5 / (F * D), None, ALU.mult))
                    for k in range(2):
                        link(nc.vector.tensor_scalar(below, nat[k], alpha[:, 6 + k:7 + k], None, ALU.is_lt))
                        nc.vector.scalar_tensor_tensor(out=ternary[k], in0=nat[k], scalar=alpha[:, k:k + 1],
                                                       in1=below, op0=ALU.is_gt, op1=ALU.subtract
                                                       ).then_inc(tern, 1)
                        dve.wait_ge(tern, k + 1)
                if j >= 2:
                    dve.wait_ge(tern_T, j - 1)
                    for a in range(2):
                        for b in range(2):
                            if j == 2:
                                ins = nc.vector.tensor_copy(wup_t[:, a, 512 * b:512 * b + 512],
                                                            (work, oacc)[a][:, b, :])
                            else:
                                ins = nc.vector.tensor_copy(
                                    wdn_t[:, 4 * b:4 * b + 4, a * P:(a + 1) * P],
                                    (work, oacc)[a][:, b, :].rearrange("p (t n) -> p t n", n=P))
                    ins.then_inc(wt_done, 1)

            p_links = [0]
            f_links = [0]

            def p_mark(ins):
                p_links[0] += 1
                ins.then_inc(p_vec, 1)

            def p_done(s, ins):
                p_mark(ins)
                dve.wait_ge(p_vec, count(s, NP_VEC, p_links[0] - 1))

            def p_step(s, k):
                def take(u):
                    bank, n = p_use(s, u)
                    dve.wait_ge(p_full[bank], n + 1)
                    return bank, n

                if k == X_T:
                    p_links[0] = 0
                if k == QK:
                    for t in range(KT):
                        bank, n = p_use(s, t)
                        dve.wait_ge(p_taken[bank], n + 1)
                    p_done(s, nc.vector.tensor_reduce(pooled[:, :, :].rearrange("p t l -> p (t l)"),
                                                      xT[:, :, :].rearrange("p t n -> p (t n)").rearrange(
                                                          "p (l c) -> p l c", c=CHUNK), X, ALU.add))
                if QK <= k < QK + 4:
                    t = k - QK
                    bank, n = take(2 + t)
                    dve.wait_ge(part0, count(s, 4, t))
                    if t >= 2:
                        dve.wait_ge(part2, count(s, 4, t - 2))
                    nc.vector.scalar_tensor_tensor(out=qk_rest[:, t % 2, :], in0=p_bank(bank),
                                                   scalar=bqk[:, t:t + 1], in1=parts[:, 0, t, :],
                                                   op0=ALU.add, op1=ALU.subtract).then_inc(p_taken[bank], 1)
                if k == LAT_IN:
                    bank, n = take(6)
                    nc.vector.tensor_scalar(rqT[:, :], p_bank(bank)[0:LD, :], brq[:, :], None, ALU.add
                                            ).then_inc(p_taken[bank], 1)
                    bank, n = take(7)
                    nc.vector.tensor_scalar(rkv_sb[:, :], p_bank(bank)[:, 0:LAT], 1.0 / CHUNK, brkv[:, :],
                                            ALU.mult, ALU.add).then_inc(p_taken[bank], 1)
                    dve.wait_ge(p_taken[bank], n + 1)
                    nc.vector.tensor_tensor(lat_bd[:, :, :],
                                            rkv_sb[:, :].unsqueeze(1).to_broadcast([P, LH, LAT]),
                                            diag_mask[:, :, :], ALU.mult).then_inc(bd_ready, 1)
                if LAT_SCORES <= k < LAT_SCORES + 2:
                    b2 = k - LAT_SCORES
                    bank, n = take(8 + b2)
                    blocks = slice(2 * b2, 2 * b2 + 2)
                    p_done(s, nc.vector.tensor_reduce(lat_st[:, 0, blocks, :].rearrange("p b h -> p (b h)"),
                                                      p_bank(bank).rearrange("p (g l) -> p g l", l=LAT),
                                                      X, ALU.max, negate=True))
                    nc.vector.tensor_tensor(
                        lat_p[:, blocks, :, :].rearrange("p b h l -> p (b h) l"),
                        p_bank(bank).rearrange("p (g l) -> p g l", l=LAT),
                        lat_st[:, 0, blocks, :].rearrange("p b h -> p (b h)").unsqueeze(2).to_broadcast(
                            [P, 2 * LH, LAT]), ALU.add).then_inc(p_taken[bank], 1)
                if VALUES <= k < VALUES + NB:
                    b = k - VALUES
                    bank, n = take(10 + b)
                    nc.vector.tensor_tensor(Vp[:, s.par, b, 0:H * VW], p_bank(bank)[:, 0:H * VW],
                                            bv[:, :, :].rearrange("p h d -> p (h d)"), ALU.add
                                            ).then_inc(p_taken[bank], 1)
                if k == LAT_V:
                    dve.wait_ge(lat_exp, count(s, 2, 1))
                    flat = lat_p[:, :, :, :].rearrange("p b h l -> p (b h) l")
                    st = [lat_st[:, j, :, :].rearrange("p b h -> p (b h)") for j in range(3)]
                    p_done(s, nc.vector.tensor_reduce(st[1], flat, X, ALU.add))
                    p_done(s, nc.vector.reciprocal(st[2], st[1]))
                    p_done(s, nc.vector.tensor_tensor(st[1], st[2], live[:, :, :].rearrange("p b h -> p (b h)"),
                                                      ALU.mult))
                    nc.vector.tensor_tensor(flat, flat, st[1].unsqueeze(2).to_broadcast([P, NB * LH, LAT]),
                                            ALU.mult).then_inc(lat_norm, 1)
                    assert p_links[0] == NP_VEC
                if REMOTE <= k < REMOTE + NB:
                    b = k - REMOTE
                    bank, n = take(18 + b)
                    nc.vector.tensor_tensor(rem[:, s.par, b, :], p_bank(bank)[:, 0:RW], brem[:, :], ALU.add
                                            ).then_inc(p_taken[bank], 1)

            def maxima(s, v):
                slot, k = work_use(s, "A", v)
                dve.wait_ge(w_full[slot], k + 1)
                b, pair = v // (H // 2), v % (H // 2)
                nc.vector.tensor_reduce(nmax[:, b, 2 * pair:2 * pair + 2],
                                        work[:, slot, 0:2 * BAND].rearrange("p (h c) -> p h c", h=2),
                                        X, ALU.max, negate=True).then_inc(w_taken[slot], 1)

            def max_low(s, t):
                slot, k = work_use(s, "T", t)
                dve.wait_ge(nmax_hi, count(s, 2, t))
                cols = slice(2 * P * t, 2 * P * (t + 1))
                nc.vector.tensor_tensor(nmaxT[:, 1, cols], work[0:H, slot, 0:2 * P], nmaxT[:, 0, cols],
                                        ALU.subtract).then_inc(w_taken[slot], 1)

            def take_o(s, hg):
                slot, k = work_use(s, "O", hg)
                dve.wait_ge(w_full[slot], k + 1)
                nc.vector.tensor_copy(
                    o_tok[:, :, 4 * hg:4 * hg + 4, :],
                    work[:, slot, :].rearrange("p (b h d) -> p b h d", b=NB, h=4)[:, :, :, 0:VW]
                ).then_inc(w_taken[slot], 1)

            def f_step(s, k):
                def mark(ins):
                    f_links[0] += 1
                    ins.then_inc(f_vec, 1)

                def sync():
                    dve.wait_ge(f_vec, count(s, NF_VEC, f_links[0] - 1))

                def done(ins):
                    mark(ins)
                    sync()

                def take(u):
                    slot, n = work_use(s, "F", u)
                    dve.wait_ge(w_full[slot], n + 1)
                    return slot, n

                if k == GATE:
                    f_links[0] = 0
                    take_o(s, HG - 1)
                    for hg in range(2, 4):
                        slot, n = work_use(s, "O", hg)
                        dve.wait_ge(w_taken[slot], n + 1)
                    z, e, ng, r, a = (gate[:, j, :, :] for j in range(5))
                    done(nc.vector.tensor_tensor(e, o_tok[:, :, :, HD], dead[:, :, :], ALU.add))
                    done(nc.vector.reciprocal(r, e))
                    done(nc.vector.tensor_tensor(a, o_tok[:, :, :, HD + 1], r, ALU.mult))
                    nc.vector.tensor_tensor(z, a, rem[:, s.par, :, D:RW], ALU.add).then_inc(gate_z, 1)
                    dve.wait_ge(gate_e, count(s, 1, 0))
                    done(nc.vector.tensor_scalar(z, e, 1.0, None, ALU.add))
                    done(nc.vector.reciprocal(e, z))
                    mark(nc.vector.tensor_tensor(a, e, r, ALU.mult))
                    nc.vector.tensor_scalar(ng, e, -1.0, 1.0, ALU.mult, ALU.add).then_inc(gate_g, 1)
                    sync()
                    for b in range(NB):
                        ins = nc.vector.tensor_tensor(mixed[:, b, :].rearrange("p (h d) -> p h d", h=H),
                                                      o_tok[:, b, :, 0:HD],
                                                      a[:, b, :].unsqueeze(2).to_broadcast([P, H, HD]), ALU.mult)
                    mark(ins)
                if k == MIX:
                    sync()
                    for b in range(NB):
                        dve.wait_ge(rem_part, count(s, NB, b))
                        nc.vector.tensor_tensor(mixed[:, b, :], mixed[:, b, :], rem[:, s.par, b, 0:D], ALU.add
                                                ).then_inc(mixed_ready, 1)
                if k == OUT:
                    dve.wait_ge(xres_done, count(s, NB, NB - 1))
                    if not s.first:
                        dve.wait_ge(y_out, count(s, 1, -1) * 16)
                    for t in range(2):
                        slot, n = take(2 + t)
                        blocks = slice(2 * t, 2 * t + 2)
                        nc.vector.tensor_tensor(ytok[:, blocks, :].rearrange("p b d -> p (b d)"),
                                                work[:, slot, :],
                                                xres[:, blocks, :].rearrange("p b d -> p (b d)"), ALU.add
                                                ).then_inc(w_taken[slot], 1)
                        dve.wait_ge(w_taken[slot], n + 1)
                        for b in range(2 * t, 2 * t + 2):
                            last_stats = nc.vector.bn_stats(stats[:, b, :], ytok[:, b, :])
                    mark(last_stats)
                    wait_alone(dve, f_vec, count(s, NF_VEC, f_links[0] - 1))
                    for b in range(NB):
                        ins = nc.vector.bn_aggr(mv[:, b, :], stats[:, b, :])
                    done(ins)
                    nc.vector.tensor_copy(rs[:, 4, :], mv[:, :, 1])
                    nc.vector.tensor_scalar(rs[:, 3, :], mv[:, :, 1], EPS, None, ALU.add).then_inc(var_ready, 1)
                if k == NORM:
                    dve.wait_ge(rstd_ready, count(s, 1, 0))
                    done(nc.vector.tensor_tensor(rs[:, 2, :], rs[:, 0, :], rs[:, 1, :], ALU.mult))
                    done(nc.vector.tensor_scalar(rs[:, 3, :], rs[:, 2, :], 1e-8, None, ALU.add))
                    done(nc.vector.reciprocal(rs[:, 2, :], rs[:, 3, :]))
                    for b in range(NB):
                        nc.vector.tensor_scalar(x1[:, b, :], ytok[:, b, :], mv[:, b, 0:1], rs[:, 0, b:b + 1],
                                                ALU.subtract, ALU.mult).then_inc(x1_ready, 1)
                if k == XN_T:
                    for t in range(KT):
                        slot, n = take(4 + t)
                        dve.wait_ge(xn_hi, count(s, KT, t))
                        nc.vector.tensor_tensor(xnT[:, 1, t, :], work[:, slot, :], xnT[:, 0, t, :], ALU.subtract
                                                ).then_inc(w_taken[slot], 1)
                if UP <= k < END:
                    t = k - UP
                    slot, n = work_use(s, "F", 6 + t)
                    dve.wait_ge(w_taken[slot], n + 1)
                    if t >= NR:
                        dve.wait_ge(down_done, count(s, FT, t - NR))
                    nc.vector.tensor_copy(h_hi[:, t % NR, :], hbuf[:, t % 2, :]).then_inc(h_hi_ready, 1)
                    if t > 0:
                        dve.wait_ge(h_sq, count(s, FT, t))
                        if t > 1:
                            dve.wait_ge(h_added, count(s, FT - 1, t - 2))
                        nc.vector.tensor_tensor(h_sum[:, :], h_sum[:, :], hsq[:, t % 2, :], ALU.add
                                                ).then_inc(h_added, 1)
                if k == END:
                    slot, n = take(14)
                    nc.vector.tensor_scalar(rs[:, 3, :], work[:, slot, 0:NB], 1.0 / F, None, ALU.mult
                                            ).then_inc(w_taken[slot], 1)
                    dve.wait_ge(w_taken[slot], n + 1)
                    dve.sem_inc(ssq_mean, 1)
                    dve.wait_ge(hroot, count(s, 1, 0))
                    done(nc.vector.tensor_scalar(rs[:, 3, :], rs[:, 2, :], 1e-8, None, ALU.add))
                    done(nc.vector.reciprocal(rs[:, 2, :], rs[:, 3, :]))
                    dve.wait_ge(down_done, count(s, FT, FT - 1))
                    for b in range(NB):
                        ins = nc.vector.scalar_tensor_tensor(
                            out=ytok[:, b, :], in0=oacc[:, b // 2, (b % 2) * D:(b % 2 + 1) * D],
                            scalar=rs[:, 2, b:b + 1], in1=x1[:, b, :], op0=ALU.mult, op1=ALU.add)
                    ins.then_inc(y2_ready, 1)
                    assert f_links[0] == NF_VEC, f_links

            def finish_before(s, u):
                if u == 0:
                    dve.wait_ge(y2_ready, count(s, 1, -1))
                if u < NB:
                    nc.vector.bn_stats(stats[:, u, :], ytok[:, u, :]).then_inc(y2_vec, 1)
                if u == NB:
                    wait_alone(dve, y2_vec, count(s, NB + 1, -2))
                    for b in range(NB):
                        ins = nc.vector.bn_aggr(mv[:, b, :], stats[:, b, :])
                    ins.then_inc(y2_vec, 1)
                    dve.wait_ge(y2_vec, count(s, NB + 1, -1))
                    nc.vector.tensor_scalar(rs[:, 3, :], mv[:, :, 1], EPS, None, ALU.add).then_inc(var2_ready, 1)
                if NB + 2 <= u < 2 * NB + 2:
                    b = u - NB - 2
                    if b == 0:
                        dve.wait_ge(rstd2_ready, count(s, 1, -1))
                    nc.vector.tensor_scalar(ytok[:, b, :], ytok[:, b, :], mv[:, b, 0:1], rs[:, 0, b:b + 1],
                                            ALU.subtract, ALU.mult).then_inc(y_ready, 1)

            def body(s):
                for u in range(FIRST_HALF):
                    if u >= STAT_AT and not s.first:
                        finish_before(s, u - STAT_AT)
                    for v in (2 * u, 2 * u + 1):
                        if v < NM and not s.last:
                            maxima(s.next(), v)
                    if u >= 7 and (u - 7) % NB == 0 and (u - 7) // NB < HG - 1:
                        take_o(s, (u - 7) // NB)
                    if not s.last:
                        for t in range(2):
                            if u == (9, NM // 2)[t]:
                                max_low(s.next(), t)
                later = s.second_next()
                for phase, k in SECOND_HALF:
                    if phase == "F":
                        f_step(s, k)
                    elif later.exists:
                        p_step(later, k)

            for phase, k in PROLOGUE:
                if phase == "W":
                    w_step(k)
                elif phase in ("P0", "P1"):
                    p_step(START[phase], k)
                else:
                    (maxima if phase == "A" else max_low)(Seq(0, 0, 0), k)
            over_sequences(dve, body)
            for u in range(2 * NB + 2):
                finish_before(Seq(B, 0, B // 2), u)

        @block.tensor
        def _(pe):
            def w_step(j):
                if j >= 2:
                    k = j - 2
                    pe.wait_ge(tern, k + 1)
                    if k:
                        pe.wait_ge(wt_done, 1)
                    for a in range(2):
                        for b in range(2):
                            for c in range(4):
                                t = 4 * b + c
                                src = ternary[0][:, t * D + a * P:t * D + (a + 1) * P] if k == 0 else \
                                    ternary[1][:, a * F + t * P:a * F + (t + 1) * P]
                                mm = nc.tensor.matmul((work, oacc)[a][:, b, c * P:(c + 1) * P], src,
                                                      identb[:, :], start=True, stop=True)
                    mm.then_inc(tern_T, 1)

            def work_bank(s, phase, u):
                slot, k = work_use(s, phase, u)
                if not (isinstance(k, int) and k == 0):
                    pe.wait_ge(w_taken[slot], k)
                return slot

            def bank_p(s, u):
                bank, k = p_use(s, u)
                if P_ORDER.index(u) < 4 and not (s.known and s.i < 2):
                    pe.wait_ge(s_taken[bank // 2], (s.i - 1) * (NU // 2))
                if not (isinstance(k, int) and k == 0):
                    pe.wait_ge(p_taken[bank], k)
                return bank

            def product(out, lhs, rhs, n=KT):
                for t in range(n):
                    mm = nc.tensor.matmul(out, lhs(t), rhs(t), start=(t == 0), stop=(t == n - 1))
                return mm

            def p_taken_by(s, *us):
                for u in us:
                    bank, n = p_use(s, u)
                    pe.wait_ge(p_taken[bank], n + 1)

            def p_step(s, k):
                if k == X_T:
                    pe.wait_ge(x_in, count(s, 1, 0) * 16)
                    for t in range(KT):
                        bank = bank_p(s, t)
                        for b in range(NB):
                            mm = nc.tensor.transpose(p_bank(bank)[:, b * P:(b + 1) * P],
                                                     xtok[:, b, t * P:(t + 1) * P], ident[:, :])
                        mm.then_inc(p_full[bank], 1)
                if QK <= k < QK + 4:
                    c = k - QK
                    bank = bank_p(s, 2 + c)
                    for t in range(KT):
                        if c == 0:
                            p_taken_by(s, t)
                        mm = nc.tensor.matmul(p_bank(bank), wqk[:, t, c * P:(c + 1) * P], xT[:, t, :],
                                              start=(t == 0), stop=(t == KT - 1))
                    mm.then_inc(p_full[bank], 1)
                if k == LAT_IN:
                    bank = bank_p(s, 6)
                    product(p_bank(bank)[0:LD, :], lambda t: wrq[:, t, :], lambda t: xT[:, t, :]
                            ).then_inc(p_full[bank], 1)
                    bank = bank_p(s, 7)
                    pe.wait_ge(p_vec, count(s, NP_VEC, 0))
                    product(p_bank(bank)[:, 0:LAT], lambda t: wrkv[:, t, :], lambda t: pooled[:, t, :]
                            ).then_inc(p_full[bank], 1)
                if k == LAT_SCORES:
                    p_taken_by(s, 6)
                    pe.wait_ge(bd_ready, count(s, 1, 0))
                if LAT_SCORES <= k < LAT_SCORES + 2:
                    b2 = k - LAT_SCORES
                    bank = bank_p(s, 8 + b2)
                    for b in range(2 * b2, 2 * b2 + 2):
                        o = p_bank(bank)[:, (b % 2) * LH * LAT:(b % 2 + 1) * LH * LAT]
                        nc.tensor.matmul(o, rqT[:, b * P:(b + 1) * P],
                                         lat_bd[0:LD, :, :].rearrange("p h l -> p (h l)"),
                                         start=(b % 2 == 0), stop=False, skip_group_check=True)
                        mm = nc.tensor.matmul(o.rearrange("p (h l) -> p h l", h=LH), identb[:, :],
                                              lat_mask[:, b, :].unsqueeze(1).to_broadcast([P, LH, LAT]),
                                              start=False, stop=(b % 2 == 1), skip_group_check=True)
                    mm.then_inc(p_full[bank], 1)
                if VALUES <= k < VALUES + NB:
                    b = k - VALUES
                    bank = bank_p(s, 10 + b)
                    product(p_bank(bank)[:, 0:H * VW], lambda t: xT[:, t, b * P:(b + 1) * P],
                            lambda t: wv[:, t, :, :].rearrange("p h d -> p (h d)")).then_inc(p_full[bank], 1)
                if k == LAT_V:
                    for t in range(2):
                        bank = bank_p(s, 14 + t)
                        nc.tensor.matmul(p_bank(bank)[:, 0:RW],
                                         lat_bd[LD:2 * LD, 2 * t:2 * t + 2, :].rearrange("p h l -> p (h l)"),
                                         wro[LD:2 * LD, :], start=True, stop=True).then_inc(p_full[bank], 1)
                if k == LAT_T:
                    pe.wait_ge(lat_norm, count(s, 1, 0))
                if LAT_T <= k < LAT_T + 2:
                    t = k - LAT_T
                    bank = bank_p(s, 16 + t)
                    for b in range(2 * t, 2 * t + 2):
                        for c in range(2):
                            q = (b % 2) * 2 + c
                            mm = nc.tensor.transpose(
                                p_bank(bank)[:, q * P:(q + 1) * P],
                                lat_p[:, b, 2 * c:2 * c + 2, :].rearrange("p h l -> p (h l)"), ident[:, :])
                    mm.then_inc(p_full[bank], 1)
                if k == REMOTE:
                    p_taken_by(s, 14, 15, 16, 17)
                if REMOTE <= k < REMOTE + NB:
                    b = k - REMOTE
                    bank = bank_p(s, 18 + b)
                    product(p_bank(bank)[:, 0:RW], lambda t: lat_pT[:, b, t, :], lambda t: rvr[:, t, :], 2
                            ).then_inc(p_full[bank], 1)

            def max_scores(s, v):
                b, pair = v // (H // 2), v % (H // 2)
                if v == 0:
                    pe.wait_ge(stacks_in[s.par], (s.half + 1) * (16 * 2 * len(QPART)))
                q, kk = Qs[s.par], Ks[s.par]
                slot = work_bank(s, "A", v)
                for hh in range(2):
                    for g in range(P // GQ):
                        h, at = 2 * pair + hh, b * P + g * GQ
                        nc.tensor.matmul(work[g * GQ:(g + 1) * GQ, slot, hh * BAND:(hh + 1) * BAND],
                                         q[0:KA, h, at:at + GQ], kk[0:KA, h, at:at + BAND],
                                         start=(hh == 0), stop=False, skip_group_check=True)
                o = work[:, slot, 0:2 * BAND]
                if b:
                    o = o.rearrange("p (h c w) -> p h c w", h=2, w=GQ)[:, :, 0:3:2, :]
                    m = mask_edge[:, :, :].unsqueeze(1).to_broadcast([P, 2, 2, GQ])
                else:
                    o = o.rearrange("p (h c) -> p h c", h=2)
                    m = mask_first[:, :].unsqueeze(1).to_broadcast([P, 2, BAND])
                nc.tensor.matmul(o, identb[:, :], m, start=False, stop=True, skip_group_check=True
                                 ).then_inc(w_full[slot], 1)

            def maxima_T(s, t):
                slot, k = work_use(s, "A", NM // 2 * (t + 1) - 1)
                pe.wait_ge(w_taken[slot], k + 1)
                slot = work_bank(s, "T", t)
                for b in range(2):
                    mm = nc.tensor.transpose(work[0:H, slot, b * P:(b + 1) * P], nmax[:, 2 * t + b, :],
                                             ident[:, :])
                mm.then_inc(w_full[slot], 1)

            def scores_T(s, u):
                q, kk = Qs[s.par], Ks[s.par]
                hg, j = u // NB, u % NB
                slot, k = score_use(s, u)
                if u < 2 and not s.last:
                    for bank in (2 * slot, 2 * slot + 1):
                        pe.wait_ge(p_taken[bank], count(s.next(), P_PER[bank], P_PER[bank] - 1))
                if not (isinstance(k, int) and k == 0):
                    pe.wait_ge(s_taken[slot], k)
                w = 2 * P if j < NB - 1 else P
                for c in range(4):
                    mm = nc.tensor.matmul(scores[:, slot, c // 2, (c % 2) * 2 * P:(c % 2) * 2 * P + w],
                                          kk[0:KB, 4 * hg + c, P + j * P:2 * P + j * P],
                                          q[0:KB, 4 * hg + c, j * P:j * P + w], start=True, stop=True)
                mm.then_inc(s_full[slot], 1)

            def weigh(s, v):
                hg, j = v // NB, v % NB
                if j == 0 and hg < 2 and not s.first:
                    pe.wait_ge(y2_ready, count(s, 1, -1))
                if j == 0 and hg >= 2:
                    pe.wait_ge(oT_ready, count(s, HG, hg - 2))
                pe.wait_ge(masked, count(s, NU, v))
                w = 2 * P if j < NB - 1 else P
                for c in range(4):
                    h = 4 * hg + c
                    mm = nc.tensor.matmul(oacc[c * PVW:(c + 1) * PVW, hg % 2, j * P:j * P + w],
                                          Vp[:, s.par, j, h * VW:h * VW + PVW],
                                          Pt[:, v % NPT, c, 0:w], start=(j == 0), stop=(j == NB - 1),
                                          skip_group_check=True)
                mm.then_inc(pv_done, 1)

            def transpose_o(s, hg):
                pe.wait_ge(oT_ready, count(s, HG, hg))
                slot = work_bank(s, "O", hg)
                for b in range(NB):
                    mm = nc.tensor.transpose(work[:, slot, b * P:(b + 1) * P], oT[:, b * P:(b + 1) * P],
                                             ident[:, :])
                mm.then_inc(w_full[slot], 1)

            def down(s, f):
                pe.wait_ge(h_lo_ready, count(s, FT, f))
                for b in range(NB):
                    for j in range(2):
                        mm = nc.tensor.matmul(oacc[:, b // 2, (b % 2) * D:(b % 2 + 1) * D],
                                              (h_hi, h_lo)[j][:, f % NR, b * P:(b + 1) * P], wdn_t[:, f, :],
                                              start=(f == 0 and b % 2 == 0 and j == 0),
                                              stop=(f == FT - 1 and b % 2 == 1 and j == 1),
                                              skip_group_check=True)
                mm.then_inc(down_done, 1)

            def f_step(s, k):
                if k == GATE:
                    transpose_o(s, HG - 1)
                if k == MIX_T:
                    slots = [work_bank(s, "F", t) for t in range(KT)]
                    for b in range(NB):
                        pe.wait_ge(mixed_ready, count(s, NB, b))
                        for t in range(KT):
                            mm = nc.tensor.transpose(work[:, slots[t], b * P:(b + 1) * P],
                                                     mixed[:, b, t * P:(t + 1) * P], ident[:, :])
                            if b == NB - 1:
                                mm.then_inc(w_full[slots[t]], 1)
                if k == OUT:
                    for t in range(KT):
                        slot, n = work_use(s, "F", t)
                        pe.wait_ge(w_taken[slot], n + 1)
                    for c in range(2):
                        slot = work_bank(s, "F", 2 + c)
                        for b in range(2 * c, 2 * c + 2):
                            mm = product(work[:, slot, (b % 2) * D:(b % 2 + 1) * D],
                                         lambda t: mixT[:, t, b * P:(b + 1) * P], lambda t: wout[:, t, :])
                        mm.then_inc(w_full[slot], 1)
                if k == XN_T:
                    slots = [work_bank(s, "F", 4 + t) for t in range(KT)]
                    for b in range(NB):
                        pe.wait_ge(xn_ready, count(s, NB, b))
                        for t in range(KT):
                            mm = nc.tensor.transpose(work[:, slots[t], b * P:(b + 1) * P],
                                                     xn[:, b, t * P:(t + 1) * P], ident[:, :])
                            if b == NB - 1:
                                mm.then_inc(w_full[slots[t]], 1)
                if k == UP:
                    pe.wait_ge(oT_ready, count(s, HG, HG - 1))
                if UP <= k < END:
                    f = k - UP
                    slot = work_bank(s, "F", 6 + f)
                    for part in range(2):
                        for t in range(KT):
                            if f == 0 and part == 0:
                                pe.wait_ge(xn_hi, count(s, KT, t))
                            if f == 0 and part == 1:
                                low_slot, n = work_use(s, "F", 4 + t)
                                pe.wait_ge(w_taken[low_slot], n + 1)
                            mm = nc.tensor.matmul(work[:, slot, :], wup_t[:, t, f * P:(f + 1) * P],
                                                  xnT[:, part, t, :], start=(part == 0 and t == 0),
                                                  stop=(part == 1 and t == KT - 1))
                    mm.then_inc(w_full[slot], 1)
                    if f >= TRAIL:
                        down(s, f - TRAIL)
                if k == END:
                    for f in range(FT - TRAIL, FT):
                        if f == FT - 1:
                            pe.wait_ge(h_added, count(s, FT - 1, FT - 2))
                            slot = work_bank(s, "F", 14)
                            for b in range(NB):
                                mm = nc.tensor.matmul(work[:, slot, b:b + 1], h_sum[:, b * P:(b + 1) * P],
                                                      ones_col[:, :], start=True, stop=True)
                            mm.then_inc(w_full[slot], 1)
                        down(s, f)

            def body(s):
                pe.wait_ge(nmax_in[s.par], (s.half + 1) * 16)
                scores_T(s, 0)
                for u in range(FIRST_HALF):
                    if u + 1 < NU:
                        scores_T(s, u + 1)
                    if 2 * u < NM and not s.last:
                        max_scores(s.next(), 2 * u)
                    if u >= 2:
                        weigh(s, u - 2)
                    if 2 * u < NM and not s.last:
                        max_scores(s.next(), 2 * u + 1)
                    if u >= 7 and (u - 7) % NB == 0 and (u - 7) // NB < HG - 1:
                        transpose_o(s, (u - 7) // NB)
                    if not s.last:
                        for t in range(2):
                            if u == (9, NM // 2)[t]:
                                maxima_T(s.next(), t)
                later = s.second_next()
                for phase, k in SECOND_HALF:
                    if phase == "F":
                        f_step(s, k)
                    elif later.exists:
                        p_step(later, k)

            for phase, k in PROLOGUE:
                if phase == "W":
                    w_step(k)
                elif phase in ("P0", "P1"):
                    if (phase, k) == ("P0", X_T):
                        pe.wait_ge(consts, 1)
                    if (phase, k) == ("P0", QK):
                        pe.wait_ge(w_in, W_ALL)
                        pe.wait_ge(consts, 2)
                    if (phase, k) == ("P0", VALUES):
                        pe.wait_ge(prep_done, 1)
                    p_step(START[phase], k)
                else:
                    if (phase, k) == ("A", 0):
                        pe.wait_ge(wt_done, 2)
                    (max_scores if phase == "A" else maxima_T)(Seq(0, 0, 0), k)
            over_sequences(pe, body)


INPUTS = ["L0_attn_x", "L0_attn_qkv_w", "L0_attn_qkv_b", "L0_attn_rq_w", "L0_attn_rq_b", "L0_attn_rkv_w",
          "L0_attn_rkv_b", "L0_attn_rout_w", "L0_attn_rout_b", "L0_attn_out_w", "L0_attn_out_b",
          "L0_attn_gl_w", "L0_attn_gr_w", "L0_ffn_w_up", "L0_ffn_w_down"]


def kernel(**inputs):
    import concourse.bacc as bacc
    from concourse.bass_utils import run_bass_kernel_spmd

    nc = bacc.Bacc("TRN2", target_bir_lowering=False, num_devices=1)
    arrays, args = {}, []
    for name in INPUTS:
        a = np.ascontiguousarray(inputs[name])
        arrays[name] = a
        args.append(nc.dram_tensor(name, a.shape, mybir.dt.from_np(a.dtype), kind="ExternalInput").ap())
    out = nc.dram_tensor("y", (B, S, D), F32, kind="ExternalOutput").ap()
    build(nc, *args, out)
    r = run_bass_kernel_spmd(nc, [arrays], core_ids=[0])
    return r.results[0]["y"]
```
